# Optimizing a Trainium2 kernel written in Bass

```python
import numpy as np
import jax
import jax.numpy as jnp

def _softmax(x, axis=-1):
    return jax.nn.softmax(x, axis=axis)

def _gelu(x):
    return jax.nn.gelu(x, approximate=True)

def _silu(x):
    return jax.nn.silu(x)

def _sigmoid(x):
    return jax.nn.sigmoid(x)

def _layernorm(x, axis=-1, eps=1e-05):
    m = jnp.mean(x, axis=axis, keepdims=True)
    v = jnp.var(x, axis=axis, keepdims=True)
    return (x - m) / jnp.sqrt(v + eps)

def _scatter_add(tgt, idx, src, axis=0):
    return tgt.at[idx].add(src)

def _segment_sum(src, seg, n):
    return jax.ops.segment_sum(src, seg, n)
kernel_name = 'mk_seq_preln_d1_jaxref_r4_4c3b13'

def setup_inputs(seed: int=0):
    np.random.seed(seed)
    _w = jnp.asarray

    def _L0_attn_setup():
        import jax, jax.numpy as jnp
        import numpy as np
        B, L, D = (8, 1024, 256)
        EPS = 1e-05
        key = jax.random.key(seed)
        ks = jax.random.split(key, 8)
        s = 0.02
        return {'x': jax.random.normal(ks[0], (B, L, D), dtype=jnp.float32), 'decay': jnp.full((D,), 0.9, dtype=jnp.float32), 'Wr': jax.random.normal(ks[1], (D, D), dtype=jnp.float32) * s, 'br': jnp.zeros((D,), dtype=jnp.float32), 'Wg': jax.random.normal(ks[2], (D, D), dtype=jnp.float32) * s, 'bg': jnp.zeros((D,), dtype=jnp.float32), 'Wo': jax.random.normal(ks[3], (D, D), dtype=jnp.float32) * s, 'bo': jnp.zeros((D,), dtype=jnp.float32), 'ln_w': jnp.ones((D,), dtype=jnp.float32), 'ln_b': jnp.zeros((D,), dtype=jnp.float32)}
    _L0_attn_in = _L0_attn_setup()

    def _L0_ffn_setup():
        import jax, jax.numpy as jnp
        import numpy as np
        NUM_HEADS = 16
        TOP_K = 2
        key = jax.random.key(seed)
        ks = jax.random.split(key, 5)
        B, S, D, E = (4, 512, 256, 8)
        scale = 0.02
        return {'x': jax.random.normal(ks[0], (B, S, D), dtype=jnp.float32), 'W_qkv': jax.random.normal(ks[1], (D, 3 * D), dtype=jnp.float32) * scale, 'b_qkv': jnp.zeros((3 * D,), dtype=jnp.float32), 'W_gate': jax.random.normal(ks[2], (D, E), dtype=jnp.float32) * scale, 'b_gate': jnp.zeros((E,), dtype=jnp.float32), 'W_experts': jax.random.normal(ks[3], (E, D, D), dtype=jnp.float32) * scale, 'b_experts': jnp.zeros((E, D), dtype=jnp.float32)}
    _L0_ffn_in = _L0_ffn_setup()
    _d = {'L0_attn_x': _L0_attn_in['x'], 'L0_attn_decay': _L0_attn_in['decay'], 'L0_attn_Wr': _L0_attn_in['Wr'], 'L0_attn_br': _L0_attn_in['br'], 'L0_attn_Wg': _L0_attn_in['Wg'], 'L0_attn_bg': _L0_attn_in['bg'], 'L0_attn_Wo': _L0_attn_in['Wo'], 'L0_attn_bo': _L0_attn_in['bo'], 'L0_attn_ln_w': _L0_attn_in['ln_w'], 'L0_attn_ln_b': _L0_attn_in['ln_b'], 'L0_ffn_W_qkv': _L0_ffn_in['W_qkv'], 'L0_ffn_b_qkv': _L0_ffn_in['b_qkv'], 'L0_ffn_W_gate': _L0_ffn_in['W_gate'], 'L0_ffn_b_gate': _L0_ffn_in['b_gate'], 'L0_ffn_W_experts': _L0_ffn_in['W_experts'], 'L0_ffn_b_experts': _L0_ffn_in['b_experts']}
    _x0 = _d['L0_attn_x']
    _d['L0_attn_x'] = jax.random.normal(jax.random.fold_in(jax.random.key(seed), 1), (4, 2048, 256), dtype=_x0.dtype)
    del _x0
    return _d

def reference(L0_attn_x, L0_attn_decay, L0_attn_Wr, L0_attn_br, L0_attn_Wg, L0_attn_bg, L0_attn_Wo, L0_attn_bo, L0_attn_ln_w, L0_attn_ln_b, L0_ffn_W_qkv, L0_ffn_b_qkv, L0_ffn_W_gate, L0_ffn_b_gate, L0_ffn_W_experts, L0_ffn_b_experts):

    def _L0_attn_ref(x, decay, Wr, br, Wg, bg, Wo, bo, ln_w, ln_b):
        import jax, jax.numpy as jnp
        import numpy as np
        B, L, D = (8, 1024, 256)
        EPS = 1e-05
        b, l, d = x.shape
        decay_factor = jax.nn.sigmoid(decay)
        one_minus = 1.0 - decay_factor
        z = jax.nn.sigmoid(jnp.einsum('bld,ed->ble', x, Wg) + bg)
        x_t_first = jnp.moveaxis(x, 1, 0)
        z_t_first = jnp.moveaxis(z, 1, 0)

        def step(h, inp):
            x_t, z_t = inp
            pred_x = h @ Wr.T + br
            error = x_t - pred_x
            h_new = decay_factor * h + one_minus * (z_t * error)
            return (h_new, h_new)
        h0 = jnp.zeros((b, d), dtype=x.dtype)
        _, ys = jax.lax.scan(step, h0, (x_t_first, z_t_first))
        y = jnp.moveaxis(ys, 0, 1)
        mean = jnp.mean(y, axis=-1, keepdims=True)
        var = jnp.mean(jnp.square(y - mean), axis=-1, keepdims=True)
        y = (y - mean) * jax.lax.rsqrt(var + EPS) * ln_w + ln_b
        return jnp.einsum('bld,ed->ble', y, Wo) + bo

    def _L0_ffn_ref(x, W_qkv, b_qkv, W_gate, b_gate, W_experts, b_experts):
        import jax, jax.numpy as jnp
        import numpy as np
        NUM_HEADS = 16
        TOP_K = 2
        B, S, D = x.shape
        H = NUM_HEADS
        hd = D // H
        E = W_gate.shape[-1]
        qkv = (x @ W_qkv + b_qkv).reshape(B, S, 3, H, hd)
        q, k, v = (qkv[:, :, 0], qkv[:, :, 1], qkv[:, :, 2])
        attn = jnp.einsum('bqhd,bkhd->bhqk', q, k) / jnp.sqrt(jnp.asarray(hd, x.dtype))
        attn = jax.nn.softmax(attn, axis=-1)
        attn_out = jnp.einsum('bhqk,bkhd->bqhd', attn, v).reshape(B, S, D)
        gate = jax.nn.softmax(x @ W_gate + b_gate, axis=-1)
        top_g, top_i = jax.lax.top_k(gate, TOP_K)
        combine = jnp.sum(jax.nn.one_hot(top_i, E, dtype=x.dtype) * top_g[..., None], axis=2)
        expert_out = jnp.einsum('bsd,edf->bsef', x, W_experts) + b_experts
        moe_out = jnp.einsum('bsef,bse->bsf', expert_out, combine)
        return attn_out + moe_out
    x = L0_attn_x
    x = x + _L0_attn_ref(_layernorm(x, axis=-1), L0_attn_decay, L0_attn_Wr, L0_attn_br, L0_attn_Wg, L0_attn_bg, L0_attn_Wo, L0_attn_bo, L0_attn_ln_w, L0_attn_ln_b)
    x = x + _L0_ffn_ref(_layernorm(x, axis=-1), L0_ffn_W_qkv, L0_ffn_b_qkv, L0_ffn_W_gate, L0_ffn_b_gate, L0_ffn_W_experts, L0_ffn_b_experts)
    return x

_drawn_inputs = setup_inputs


def setup_inputs(seed=0):
    import zlib

    import numpy as np

    out = dict(_drawn_inputs(seed))
    spreads = {'L0_attn_decay': (0.8999999761581421, 0.2),
     'L0_attn_br': (0.0, 0.1),
     'L0_attn_bg': (0.0, 0.447),
     'L0_attn_bo': (0.0, 0.1),
     'L0_attn_ln_w': (1.0, 0.2),
     'L0_attn_ln_b': (0.0, 0.1),
     'L0_ffn_b_qkv': (0.0, 0.1),
     'L0_ffn_b_gate': (0.0, 0.1),
     'L0_ffn_b_experts': (0.0, 0.349)}
    factors = {}
    for name, (base, spread) in spreads.items():
        noise = np.random.default_rng([zlib.crc32(name.encode()), seed]).standard_normal(out[name].shape)
        drawn = base * np.exp(spread * noise) if base else spread * noise
        out[name] = jnp.asarray(drawn.astype(out[name].dtype))
    for name, factor in factors.items():
        out[name] = (out[name] * factor).astype(out[name].dtype)
    return out
```

```python
from contextlib import ExitStack, nullcontext

import concourse.bass as bass
from concourse import mybir

F32 = mybir.dt.float32
BF16 = mybir.dt.bfloat16
I32 = mybir.dt.int32
ALU = mybir.AluOpType
ACT = mybir.ActivationFunctionType
AX = mybir.AxisListType

P = 128
B, L, D = 4, 2048, 256
DH = D // P
T = B * L
TILES = T // P
EPS = 1e-5

SPAN = 512
SPANS = T // SPAN

STEPS = 32
CHUNKS = L // STEPS
LANES = B * CHUNKS
GL = LANES // 2
GB = B // 2
SWEEPS = 4
TOLERANCE = 2.0 ** -21

HEADS, HD = 16, 16
E, TOP_K = 8, 2

V_DECAY, V_BR, V_BG, V_LNW, V_LNB, V_BQ, V_BK = range(0, 14, 2)
NVEC = 14


class Steps:

    def __init__(self, sem, start=0):
        self.sem, self.start, self.n = sem, start, 0

    def add(self, ins):
        ins.then_inc(self.sem, 1)
        self.n += 1
        return self.start + self.n

    def wait(self, eng):
        eng.wait_ge(self.sem, self.start + self.n)


def statistics(nc, vec, own, s, sums, spread, n):
    me, mo = sums[:, 0:n, 1], sums[:, 0:n, 4]
    qe, qo = sums[:, 0:n, 2], sums[:, 0:n, 5]
    own.wait(vec)
    own.add(nc.vector.tensor_tensor(s["a"][:, 0:n], me, mo, ALU.add))
    own.add(nc.vector.tensor_tensor(s["b"][:, 0:n], me, mo, ALU.subtract))
    own.add(nc.vector.tensor_tensor(s["c"][:, 0:n], qe, qo, ALU.add))
    own.wait(vec)
    own.add(nc.vector.tensor_scalar(s["mean"][:, 0:n], s["a"][:, 0:n], 0.5, None, ALU.mult))
    own.add(nc.vector.tensor_tensor(s["d"][:, 0:n], s["b"][:, 0:n], s["b"][:, 0:n], ALU.mult))
    own.wait(vec)
    own.add(nc.vector.tensor_scalar(s["e"][:, 0:n], s["d"][:, 0:n], 0.25, EPS, ALU.mult, ALU.add))
    own.wait(vec)
    spread(nc.vector.scalar_tensor_tensor(out=s["var"][:, 0:n], in0=s["c"][:, 0:n], scalar=1.0 / D,
                                          in1=s["e"][:, 0:n], op0=ALU.mult, op1=ALU.add))


def inverse_root(nc, vec, own, s, n):
    own.add(nc.vector.reciprocal(s["a"][:, 0:n], s["root"][:, 0:n]))
    own.wait(vec)
    own.add(nc.vector.tensor_tensor(s["b"][:, 0:n], s["a"][:, 0:n], s["a"][:, 0:n], ALU.mult))
    own.wait(vec)
    own.add(nc.vector.tensor_tensor(s["c"][:, 0:n], s["b"][:, 0:n], s["var"][:, 0:n], ALU.mult))
    own.wait(vec)
    own.add(nc.vector.tensor_scalar(s["d"][:, 0:n], s["c"][:, 0:n], -0.5, 1.5, ALU.mult, ALU.add))
    own.wait(vec)
    own.add(nc.vector.tensor_tensor(s["rstd"][:, 0:n], s["a"][:, 0:n], s["d"][:, 0:n], ALU.mult))


def normalise_and_gate(nc, k):
    X, gain, drive, vec_in = k["xy"], k["gain"], k["drive"], k["vec"]
    with ExitStack() as ctx:
        sem = lambda name: ctx.enter_context(nc.semaphore(name))
        sb = lambda name, shape, dt=F32: ctx.enter_context(nc.sbuf_tensor(name, shape, dt))
        ps = lambda name, shape, dt=F32: ctx.enter_context(nc.psum_tensor(name, shape, dt))
        PARTS = 8
        PT = TILES // PARTS
        x_in = [sem(f"x_in{c}") for c in range(PARTS)]
        const_in, stats_own, var_ready, root_ready = sem("const_in"), sem("stats_own"), sem("var_ready"), sem("root_ready")
        decay_ready, gates_ready = sem("decay_ready"), sem("gates_ready")
        xn_ready, xnT_psum, xnT_ready, z_psum, z_ready, drive_own, xnT_act = (
            sem("xn_ready"), sem("xnT_psum"), sem("xnT_ready"), sem("z_psum"), sem("z_ready"), sem("drive_own"), sem("xnT_act"))
        sums = sb("sums", [P, TILES, 6])
        s = {n: sb(f"st_{n}", [P, TILES]) for n in ("a", "b", "c", "d", "e", "mean", "var", "root", "rstd")}
        xn = sb("xn", [P, 4, D])
        wg = sb("wg", [P, DH, D])
        xnT_ps = ps("xnT_ps", [P, 2, DH, SPAN])
        z_ps = ps("z_ps", [P, 2, DH, SPAN])
        block = ctx.enter_context(nc.Block())

        @block.sync
        def _(sp):
            xv = k["in_x"].rearrange("(t p) d -> p t d", p=P)
            for c in range(PARTS):
                sp.dma_start(X[:, c * PT:(c + 1) * PT, :], xv[:, c * PT:(c + 1) * PT, :]).then_inc(x_in[c], 16)
                if c == 0:
                    sp.dma_start(vec_in[:], k["in_vec"]).then_inc(const_in, 16)
                    sp.dma_start(k["ident"][:], k["in_ident"]).then_inc(const_in, 16)
                    sp.dma_start(wg[:], k["in_wg"].rearrange("(k p) e -> p k e", p=P)).then_inc(const_in, 16)
                    sp.dma_start(k["wr"][:], k["in_wr"].rearrange("(k p) e -> p k e", p=P)).then_inc(const_in, 16)

        @block.vector
        def _(vec):
            own = Steps(stats_own)
            for c in range(PARTS):
                vec.wait_ge(x_in[c], 16)
                for t in range(c * PT, (c + 1) * PT):
                    own.add(nc.vector.bn_stats(sums[:, t, :], X[:, t, :]))
            statistics(nc, vec, own, s, sums, lambda ins: ins.then_inc(var_ready, 1), TILES)
            vec.wait_ge(decay_ready, 1)
            own.add(nc.vector.tensor_scalar(k["away"][:], k["keep"][:], -1.0, 1.0, ALU.mult, ALU.add))
            vec.wait_ge(root_ready, 1)
            inverse_root(nc, vec, own, s, TILES)
            own.wait(vec)
            with vec.Fori(0, SPANS // 2) as i:
                for u in range(2):
                    g = i * 2 + u
                    mine = Steps(drive_own, g * 4)
                    vec.wait_ge(xnT_psum, g + 2)
                    for j in range(4):
                        ins = nc.vector.tensor_scalar(xn[:, j, :], X[:, bass.ds(g * 4 + j, 1), :],
                                                      s["mean"][:, bass.ds(g * 4 + j, 1)],
                                                      s["rstd"][:, bass.ds(g * 4 + j, 1)], ALU.subtract, ALU.mult)
                    ins.then_inc(xn_ready, 1)
                    vec.wait_ge(xnT_psum, g + 3)
                    nc.vector.tensor_copy(drive[:, 1, bass.ds(g * SPAN, SPAN)], xnT_ps[:, u, 1, :]).then_inc(xnT_ready, 1)
                    vec.wait_ge(z_ready, 2 * g + 2)
                    vec.wait_ge(xnT_act, g + 1)
                    vec.wait_ge(xnT_ready, g + 1)
                    for m in range(DH):
                        mine.add(nc.vector.tensor_scalar(gain[:, m, bass.ds(g * SPAN, SPAN)], gain[:, m, bass.ds(g * SPAN, SPAN)],
                                                         k["away"][:, m:m + 1], None, ALU.mult))
                    mine.wait(vec)
                    for m in range(DH):
                        mine.add(nc.vector.scalar_tensor_tensor(
                            out=drive[:, m, bass.ds(g * SPAN, SPAN)], in0=drive[:, m, bass.ds(g * SPAN, SPAN)],
                            scalar=vec_in[:, V_BR + m:V_BR + m + 1], in1=gain[:, m, bass.ds(g * SPAN, SPAN)],
                            op0=ALU.subtract, op1=ALU.mult))

        @block.scalar
        def _(act):
            act.wait_ge(const_in, 64)
            nc.scalar.activation(k["keep"][:], vec_in[:, V_DECAY:V_DECAY + DH], ACT.Sigmoid).then_inc(decay_ready, 1)
            act.wait_ge(var_ready, 1)
            nc.scalar.activation(s["root"][:], s["var"][:], ACT.Sqrt).then_inc(root_ready, 1)
            with act.Fori(0, SPANS // 2) as i:
                for u in range(2):
                    g = i * 2 + u
                    act.wait_ge(xnT_psum, g + 3)
                    nc.scalar.copy(drive[:, 0, bass.ds(g * SPAN, SPAN)], xnT_ps[:, u, 0, :]).then_inc(xnT_act, 1)
                    for m in range(DH):
                        act.wait_ge(z_psum, 2 * g + m + 1)
                        nc.scalar.activation(gain[:, m, bass.ds(g * SPAN, SPAN)], z_ps[:, u, m, :], ACT.Sigmoid,
                                             bias=vec_in[:, V_BG + m:V_BG + m + 1]).then_inc(z_ready, 1)

        @block.tensor
        def _(pe):
            pe.wait_ge(const_in, 64)
            pe.sem_inc(xnT_psum, 2)
            with pe.Fori(0, SPANS // 2) as i:
                for u in range(2):
                    g = i * 2 + u
                    pe.wait_ge(xn_ready, g + 1)
                    for m in range(DH):
                        for j in range(4):
                            ins = nc.tensor.transpose(xnT_ps[:, u, m, j * P:(j + 1) * P],
                                                      xn[:, j, m * P:(m + 1) * P], k["ident"][:])
                    ins.then_inc(xnT_psum, 1)
                    pe.wait_ge(xnT_ready, g + 1)
                    pe.wait_ge(xnT_act, g + 1)
                    for m in range(DH):
                        for q in range(DH):
                            ins = nc.tensor.matmul(z_ps[:, u, m, :], wg[:, q, m * P:(m + 1) * P],
                                                   drive[:, q, bass.ds(g * SPAN, SPAN)], start=(q == 0), stop=(q == DH - 1))
                        ins.then_inc(z_psum, 1)


def lanes_of(ap, g):
    return ap[:, g, :, :].rearrange("p m (b c) -> p m b c", c=CHUNKS)


def always(eng):
    return nullcontext()


def unless(flag):
    return lambda eng: eng.If(eng.value_load(flag[:], min_val=0, max_val=P) != P)


def sweep(nc, k, name, count, when=always):
    state, start = k["state"], k["start"]
    hist = k["xy"][:].rearrange("p t d -> p (t d)").rearrange("p (m c s) -> p m c s", m=DH, s=STEPS)
    drive = k["drive"][:].rearrange("p m (c s) -> p m c s", s=STEPS)
    gain = k["gain"][:].rearrange("p m (c s) -> p m c s", s=STEPS)
    with ExitStack() as ctx:
        sem = lambda n: ctx.enter_context(nc.semaphore(f"{name}_{n}"))
        sb = lambda n, shape, dt=F32: ctx.enter_context(nc.sbuf_tensor(f"{name}_{n}", shape, dt))
        ps = lambda n, shape, dt=F32: ctx.enter_context(nc.psum_tensor(f"{name}_{n}", shape, dt))
        free = sb("free", [P, 2, DH, GL])
        bent = sb("bent", [P, 2, DH, GL])
        pred = ps("pred", [P, 2, 512])
        own = sem("own")
        state_ready = [sem(f"state_ready{g}") for g in range(2)]
        pred_ready = [sem(f"pred_ready{g}") for g in range(2)]
        stored = [sem(f"stored{g}") for g in range(2)]
        block = ctx.enter_context(nc.Block())
        TURN = 8

        @block.vector
        def _(vec):
            with when(vec), vec.Fori(0, count) as n:
                mine = Steps(own, n * (4 + TURN * STEPS))
                for g in range(2):
                    for m in range(DH):
                        mine.add(nc.vector.tensor_copy(lanes_of(start, g)[:, m, :, 1:CHUNKS],
                                                       lanes_of(state, g)[:, m, :, 0:CHUNKS - 1]))
                mine.wait(vec)
                for g in range(2):
                    nc.vector.tensor_copy(state[:, g, :, :], start[:, g, :, :]).then_inc(state_ready[g], 1)
                with vec.Fori(0, STEPS) as t:
                    turn = Steps(own, n * (4 + TURN * STEPS) + 4 + t * TURN)
                    for g in range(2):
                        at = slice(g * GL, (g + 1) * GL)
                        vec.wait_ge(state_ready[g], n * (STEPS + 1) + t + 1)
                        for m in range(DH):
                            turn.add(nc.vector.scalar_tensor_tensor(
                                out=free[:, g, m, :], in0=state[:, g, m, :], scalar=k["keep"][:, m:m + 1],
                                in1=drive[:, m, at, bass.ds(t, 1)].rearrange("p c o -> p (c o)"),
                                op0=ALU.mult, op1=ALU.add))
                        vec.wait_ge(pred_ready[g], n * STEPS + t + 1)
                        for m in range(DH):
                            turn.add(nc.vector.tensor_tensor(
                                bent[:, g, m, :], pred[:, g, m * GL:(m + 1) * GL],
                                gain[:, m, at, bass.ds(t, 1)].rearrange("p c o -> p (c o)"), ALU.mult))
                        turn.wait(vec)
                        vec.wait_ge(stored[g], n * STEPS + t + 1)
                        nc.vector.tensor_tensor(state[:, g, :, :], free[:, g, :, :], bent[:, g, :, :],
                                                ALU.subtract).then_inc(state_ready[g], 1)
                for g in range(2):
                    vec.wait_ge(state_ready[g], (n + 1) * (STEPS + 1))
                    vec.wait_ge(stored[g], (n + 1) * STEPS + 1)

        @block.tensor
        def _(pe):
            with when(pe), pe.Fori(0, count) as n:
                with pe.Fori(0, STEPS) as t:
                    for g in range(2):
                        pe.wait_ge(state_ready[g], n * (STEPS + 1) + t + 1)
                        for m in range(DH):
                            for q in range(DH):
                                ins = nc.tensor.matmul(pred[:, g, m * GL:(m + 1) * GL], k["wr"][:, q, m * P:(m + 1) * P],
                                                       state[:, g, q, :], start=(q == 0), stop=(q == DH - 1))
                        ins.then_inc(pred_ready[g], 1)

        @block.scalar
        def _(act):
            for g in range(2):
                act.sem_inc(stored[g], 1)
            with when(act), act.Fori(0, count) as n:
                with act.Fori(0, STEPS) as t:
                    for g in range(2):
                        at = slice(g * GL, (g + 1) * GL)
                        act.wait_ge(state_ready[g], n * (STEPS + 1) + t + 2)
                        nc.scalar.copy(hist[:, :, at, bass.ds(t, 1)].rearrange("p m c o -> p m (c o)"),
                                       state[:, g, :, :]).then_inc(stored[g], 1)


def clear_states(nc, k):
    with nc.Block() as block:
        @block.vector
        def _(vec):
            nc.vector.memset(k["state"][:], 0.0)
            nc.vector.memset(k["start"][:], 0.0)
            nc.vector.memset(k["ones"][:], 1.0)


def look_at_defect(nc, k):
    with ExitStack() as ctx:
        sem = lambda n: ctx.enter_context(nc.semaphore(f"defect_{n}"))
        sb = lambda n, shape, dt=F32: ctx.enter_context(nc.sbuf_tensor(f"defect_{n}", shape, dt))
        size, gap, wide = sb("size", [P, 2, DH, GL]), sb("gap", [P, 2, DH, GL]), sb("wide", [P, 2, DH, GL])
        most, bound, close, all_close = sb("most", [P, DH]), sb("bound", [P, DH]), sb("close", [P, 2, DH, GL]), sb("all_close", [P, 1])
        total = ctx.enter_context(nc.psum_tensor("defect_total", [P, 1], F32))
        own, flags_ready, total_ready = sem("own"), sem("flags_ready"), sem("total_ready")
        block = ctx.enter_context(nc.Block())

        @block.vector
        def _(vec):
            mine = Steps(own)
            flat = lambda ap: ap[:].rearrange("p g m c -> p (g m c)")
            mine.add(nc.vector.scalar_tensor_tensor(out=flat(size), in0=flat(k["state"]), scalar=-1.0, in1=flat(k["state"]),
                                                    op0=ALU.mult, op1=ALU.max))
            mine.add(nc.vector.memset(gap[:], 0.0))
            mine.wait(vec)
            for g in range(2):
                for m in range(DH):
                    mine.add(nc.vector.tensor_tensor(lanes_of(gap, g)[:, m, :, 1:CHUNKS],
                                                     lanes_of(k["state"], g)[:, m, :, 0:CHUNKS - 1],
                                                     lanes_of(k["start"], g)[:, m, :, 1:CHUNKS], ALU.subtract))
            mine.add(nc.vector.tensor_reduce(most[:], size[:].rearrange("p g m c -> p m g c"), AX.XY, ALU.max))
            mine.wait(vec)
            mine.add(nc.vector.tensor_scalar(bound[:], most[:], TOLERANCE, None, ALU.mult))
            mine.add(nc.vector.scalar_tensor_tensor(out=flat(wide), in0=flat(gap), scalar=-1.0, in1=flat(gap),
                                                    op0=ALU.mult, op1=ALU.max))
            mine.wait(vec)
            for m in range(DH):
                mine.add(nc.vector.tensor_scalar(close[:, :, m, :], wide[:, :, m, :], bound[:, m:m + 1], None, ALU.is_le))
            mine.wait(vec)
            nc.vector.tensor_reduce(all_close[:], close[:], AX.XYZ, ALU.min).then_inc(flags_ready, 1)
            vec.wait_ge(total_ready, 1)
            nc.vector.tensor_copy(k["agree"][:], total[0:1, :])

        @block.tensor
        def _(pe):
            pe.wait_ge(flags_ready, 1)
            nc.tensor.matmul(total[:], k["ones"][:], all_close[:], start=True, stop=True).then_inc(total_ready, 1)


def over_spans(eng, body):
    for u in range(2):
        body(u, u, u == 0, False)
    with eng.Fori(1, SPANS // 2 - 1) as i:
        for u in range(2):
            body(i * 2 + u, u, False, False)
    for u in range(2):
        body(SPANS - 2 + u, u, False, u == 1)


def project_states(nc, k):
    hist = k["xy"][:].rearrange("p t d -> p (t d)").rearrange("p (m t) -> p m t", m=DH)
    vec_in = k["vec"]
    with ExitStack() as ctx:
        sem = lambda n: ctx.enter_context(nc.semaphore(f"proj_{n}"))
        sb = lambda n, shape, dt=F32: ctx.enter_context(nc.sbuf_tensor(f"proj_{n}", shape, dt))
        ps = lambda n, shape, dt=F32: ctx.enter_context(nc.psum_tensor(f"proj_{n}", shape, dt))
        wo, bo = sb("wo", [P, DH, D]), sb("bo", [P, D])
        hs = sb("hs", [P, 2, DH, SPAN])
        hn = sb("hn", [P, 4, D])
        hT = sb("hT", [P, DH, SPAN])
        x1 = sb("x1", [P, 2, 4, D])
        sums, sums1 = sb("sums", [P, 4, 6]), sb("sums1", [P, TILES, 6])
        s = {n: sb(f"st_{n}", [P, 4]) for n in ("a", "b", "c", "d", "e", "mean", "var", "root", "rstd")}
        s1 = {n: sb(f"st1_{n}", [P, TILES]) for n in ("a", "b", "c", "d", "e", "var", "root")}
        s1["mean"], s1["rstd"] = k["mean1"], k["rstd1"]
        h_ps = ps("h_ps", [P, 2, 4, D])
        hT_ps = ps("hT_ps", [P, DH, SPAN])
        o_ps = ps("o_ps", [P, 4, D])
        const_in, own = sem("const_in"), sem("own")
        hs_ready, h_psum, var_ready, root_ready, hn_ready, hT_psum, hT_ready, o_psum, x1_ready, xb_ready = (
            sem(n) for n in ("hs_ready", "h_psum", "var_ready", "root_ready", "hn_ready", "hT_psum", "hT_ready",
                             "o_psum", "x1_ready", "xb_ready"))
        x_in = [sem(f"x_in{u}") for u in range(2)]
        x1_out = [sem(f"x1_out{u}") for u in range(2)]
        block = ctx.enter_context(nc.Block())
        xv = k["in_x"].rearrange("(g j p) d -> p g j d", p=P, j=4)
        x1v = k["x1"].rearrange("(g j p) d -> p g j d", p=P, j=4)

        @block.sync
        def _(sp):
            sp.dma_start(wo[:], k["in_wo"].rearrange("(k p) e -> p k e", p=P)).then_inc(const_in, 16)
            sp.dma_start(bo[:], k["in_bo"]).then_inc(const_in, 16)
            for u in range(2):
                sp.dma_start(x1[:, u, :, :], xv[:, u, :, :]).then_inc(x_in[u], 16)
            with sp.Fori(0, SPANS // 2 - 1) as i:
                for u in range(2):
                    sp.wait_ge(x1_ready, i * 2 + u + 1)
                    sp.dma_start(x1v[:, bass.ds(i * 2 + u, 1), :, :].rearrange("p g j d -> p (g j) d"),
                                 x1[:, u, :, :]).then_inc(x1_out[u], 16)
                    sp.wait_ge(x1_out[u], i * 16 + 16)
                    sp.dma_start(x1[:, u, :, :],
                                 xv[:, bass.ds(i * 2 + 2 + u, 1), :, :].rearrange("p g j d -> p (g j) d")).then_inc(x_in[u], 16)
            for u in range(2):
                sp.wait_ge(x1_ready, SPANS - 1 + u)
                sp.dma_start(x1v[:, SPANS - 2 + u, :, :], x1[:, u, :, :]).then_inc(x1_out[u], 16)
            for u in range(2):
                sp.wait_ge(x1_out[u], 16 * SPANS // 2)

        @block.gpsimd
        def _(pool):
            pool.wait_ge(const_in, 32)
            with pool.Fori(0, SPANS // 2) as i:
                for u in range(2):
                    pool.wait_ge(x_in[u], i * 16 + 16)
                    nc.gpsimd.tensor_tensor(x1[:, u, :, :], x1[:, u, :, :], bo[:].unsqueeze(1).to_broadcast([P, 4, D]),
                                            ALU.add).then_inc(xb_ready, 1)

        @block.scalar
        def _(act):
            nc.scalar.copy(hs[:, 0, :, :], hist[:, :, 0:SPAN]).then_inc(hs_ready, 1)

            def body(g, u, is_first, is_last):
                if not is_last:
                    if not is_first:
                        act.wait_ge(h_psum, g)
                    nc.scalar.copy(hs[:, 1 - u, :, :], hist[:, :, bass.ds((g + 1) * SPAN, SPAN)]).then_inc(hs_ready, 1)
                act.wait_ge(var_ready, g + 1)
                nc.scalar.activation(s["root"][:], s["var"][:], ACT.Sqrt).then_inc(root_ready, 1)
                act.wait_ge(hT_psum, g + 1)
                if not is_first:
                    act.wait_ge(o_psum, g)
                for m in range(DH):
                    ins = nc.scalar.activation(hT[:, m, :], hT_ps[:, m, :], ACT.Identity,
                                               bias=vec_in[:, V_LNB + m:V_LNB + m + 1],
                                               scale=vec_in[:, V_LNW + m:V_LNW + m + 1])
                ins.then_inc(hT_ready, 1)

            over_spans(act, body)
            act.wait_ge(var_ready, SPANS + 1)
            nc.scalar.activation(s1["root"][:], s1["var"][:], ACT.Sqrt).then_inc(root_ready, 1)

        @block.tensor
        def _(pe):
            pe.wait_ge(const_in, 32)

            def turn_to_tokens(g, u):
                pe.wait_ge(hs_ready, g + 1)
                for j in range(4):
                    for m in range(DH):
                        ins = nc.tensor.transpose(h_ps[:, u, j, m * P:(m + 1) * P], hs[:, u, m, j * P:(j + 1) * P], k["ident"][:])
                ins.then_inc(h_psum, 1)

            turn_to_tokens(0, 0)

            def body(g, u, is_first, is_last):
                if not is_last:
                    turn_to_tokens(g + 1, 1 - u)
                pe.wait_ge(hn_ready, g + 1)
                for m in range(DH):
                    for j in range(4):
                        ins = nc.tensor.transpose(hT_ps[:, m, j * P:(j + 1) * P], hn[:, j, m * P:(m + 1) * P], k["ident"][:])
                ins.then_inc(hT_psum, 1)
                pe.wait_ge(hT_ready, g + 1)
                if not is_first:
                    pe.wait_ge(x1_ready, g)
                for j in range(4):
                    for q in range(DH):
                        ins = nc.tensor.matmul(o_ps[:, j, :], hT[:, q, j * P:(j + 1) * P], wo[:, q, :],
                                               start=(q == 0), stop=(q == DH - 1))
                ins.then_inc(o_psum, 1)

            over_spans(pe, body)

        @block.vector
        def _(vec):
            def take_products(mine, g, u):
                vec.wait_ge(o_psum, g + 1)
                vec.wait_ge(xb_ready, g + 1)
                mine.add(nc.vector.tensor_tensor(x1[:, u, :, :], o_ps[:], x1[:, u, :, :], ALU.add))
                mine.wait(vec)
                for j in range(4):
                    ins = nc.vector.bn_stats(sums1[:, bass.ds(g * 4 + j, 1), :].rearrange("p o c -> p (o c)"), x1[:, u, j, :])
                ins.then_inc(x1_ready, 1)

            def body(g, u, is_first, is_last):
                mine = Steps(own, 0 if is_first else g * 16 - 1)
                vec.wait_ge(h_psum, g + 1)
                for j in range(4):
                    mine.add(nc.vector.bn_stats(sums[:, j, :], h_ps[:, u, j, :]))
                statistics(nc, vec, mine, s, sums, lambda ins: ins.then_inc(var_ready, 1), 4)
                if not is_first:
                    take_products(mine, g - 1, 1 - u)
                vec.wait_ge(root_ready, g + 1)
                inverse_root(nc, vec, mine, s, 4)
                mine.wait(vec)
                if not is_first:
                    vec.wait_ge(hT_psum, g)
                for j in range(4):
                    ins = nc.vector.tensor_scalar(hn[:, j, :], h_ps[:, u, j, :], s["mean"][:, j:j + 1], s["rstd"][:, j:j + 1],
                                                  ALU.subtract, ALU.mult)
                ins.then_inc(hn_ready, 1)

            over_spans(vec, body)
            mine = Steps(own, SPANS * 16 - 1)
            take_products(mine, SPANS - 1, 1)
            vec.wait_ge(x1_ready, SPANS)
            statistics(nc, vec, mine, s1, sums1, lambda ins: ins.then_inc(var_ready, 1), TILES)
            vec.wait_ge(root_ready, SPANS + 1)
            inverse_root(nc, vec, mine, s1, TILES)


def run_block(nc, sems, build_block):
    with nc.Block() as block:
        build_block(block)
    for s in sems:
        nc.gpsimd.sem_clear(s)
    nc.all_engine_barrier()


def project_batch(nc, k, b):
    acc, parts, values, vec_in = k["acc"], k["parts"], k["values"], k["vec"]
    NT = L // P
    with ExitStack() as ctx:
        names = []

        def sem(n):
            names.append(ctx.enter_context(nc.semaphore(f"tok_{n}")))
            return names[-1]

        sb = lambda n, shape, dt=F32: ctx.enter_context(nc.sbuf_tensor(f"tok_{n}", shape, dt))
        ps = lambda n, shape, dt=F32: ctx.enter_context(nc.psum_tensor(f"tok_{n}", shape, dt))
        xn = sb("xn", [P, 4, D])
        xs = sb("xs", [P, DH, SPAN])
        whole = sb("whole", [P, 2, SPAN])
        rest = sb("rest", [P, 2, SPAN])
        top, lg, ex, tot, inv, pr = (sb("top", [P, 4]), sb("lg", [P, 4, E]), sb("ex", [P, 4, E]), sb("tot", [P, 4]),
                                     sb("inv", [P, 4]), sb("pr", [P, 4, E]))
        more, same, same_before, ahead = (sb(n, [P, 4, E, E]) for n in ("more", "same", "same_before", "ahead"))
        rank = sb("rank", [P, 4, E])
        highest, lowest = sb("highest", [P, 4 * (L // SPAN)]), sb("lowest", [P, 4 * (L // SPAN)])
        widest, wide, both, by_head = (sb("widest", [P, 4 * (L // SPAN)]), sb("wide", [P, 4]), sb("both", [P, DH]), sb("by_head", [P, HEADS]))
        bound, safe, all_safe = sb("bound", [P, HEADS]), sb("safe", [P, HEADS]), sb("all_safe", [P, 1])
        share = sb("share", [P, 4, 32])
        shareT = sb("shareT", [P, 4, 32])
        xT_ps = ps("xT_ps", [P, DH, SPAN])
        qk_ps, v_ps = ps("qk_ps", [P, 2, SPAN]), ps("v_ps", [P, 2, D])
        e_ps, l_ps = ps("e_ps", [P, 2, 2 * D]), ps("l_ps", [P, 4, E])
        bias_ps = xT_ps[:].rearrange("p m t -> p (m t)").rearrange("p (j d) -> p j d", j=4)
        head_ps, safe_ps = l_ps[:].rearrange("p j e -> p (j e)")[:, 0:HEADS], l_ps[0:1, 2, 0:1]
        x_first, x_rest, own = sem("x_first"), sem("x_rest"), sem("own")
        by_head_ready, bound_psum, safe_ready, safe_psum = (sem(n) for n in ("by_head_ready", "bound_psum", "safe_ready", "safe_psum"))
        xn_ready, xT_psum, xs_low, xs_high, l_psum, lg_ready, ex_ready, share_ready, bias_psum, bias_taken = (
            sem(n) for n in ("xn_ready", "xT_psum", "xs_low", "xs_high", "l_psum", "lg_ready", "ex_ready",
                             "share_ready", "bias_psum", "bias_taken"))
        v_psum, v_taken, qk_psum, qk_taken, rest_taken, e_psum, e_taken = (
            sem(n) for n in ("v_psum", "v_taken", "qk_psum", "qk_taken", "rest_taken", "e_psum", "e_taken"))
        G = L // SPAN

        def spans(eng, body):
            body(0, True)
            with eng.Fori(1, G) as g:
                body(g, False)

        def blocks(block):
            x1v = k["x1"].rearrange("(b j p) d -> p b j d", p=P, j=NT)

            @block.sync
            def _(sp):
                for sem_, lo, hi in ((x_first, 0, 4), (x_rest, 4, NT)):
                    sp.dma_start(acc[:, lo:hi, :], x1v[:, bass.ds(b, 1), lo:hi, :].rearrange("p b j d -> p (b j) d")).then_inc(sem_, 16)

            @block.scalar
            def _(act):
                def body(g, is_first):
                    act.wait_ge(xT_psum, g + 1)
                    if not is_first:
                        act.wait_ge(e_psum, g * 16)
                    nc.scalar.copy(xs[:, 0, :], xT_ps[:, 0, :]).then_inc(xs_low, 1)
                    act.wait_ge(lg_ready, g + 1)
                    nc.scalar.activation(ex[:], lg[:], ACT.Exp).then_inc(ex_ready, 1)
                    for o in range(4):
                        v = V_BQ + o if o < 2 else V_BK + o - 2
                        act.wait_ge(qk_psum, g * 4 + o + 1)
                        if o >= 2 or not is_first:
                            act.wait_ge(rest_taken, g * 4 + o - 1)
                        nc.scalar.activation(parts[:, 3 * (o // 2), o % 2, bass.ds(g * SPAN, SPAN)], qk_ps[:, o % 2, :],
                                             ACT.Identity, bias=vec_in[:, v:v + 1])
                        nc.scalar.activation(whole[:, o % 2, :], qk_ps[:, o % 2, :], ACT.Identity,
                                             bias=vec_in[:, v:v + 1]).then_inc(qk_taken, 1)

                spans(act, body)

            @block.tensor
            def _(pe):
                def body(g, is_first):
                    pe.wait_ge(xn_ready, g + 1)
                    if not is_first:
                        pe.wait_ge(bias_taken, g)
                    for m in range(DH):
                        for j in range(4):
                            ins = nc.tensor.transpose(xT_ps[:, m, j * P:(j + 1) * P], xn[:, j, m * P:(m + 1) * P], k["ident"][:])
                    ins.then_inc(xT_psum, 1)
                    pe.wait_ge(xs_low, g + 1)
                    pe.wait_ge(xs_high, g + 1)
                    if not is_first:
                        pe.wait_ge(lg_ready, g)
                    for j in range(4):
                        at = slice(j * P, (j + 1) * P)
                        for q in range(DH):
                            nc.tensor.matmul(l_ps[:, j, :], xs[:, q, at], k["wgate"][:, q, :], start=(q == 0), stop=False)
                        ins = nc.tensor.matmul(l_ps[:, j, :], k["row"][0:1, 0:P], k["row"][0:1, P:P + E], start=False, stop=True)
                    ins.then_inc(l_psum, 1)

                    def two_values(pair):
                        if pair or not is_first:
                            pe.wait_ge(v_taken, g * 2 + pair)
                        for j in range(2 * pair, 2 * pair + 2):
                            for q in range(DH):
                                ins = nc.tensor.matmul(v_ps[:, j % 2, :], xs[:, q, j * P:(j + 1) * P], k["wqkv"][:, q, 2 * D:3 * D],
                                                       start=(q == 0), stop=(q == DH - 1))
                        ins.then_inc(v_psum, 1)

                    two_values(0)
                    for o in range(4):
                        if o == 2:
                            two_values(1)
                        if o >= 2 or not is_first:
                            pe.wait_ge(qk_taken, g * 4 + o - 1)
                        for q in range(DH):
                            ins = nc.tensor.matmul(qk_ps[:, o % 2, :], k["wqkv"][:, q, o * P:(o + 1) * P], xs[:, q, :],
                                                   start=(q == 0), stop=(q == DH - 1))
                        ins.then_inc(qk_psum, 1)
                    for n in range(16):
                        j, e2 = n // 4, n % 4
                        if n >= 2 or not is_first:
                            pe.wait_ge(e_taken, g * 16 + n - 1)
                        for q in range(DH):
                            ins = nc.tensor.matmul(e_ps[:, n % 2, :], xs[:, q, j * P:(j + 1) * P],
                                                   k["wexp"][:, q, e2 * 2 * D:(e2 + 1) * 2 * D], start=(q == 0), stop=(q == DH - 1))
                        ins.then_inc(e_psum, 1)
                    for j in range(4):
                        for r in range(4):
                            at = slice(32 * r, 32 * r + 32)
                            ins = nc.tensor.matmul(bias_ps[at, j, :], shareT[at, j, :], k["bexp"][at, :], start=True, stop=True)
                    ins.then_inc(bias_psum, 1)

                spans(pe, body)
                pe.wait_ge(by_head_ready, 1)
                nc.tensor.matmul(head_ps, k["all_ones"][:], by_head[:], start=True, stop=True).then_inc(bound_psum, 1)
                pe.wait_ge(safe_ready, 1)
                nc.tensor.matmul(safe_ps, k["all_ones"][:, 0:1], all_safe[:], start=True, stop=True).then_inc(safe_psum, 1)

            @block.vector
            def _(vec):
                OWN = 34

                def body(g, is_first):
                    mine = Steps(own, g * OWN + 1)
                    t0 = b * NT + g * 4
                    for j in range(4):
                        ins = nc.vector.tensor_scalar(xn[:, j, :], acc[:, bass.ds(g * 4 + j, 1), :].rearrange("p o d -> p (o d)"),
                                                      k["mean1"][:, bass.ds(t0 + j, 1)], k["rstd1"][:, bass.ds(t0 + j, 1)],
                                                      ALU.subtract, ALU.mult)
                    ins.then_inc(xn_ready, 1)
                    vec.wait_ge(xT_psum, g + 1)
                    nc.vector.tensor_copy(xs[:, 1, :], xT_ps[:, 1, :]).then_inc(xs_high, 1)
                    vec.wait_ge(l_psum, g + 1)
                    mine.add(nc.vector.tensor_reduce(top[:], l_ps[:], AX.X, ALU.max))
                    mine.wait(vec)
                    nc.vector.tensor_tensor(lg[:], l_ps[:], top[:].unsqueeze(2).to_broadcast([P, 4, E]),
                                            ALU.subtract).then_inc(lg_ready, 1)
                    for pair in range(2):
                        vec.wait_ge(v_psum, g * 2 + pair + 1)
                        nc.vector.tensor_tensor(values[:, bass.ds(g * 4 + 2 * pair, 2), :, 0:HD],
                                                v_ps[:].rearrange("p j (h d) -> p j h d", d=HD),
                                                k["bv"][:].rearrange("p (h d) -> p h d", d=HD).unsqueeze(1).to_broadcast([P, 2, HEADS, HD]),
                                                ALU.add).then_inc(v_taken, 1)
                    vec.wait_ge(ex_ready, g + 1)
                    mine.add(nc.vector.tensor_reduce(tot[:], ex[:], AX.X, ALU.add))
                    mine.wait(vec)
                    mine.add(nc.vector.reciprocal(inv[:], tot[:]))
                    mine.wait(vec)
                    mine.add(nc.vector.tensor_tensor(pr[:], ex[:], inv[:].unsqueeze(2).to_broadcast([P, 4, E]), ALU.mult))
                    mine.wait(vec)
                    each = pr[:].unsqueeze(3).to_broadcast([P, 4, E, E])
                    other = pr[:].unsqueeze(2).to_broadcast([P, 4, E, E])
                    mine.add(nc.vector.tensor_tensor(more[:], other, each, ALU.is_gt))
                    mine.add(nc.vector.tensor_tensor(same[:], other, each, ALU.is_equal))
                    mine.wait(vec)
                    mine.add(nc.vector.tensor_tensor(same_before[:], same[:], k["lower"][:].unsqueeze(1).to_broadcast([P, 4, E, E]), ALU.mult))
                    mine.wait(vec)
                    mine.add(nc.vector.tensor_tensor(ahead[:], more[:], same_before[:], ALU.add))
                    mine.wait(vec)
                    mine.add(nc.vector.tensor_reduce(rank[:], ahead[:], AX.X, ALU.add))
                    mine.wait(vec)
                    mine.add(nc.vector.scalar_tensor_tensor(out=share[:, :, 0:E], in0=rank[:], scalar=TOP_K - 0.5, in1=pr[:],
                                                            op0=ALU.is_lt, op1=ALU.mult))
                    mine.wait(vec)
                    nc.vector.transpose(shareT[:].rearrange("p j c -> p (j c)"), share[:].rearrange("p j c -> p (j c)")).then_inc(share_ready, 1)
                    for o in range(4):
                        first = 3 * (o // 2)
                        at = bass.ds(g * SPAN, SPAN)
                        vec.wait_ge(qk_taken, g * 4 + o + 1)
                        nc.vector.tensor_reduce(highest[:, bass.ds(g * 4 + o, 1)], whole[:, o % 2, :], AX.X, ALU.max)
                        nc.vector.tensor_reduce(lowest[:, bass.ds(g * 4 + o, 1)], whole[:, o % 2, :], AX.X, ALU.min)
                        nc.vector.tensor_tensor(rest[:, o % 2, :], whole[:, o % 2, :], parts[:, first, o % 2, at],
                                                ALU.subtract).then_inc(rest_taken, 1)
                        vec.wait_ge(rest_taken, g * 4 + o + 1)
                        mine.add(nc.vector.tensor_copy(parts[:, first + 1, o % 2, at], rest[:, o % 2, :]))
                        mine.wait(vec)
                        mine.add(nc.vector.tensor_tensor(parts[:, first + 2, o % 2, at], rest[:, o % 2, :],
                                                         parts[:, first + 1, o % 2, at], ALU.subtract))
                    for n in range(16):
                        j, e2 = n // 4, n % 4
                        mine_at = acc[:, bass.ds(g * 4 + j, 1), :].rearrange("p o d -> p (o d)")
                        vec.wait_ge(e_psum, g * 16 + n + 1)
                        for e in range(2):
                            ins = nc.vector.scalar_tensor_tensor(
                                out=mine_at, in0=e_ps[:, n % 2, e * D:(e + 1) * D],
                                scalar=share[:, j, 2 * e2 + e:2 * e2 + e + 1], in1=mine_at, op0=ALU.mult, op1=ALU.add)
                            if e == 0:
                                mine.add(ins)
                                mine.wait(vec)
                        ins.then_inc(e_taken, 1)
                        vec.wait_ge(e_taken, g * 16 + n + 1)
                    vec.wait_ge(bias_psum, g + 1)
                    nc.vector.tensor_tensor(acc[:, bass.ds(g * 4, 4), :], bias_ps, acc[:, bass.ds(g * 4, 4), :],
                                            ALU.add).then_inc(bias_taken, 1)
                    vec.wait_ge(bias_taken, g + 1)
                    assert mine.n == OWN, mine.n

                nc.vector.memset(share[:], 0.0).then_inc(own, 1)
                vec.wait_ge(own, 1)
                vec.wait_ge(x_first, 16)
                body(0, True)
                vec.wait_ge(x_rest, 16)
                with vec.Fori(1, G) as g:
                    body(g, False)
                mine = Steps(own, G * OWN + 1)
                mine.wait(vec)
                mine.add(nc.vector.scalar_tensor_tensor(out=widest[:], in0=lowest[:], scalar=-1.0, in1=highest[:],
                                                        op0=ALU.mult, op1=ALU.max))
                mine.wait(vec)
                mine.add(nc.vector.tensor_reduce(wide[:], widest[:].rearrange("p (g o) -> p o g", o=4), AX.X, ALU.max))
                mine.wait(vec)
                mine.add(nc.vector.tensor_tensor(both[:], wide[:, 0:2], wide[:, 2:4], ALU.mult))
                mine.wait(vec)
                for m in range(DH):
                    ins = nc.vector.tensor_scalar(by_head[:, 8 * m:8 * m + 8], k["member"][:, 0:8], both[:, m:m + 1], None, ALU.mult)
                ins.then_inc(by_head_ready, 1)
                vec.wait_ge(bound_psum, 1)
                mine.add(nc.vector.tensor_scalar(k["shift"][:], head_ps, k["member"][:, 8:9], None, ALU.mult))
                mine.add(nc.vector.tensor_scalar(safe[:], head_ps, SAFE, None, ALU.is_le))
                mine.wait(vec)
                nc.vector.tensor_reduce(all_safe[:], safe[:], AX.X, ALU.min).then_inc(safe_ready, 1)
                vec.wait_ge(safe_psum, 1)
                nc.vector.tensor_copy(k["ranged"][:], safe_ps)

        run_block(nc, names, blocks)


SAFE = 160.0

Q_PARTS = (0, 0, 1, 0, 2, 1)
K_PARTS = (3, 4, 3, 5, 3, 4)
ROWS = 6 * 16
GH = 4


def load_stacks(nc, k, eng, s, m, arrived):
    for which, plan in (("qst", Q_PARTS), ("kst", K_PARTS)):
        for i, part in enumerate(plan):
            for h in range(GH):
                at = 64 * s + HD * h
                eng.dma_start(k[which][HD * i:HD * i + HD, s, h, :],
                              k["parts"][at:at + HD, part, bass.ds(m, 1), :].rearrange("p o t -> p (o t)")).then_inc(arrived, 16)
    return 2 * 6 * GH * 16


def load_first(nc, k):
    with ExitStack() as ctx:
        arrived = ctx.enter_context(nc.semaphore("first_arrived"))

        def blocks(block):
            @block.sync
            def _(sp):
                sp.wait_ge(arrived, load_stacks(nc, k, sp, 0, 0, arrived))

            @block.gpsimd
            def _(pool):
                shift_by_bound(nc, k, 0, 0)

        run_block(nc, [arrived], blocks)


def shift_by_bound(nc, k, s, m):
    return nc.gpsimd.tensor_tensor(k["qst"][ROWS:ROWS + 3, s, :, :], k["kst"][ROWS:ROWS + 3, s, :, :],
                                   k["shift"][ROWS:ROWS + 3, bass.ds(m * 8 + s * GH, GH)].unsqueeze(2).to_broadcast([3, GH, L]),
                                   ALU.mult)


def find_maxima(nc, k, s, when):
    qst, kst = k["qst"], k["kst"]
    QT = L // P
    with ExitStack() as ctx:
        names = []

        def sem(n):
            names.append(ctx.enter_context(nc.semaphore(f"max{s}_{n}")))
            return names[-1]

        sb = lambda n, shape, dt=F32: ctx.enter_context(nc.sbuf_tensor(f"max{s}_{n}", shape, dt))
        ps = lambda n, shape, dt=F32: ctx.enter_context(nc.psum_tensor(f"max{s}_{n}", shape, dt))
        big, neg = sb("big", [P, GH * QT]), sb("neg", [P, GH * QT])
        rows, left = sb("rows", [GH * QT, P]), sb("left", [GH * QT, P])
        three = sb("three", [GH * QT, 3, P], BF16)
        s_ps = ps("s_ps", [P, 4, SPAN])
        n_ps = ps("n_ps", [P, P])
        s_psum, s_taken, neg_ready, n_psum, own, three_ready, moved = (
            sem(n) for n in ("s_psum", "s_taken", "neg_ready", "n_psum", "own", "three_ready", "moved"))

        def blocks(block):
            @block.tensor
            def _(pe):
                pe.sem_inc(s_taken, 1)
                with when(pe):
                    with pe.Fori(0, GH * QT) as n:
                        pe.wait_ge(s_taken, n + 1)
                        q_tile = qst[0:ROWS, s, :, :].rearrange("r h t -> r (h t)")[:, bass.ds(n * P, P)]
                        for c in range(4):
                            h_off = (n // QT) * L + c * SPAN
                            ins = nc.tensor.matmul(s_ps[:, c, :], q_tile,
                                                   kst[0:ROWS, s, :, :].rearrange("r h t -> r (h t)")[:, bass.ds(h_off, SPAN)],
                                                   start=True, stop=True)
                        ins.then_inc(s_psum, 1)
                    pe.wait_ge(neg_ready, 1)
                    nc.tensor.transpose(n_ps[0:GH * QT, :], neg[:], k["ident"][:]).then_inc(n_psum, 1)

            @block.vector
            def _(vec):
                with when(vec):
                    with vec.Fori(0, GH * QT) as n:
                        vec.wait_ge(s_psum, n + 1)
                        nc.vector.tensor_reduce(big[:, bass.ds(n, 1)], s_ps[:], AX.XY, ALU.max).then_inc(s_taken, 1)
                    vec.wait_ge(s_taken, GH * QT + 1)
                    nc.vector.tensor_scalar(neg[:], big[:], -1.0, None, ALU.mult).then_inc(neg_ready, 1)
                    mine = Steps(own)
                    vec.wait_ge(n_psum, 1)
                    mine.add(nc.vector.tensor_copy(rows[:], n_ps[0:GH * QT, :]))
                    mine.wait(vec)
                    mine.add(nc.vector.tensor_copy(three[:, 0, :], rows[:]))
                    mine.wait(vec)
                    mine.add(nc.vector.tensor_tensor(left[:], rows[:], three[:, 0, :], ALU.subtract))
                    mine.wait(vec)
                    mine.add(nc.vector.tensor_copy(three[:, 1, :], left[:]))
                    mine.wait(vec)
                    nc.vector.tensor_tensor(three[:, 2, :], left[:], three[:, 1, :], ALU.subtract).then_inc(three_ready, 1)

            @block.sync
            def _(sp):
                with when(sp):
                    sp.wait_ge(three_ready, 1)
                    for i in range(3):
                        sp.dma_start(qst[ROWS + i:ROWS + i + 1, s, :, :].rearrange("o h (t c) -> o (h t) c", c=P),
                                     three[:, i, :]).then_inc(moved, 16)
                    sp.wait_ge(moved, 48)

        run_block(nc, names, blocks)


def attend(nc, k, s, hp):
    qst, kst, acc = k["qst"], k["kst"], k["acc"]
    KT, UNITS = L // P, 2 * (L // P)
    VC = HD + 1
    with ExitStack() as ctx:
        names = []

        def sem(n):
            names.append(ctx.enter_context(nc.semaphore(f"att{s}_{n}")))
            return names[-1]

        sb = lambda n, shape, dt=F32: ctx.enter_context(nc.sbuf_tensor(f"att{s}_{n}", shape, dt))
        ps = lambda n, shape, dt=F32: ctx.enter_context(nc.psum_tensor(f"att{s}_{n}", shape, dt))
        probs = sb("probs", [P, 4, 2, SPAN])
        mixed = sb("mixed", [P, SPAN])
        vg = sb("vg", [P, KT, GH, VC])
        inv, out = sb("inv", [P, 4 * GH]), sb("out", [P, 4 * GH, HD])
        s_ps = ps("s_ps", [P, 3, 2, SPAN])
        pv_ps, oT_ps = ps("pv_ps", [P, SPAN]), ps("oT_ps", [P, 4, P])
        s_psum, exp_done, pv_done, mixed_ready, oT_psum, own, vg_ready, arrived, added = (
            sem(n) for n in ("s_psum", "exp_done", "pv_done", "mixed_ready", "oT_psum", "own", "vg_ready", "arrived", "added"))

        def query_spans(eng, body):
            body(0, True)
            with eng.Fori(1, L // SPAN) as it:
                body(it, False)

        def blocks(block):
            @block.sync
            def _(sp):
                sp.wait_ge(arrived, load_stacks(nc, k, sp, 1 - s, hp if s == 0 else 1 - hp, arrived))

            @block.gpsimd
            def _(pool):
                nc.gpsimd.tensor_copy(vg[:], k["values"][:, :, bass.ds(hp * 8 + s * 4, 4), :]).then_inc(vg_ready, 1)
                pool.wait_ge(vg_ready, 1)
                shift_by_bound(nc, k, 1 - s, hp if s == 0 else 1 - hp)

            @block.tensor
            def _(pe):
                def scores(it, u):
                    kt, pair = u // 2, u % 2
                    for h in range(2):
                        ins = nc.tensor.matmul(s_ps[:, u % 3, h, :], kst[0:ROWS + 3, s, 2 * pair + h, kt * P:(kt + 1) * P],
                                               qst[0:ROWS + 3, s, 2 * pair + h, bass.ds(it * SPAN, SPAN)], start=True, stop=True)
                    ins.then_inc(s_psum, 1)

                def turn_back(it):
                    pe.wait_ge(mixed_ready, it)
                    for c in range(4):
                        ins = nc.tensor.transpose(oT_ps[:, c, :], mixed[:, c * P:(c + 1) * P], k["ident"][:])
                    ins.then_inc(oT_psum, 1)

                def body(it, is_first):
                    for u, last in ((0, 30), (1, 31), (2, 29)):
                        if not is_first:
                            pe.wait_ge(exp_done, it * UNITS - UNITS + last + 1)
                        scores(it, u)
                    for kt in range(KT):
                        if 2 * kt + 3 < UNITS:
                            pe.wait_ge(exp_done, it * UNITS + 2 * kt + 1)
                            scores(it, 2 * kt + 3)
                        pe.wait_ge(exp_done, it * UNITS + 2 * kt + 2)
                        if kt == 0:
                            if is_first:
                                pe.wait_ge(vg_ready, 1)
                            else:
                                pe.wait_ge(mixed_ready, it)
                        for h in range(GH):
                            ins = nc.tensor.matmul(pv_ps[32 * h:32 * h + VC, :], vg[:, kt, h, :],
                                                   probs[:, (2 * kt + h // 2) % 4, h % 2, :], start=(kt == 0), stop=(kt == KT - 1))
                        ins.then_inc(pv_done, 1)
                        if 2 * kt + 4 < UNITS:
                            scores(it, 2 * kt + 4)
                        if kt == 3 and not is_first:
                            turn_back(it)

                nc.tensor.matmul(pv_ps[:], k["zero"][0:ROWS, :], kst[0:ROWS, s, 0, 0:SPAN], start=True, stop=True)
                query_spans(pe, body)
                turn_back(L // SPAN)

            @block.scalar
            def _(act):
                def body(it, is_first):
                    for u in range(UNITS):
                        act.wait_ge(s_psum, it * UNITS + u + 1)
                        if u >= 4 or not is_first:
                            act.wait_ge(pv_done, it * KT + u // 2 - 1)
                        nc.scalar.activation(probs[:, u % 4, :, :], s_ps[:, u % 3, :, :], ACT.Exp,
                                             scale=HD ** -0.5).then_inc(exp_done, 1)

                query_spans(act, body)

            @block.vector
            def _(vec):
                with vec.Fori(0, L // SPAN) as it:
                    mine = Steps(own, it * 2)
                    vec.wait_ge(pv_done, it * KT + KT)
                    nc.vector.tensor_copy(mixed[:], pv_ps[:]).then_inc(mixed_ready, 1)
                    vec.wait_ge(oT_psum, it + 1)
                    heads = oT_ps[:].rearrange("p c (h e) -> p (c h) e", e=32)
                    mine.add(nc.vector.reciprocal(inv[:], heads[:, :, HD]))
                    mine.wait(vec)
                    mine.add(nc.vector.tensor_tensor(out[:], heads[:, :, 0:HD], inv[:].unsqueeze(2).to_broadcast([P, 4 * GH, HD]), ALU.mult))
                    mine.wait(vec)
                    at = acc[:, bass.ds(it * 4, 4), bass.ds(hp * P + s * 64, GH * HD)]
                    nc.vector.tensor_tensor(at, at, out[:].rearrange("p (c h) d -> p c (h d)", c=4), ALU.add).then_inc(added, 1)

        run_block(nc, names, blocks)


def store_batch(nc, k, b):
    with ExitStack() as ctx:
        stored = ctx.enter_context(nc.semaphore("batch_stored"))

        def blocks(block):
            @block.sync
            def _(sp):
                sp.dma_start(k["out"].rearrange("(b j p) d -> p b j d", p=P, j=L // P)[:, bass.ds(b, 1), :, :]
                             .rearrange("p b j d -> p (b j) d"), k["acc"][:]).then_inc(stored, 16)
                sp.wait_ge(stored, 16)

        run_block(nc, [stored], blocks)


def load_ffn_constants(nc, k):
    with ExitStack() as ctx:
        arrived = ctx.enter_context(nc.semaphore("ffn_arrived"))
        block = ctx.enter_context(nc.Block())

        @block.sync
        def _(sp):
            halves = lambda a: a.rearrange("(k p) e -> p k e", p=P)
            for dst, src in (("wqkv", halves(k["in_wqkv"])), ("wexp", halves(k["in_wexp"])), ("wgate", halves(k["in_wgate"])),
                             ("bv", k["in_bv"]), ("bexp", k["in_bexp"]), ("row", k["in_row"]), ("lower", k["in_lower"]),
                             ("member", k["in_member"])):
                sp.dma_start(k[dst][:], src).then_inc(arrived, 16)
            sp.wait_ge(arrived, 8 * 16)

        @block.vector
        def _(vec):
            nc.vector.memset(k["zero"][:], 0.0)
            nc.vector.memset(k["all_ones"][:], 1.0)
            nc.vector.memset(k["qst"][ROWS:ROWS + 3, :, :, :], 0.0)
            nc.vector.memset(k["values"][:], 1.0)
            nc.vector.memset(k["kst"][ROWS:ROWS + 3, :, :, :], 1.0)


def feed_forward(nc, k):
    with ExitStack() as ctx:
        sb = lambda n, shape, dt=F32: ctx.enter_context(nc.sbuf_tensor(n, shape, dt))
        k["acc"] = sb("acc", [P, L // P, D])
        k["parts"] = sb("parts", [P, 6, DH, L], BF16)
        k["values"] = sb("values", [P, L // P, HEADS, HD + 1])
        k["qst"] = sb("qst", [P, 2, GH, L], BF16)
        k["kst"] = sb("kst", [P, 2, GH, L], BF16)
        k["wqkv"], k["wexp"], k["wgate"] = sb("wqkv", [P, DH, 3 * D]), sb("wexp", [P, DH, E * D]), sb("wgate", [P, DH, E])
        k["bv"], k["bexp"], k["row"], k["lower"] = sb("bv", [P, D]), sb("bexp", [P, D]), sb("row", [1, P + E]), sb("lower", [P, E, E])
        k["zero"] = sb("zero", [P, P], BF16)
        k["all_ones"], k["member"], k["shift"] = sb("all_ones", [P, P]), sb("member", [P, 9]), sb("shift", [P, HEADS])
        k["ranged"] = sb("ranged", [1, 1], I32)
        load_ffn_constants(nc, k)
        with nc.Fori(0, B) as b:
            project_batch(nc, k, b)
            load_first(nc, k)
            with nc.Fori(0, 2) as hp:
                for s in range(2):
                    find_maxima(nc, k, s, unless(k["ranged"]))
                    attend(nc, k, s, hp)
            store_batch(nc, k, b)


def build(nc, io):
    with ExitStack() as ctx:
        sb = lambda name, shape, dt=F32: ctx.enter_context(nc.sbuf_tensor(name, shape, dt))
        k = dict(io)
        k["vec"] = sb("vec", [P, NVEC])
        k["ident"] = sb("ident", [P, P])
        k["wr"] = sb("wr", [P, DH, D])
        k["keep"] = sb("keep", [P, DH])
        k["away"] = sb("away", [P, DH])
        k["mean1"], k["rstd1"] = sb("mean1", [P, TILES]), sb("rstd1", [P, TILES])
        with ExitStack() as scan:
            sb2 = lambda name, shape, dt=F32: scan.enter_context(nc.sbuf_tensor(name, shape, dt))
            k["xy"] = sb2("xy", [P, TILES, D])
            inner = scan.enter_context(ExitStack())
            sb2 = lambda name, shape, dt=F32: inner.enter_context(nc.sbuf_tensor(name, shape, dt))
            k["gain"] = sb2("gain", [P, DH, T])
            k["drive"] = sb2("drive", [P, DH, T])
            normalise_and_gate(nc, k)
            k["state"] = sb2("state", [P, 2, DH, GL])
            k["start"] = sb2("start", [P, 2, DH, GL])
            k["ones"] = sb2("ones", [P, P])
            k["agree"] = sb2("agree", [1, 1], I32)
            clear_states(nc, k)
            sweep(nc, k, "sweep", SWEEPS)
            look_at_defect(nc, k)
            sweep(nc, k, "rest", CHUNKS, unless(k["agree"]))
            inner.close()
            project_states(nc, k)
        feed_forward(nc, k)


def kernel(L0_attn_x, L0_attn_decay, L0_attn_Wr, L0_attn_br, L0_attn_Wg, L0_attn_bg, L0_attn_Wo, L0_attn_bo,
           L0_attn_ln_w, L0_attn_ln_b, L0_ffn_W_qkv, L0_ffn_b_qkv, L0_ffn_W_gate, L0_ffn_b_gate,
           L0_ffn_W_experts, L0_ffn_b_experts):
    import numpy as np
    import concourse.bacc as bacc
    from concourse.bass_utils import run_bass_kernel_spmd

    lay = np.ascontiguousarray
    halves = lambda v: np.asarray(v).reshape(DH, P).T
    bqkv = np.asarray(L0_ffn_b_qkv)
    member = np.zeros((P, 9), np.float32)
    member[:, 0:8] = np.repeat(np.eye(8, dtype=np.float32), HD, axis=0)
    member[ROWS, 8] = -1.0
    spread = np.zeros((P, D), np.float32)
    for r in range(0, P, 32):
        spread[r:r + E] = np.asarray(L0_ffn_b_experts)
    arrays = {
        "in_x": lay(np.asarray(L0_attn_x).reshape(T, D)),
        "in_vec": lay(np.concatenate([halves(v) for v in (L0_attn_decay, L0_attn_br, L0_attn_bg, L0_attn_ln_w,
                                                          L0_attn_ln_b, bqkv[0:D], bqkv[D:2 * D])], axis=1)),
        "in_ident": np.eye(P, dtype=np.float32),
        "in_wg": lay(np.asarray(L0_attn_Wg).T),
        "in_wr": lay(np.asarray(L0_attn_Wr).T),
        "in_wo": lay(np.asarray(L0_attn_Wo).T),
        "in_wqkv": lay(np.asarray(L0_ffn_W_qkv)),
        "in_wexp": lay(np.asarray(L0_ffn_W_experts).transpose(1, 0, 2).reshape(D, E * D)),
        "in_wgate": lay(np.asarray(L0_ffn_W_gate)),
        "in_bv": lay(np.broadcast_to(bqkv[2 * D:], (P, D))),
        "in_bexp": spread,
        "in_row": lay(np.concatenate([np.ones(P, np.float32), np.asarray(L0_ffn_b_gate)])[None]),
        "in_member": member,
        "in_lower": lay(np.broadcast_to(np.tri(E, k=-1, dtype=np.float32), (P, E, E))),
        "in_bo": lay(np.broadcast_to(np.asarray(L0_attn_bo), (P, D))),
    }
    nc = bacc.Bacc("TRN2", target_bir_lowering=False, num_devices=1)
    io = {n: nc.dram_tensor(n, a.shape, mybir.dt.from_np(a.dtype), kind="ExternalInput").ap() for n, a in arrays.items()}
    io["out"] = nc.dram_tensor("out", (T, D), F32, kind="ExternalOutput").ap()
    io["x1"] = nc.dram_tensor("x1", (T, D), F32).ap()
    build(nc, io)
    r = run_bass_kernel_spmd(nc, [arrays], core_ids=[0])
    return r.results[0]["out"].reshape(B, L, D)
```

```python
from contextlib import ExitStack, nullcontext

import concourse.bass as bass
from concourse import mybir

F32 = mybir.dt.float32
BF16 = mybir.dt.bfloat16
I32 = mybir.dt.int32
ALU = mybir.AluOpType
ACT = mybir.ActivationFunctionType
AX = mybir.AxisListType

P = 128
B, L, D = 4, 2048, 256
DH = D // P
T = B * L
TILES = T // P
EPS = 1e-5

SPAN = 512
SPANS = T // SPAN

STEPS = 32
CHUNKS = L // STEPS
LANES = B * CHUNKS
GL = LANES // 2
GB = B // 2
SWEEPS = 4
TOLERANCE = 2.0 ** -21

HEADS, HD = 16, 16
E, TOP_K = 8, 2

V_DECAY, V_BR, V_BG, V_LNW, V_LNB, V_BQ, V_BK = range(0, 14, 2)
NVEC = 14


class Steps:

    def __init__(self, sem, start=0):
        self.sem, self.start, self.n = sem, start, 0

    def add(self, ins):
        ins.then_inc(self.sem, 1)
        self.n += 1
        return self.start + self.n

    def wait(self, eng):
        eng.wait_ge(self.sem, self.start + self.n)


def statistics(nc, vec, own, s, sums, spread, n):
    me, mo = sums[:, 0:n, 1], sums[:, 0:n, 4]
    qe, qo = sums[:, 0:n, 2], sums[:, 0:n, 5]
    own.wait(vec)
    own.add(nc.vector.tensor_tensor(s["a"][:, 0:n], me, mo, ALU.add))
    own.add(nc.vector.tensor_tensor(s["b"][:, 0:n], me, mo, ALU.subtract))
    own.add(nc.vector.tensor_tensor(s["c"][:, 0:n], qe, qo, ALU.add))
    own.wait(vec)
    own.add(nc.vector.tensor_scalar(s["mean"][:, 0:n], s["a"][:, 0:n], 0.5, None, ALU.mult))
    own.add(nc.vector.tensor_tensor(s["d"][:, 0:n], s["b"][:, 0:n], s["b"][:, 0:n], ALU.mult))
    own.wait(vec)
    own.add(nc.vector.tensor_scalar(s["e"][:, 0:n], s["d"][:, 0:n], 0.25, EPS, ALU.mult, ALU.add))
    own.wait(vec)
    spread(nc.vector.scalar_tensor_tensor(out=s["var"][:, 0:n], in0=s["c"][:, 0:n], scalar=1.0 / D,
                                          in1=s["e"][:, 0:n], op0=ALU.mult, op1=ALU.add))


def inverse_root(nc, vec, own, s, n):
    own.add(nc.vector.reciprocal(s["a"][:, 0:n], s["root"][:, 0:n]))
    own.wait(vec)
    own.add(nc.vector.tensor_tensor(s["b"][:, 0:n], s["a"][:, 0:n], s["a"][:, 0:n], ALU.mult))
    own.wait(vec)
    own.add(nc.vector.tensor_tensor(s["c"][:, 0:n], s["b"][:, 0:n], s["var"][:, 0:n], ALU.mult))
    own.wait(vec)
    own.add(nc.vector.tensor_scalar(s["d"][:, 0:n], s["c"][:, 0:n], -0.5, 1.5, ALU.mult, ALU.add))
    own.wait(vec)
    own.add(nc.vector.tensor_tensor(s["rstd"][:, 0:n], s["a"][:, 0:n], s["d"][:, 0:n], ALU.mult))


def over_spans(eng, body):
    for u in range(2):
        body(u, u, u == 0, False, False)
    with eng.Fori(1, SPANS // 2 - 1) as i:
        for u in range(2):
            body(i * 2 + u, u, False, False, False)
    for u in range(2):
        body(SPANS - 2 + u, u, False, u == 1, True)


def normalise_and_gate(nc, k):
    X, gain, drive, vec_in = k["xy"], k["gain"], k["drive"], k["vec"]
    with ExitStack() as ctx:
        sem = lambda name: ctx.enter_context(nc.semaphore(name))
        sb = lambda name, shape, dt=F32: ctx.enter_context(nc.sbuf_tensor(name, shape, dt))
        ps = lambda name, shape, dt=F32: ctx.enter_context(nc.psum_tensor(name, shape, dt))
        PARTS = 8
        PT = TILES // PARTS
        x_in = [sem(f"x_in{c}") for c in range(PARTS)]
        const_in, stats_own, var_ready, root_ready = sem("const_in"), sem("stats_own"), sem("var_ready"), sem("root_ready")
        decay_ready, gates_ready = sem("decay_ready"), sem("gates_ready")
        xn_ready, xnT_psum, xnT_ready, z_psum, z_ready, drive_own, xnT_act = (
            sem("xn_ready"), sem("xnT_psum"), sem("xnT_ready"), sem("z_psum"), sem("z_ready"), sem("drive_own"), sem("xnT_act"))
        sums = sb("sums", [P, TILES, 6])
        s = {n: sb(f"st_{n}", [P, TILES]) for n in ("a", "b", "c", "d", "e", "mean", "var", "root", "rstd")}
        xn = sb("xn", [P, 2, 4, D])
        wg = sb("wg", [P, DH, D])
        xnT_ps = ps("xnT_ps", [P, 2, DH, SPAN])
        z_ps = ps("z_ps", [P, 2, DH, SPAN])
        block = ctx.enter_context(nc.Block())

        @block.sync
        def _(sp):
            xv = k["in_x"].rearrange("(t p) d -> p t d", p=P)
            for c in range(PARTS):
                sp.dma_start(X[:, c * PT:(c + 1) * PT, :], xv[:, c * PT:(c + 1) * PT, :]).then_inc(x_in[c], 16)
                if c == 0:
                    sp.dma_start(vec_in[:], k["in_vec"]).then_inc(const_in, 16)
                    sp.dma_start(k["ident"][:], k["in_ident"]).then_inc(const_in, 16)
                    sp.dma_start(wg[:], k["in_wg"].rearrange("(k p) e -> p k e", p=P)).then_inc(const_in, 16)

        @block.vector
        def _(vec):
            own = Steps(stats_own)
            for c in range(PARTS):
                vec.wait_ge(x_in[c], 16)
                for t in range(c * PT, (c + 1) * PT):
                    own.add(nc.vector.bn_stats(sums[:, t, :], X[:, t, :]))
            statistics(nc, vec, own, s, sums, lambda ins: ins.then_inc(var_ready, 1), TILES)
            vec.wait_ge(decay_ready, 1)
            own.add(nc.vector.tensor_scalar(k["away"][:], k["keep"][:], -1.0, 1.0, ALU.mult, ALU.add))
            vec.wait_ge(root_ready, 1)
            inverse_root(nc, vec, own, s, TILES)
            own.wait(vec)

            def normalised(g, u):
                for j in range(4):
                    ins = nc.vector.tensor_scalar(xn[:, u, j, :], X[:, bass.ds(g * 4 + j, 1), :].rearrange("p o d -> p (o d)"),
                                                  s["mean"][:, bass.ds(g * 4 + j, 1)],
                                                  s["rstd"][:, bass.ds(g * 4 + j, 1)], ALU.subtract, ALU.mult)
                ins.then_inc(xn_ready, 1)

            def second_half(g, u):
                vec.wait_ge(xnT_psum, g + 1)
                nc.vector.tensor_copy(drive[:, 1, bass.ds(g * SPAN, SPAN)], xnT_ps[:, u, 1, :]).then_inc(xnT_ready, 1)

            def gain_and_drive(mine, g):
                vec.wait_ge(z_ready, 2 * g + 6)
                for m in range(DH):
                    mine.add(nc.vector.tensor_scalar(gain[:, m, bass.ds(g * SPAN, SPAN)], gain[:, m, bass.ds(g * SPAN, SPAN)],
                                                     k["away"][:, m:m + 1], None, ALU.mult))
                mine.wait(vec)
                for m in range(DH):
                    mine.add(nc.vector.scalar_tensor_tensor(
                        out=drive[:, m, bass.ds(g * SPAN, SPAN)], in0=drive[:, m, bass.ds(g * SPAN, SPAN)],
                        scalar=vec_in[:, V_BR + m:V_BR + m + 1], in1=gain[:, m, bass.ds(g * SPAN, SPAN)],
                        op0=ALU.subtract, op1=ALU.mult))

            def body(g, u, is_first, is_last, ends):
                if not is_last:
                    second_half(g + 1, 1 - u)
                if not ends:
                    normalised(g + 2, u)
                if not is_first:
                    gain_and_drive(Steps(drive_own, g * 4 - 4), g - 1)

            for u in range(2):
                normalised(u, u)
            second_half(0, 0)
            over_spans(vec, body)
            gain_and_drive(Steps(drive_own, SPANS * 4 - 4), SPANS - 1)

        @block.scalar
        def _(act):
            act.sem_inc(z_ready, 4)
            act.wait_ge(var_ready, 1)
            nc.scalar.activation(s["root"][:], s["var"][:], ACT.Sqrt).then_inc(root_ready, 1)
            act.wait_ge(const_in, 48)
            nc.scalar.activation(k["keep"][:], vec_in[:, V_DECAY:V_DECAY + DH], ACT.Sigmoid).then_inc(decay_ready, 1)

            def first_half(g, u):
                act.wait_ge(xnT_psum, g + 1)
                nc.scalar.activation(drive[:, 0, bass.ds(g * SPAN, SPAN)], xnT_ps[:, u, 0, :], ACT.Identity).then_inc(xnT_act, 1)

            def body(g, u, is_first, is_last, ends):
                if not is_last:
                    first_half(g + 1, 1 - u)
                for m in range(DH):
                    act.wait_ge(z_psum, 2 * g + m + 1)
                    nc.scalar.activation(gain[:, m, bass.ds(g * SPAN, SPAN)], z_ps[:, u, m, :], ACT.Sigmoid,
                                         bias=vec_in[:, V_BG + m:V_BG + m + 1]).then_inc(z_ready, 1)

            first_half(0, 0)
            over_spans(act, body)

        @block.tensor
        def _(pe):
            def turn(g, u):
                pe.wait_ge(xn_ready, g + 1)
                for m in range(DH):
                    for j in range(4):
                        ins = nc.tensor.transpose(xnT_ps[:, u, m, j * P:(j + 1) * P],
                                                  xn[:, u, j, m * P:(m + 1) * P], k["ident"][:])
                ins.then_inc(xnT_psum, 1)

            def body(g, u, is_first, is_last, ends):
                if not is_last:
                    turn(g + 1, 1 - u)
                pe.wait_ge(xnT_ready, g + 1)
                pe.wait_ge(xnT_act, g + 1)
                pe.wait_ge(z_ready, 2 * g + 2)
                for m in range(DH):
                    for q in range(DH):
                        ins = nc.tensor.matmul(z_ps[:, u, m, :], wg[:, q, m * P:(m + 1) * P],
                                               drive[:, q, bass.ds(g * SPAN, SPAN)], start=(q == 0), stop=(q == DH - 1))
                    ins.then_inc(z_psum, 1)

            pe.wait_ge(const_in, 48)
            turn(0, 0)
            over_spans(pe, body)


def lanes_of(ap, g):
    return ap[:, g, :, :].rearrange("p m (b c) -> p m b c", c=CHUNKS)


def always(eng):
    return nullcontext()


def unless(flag):
    return lambda eng: eng.If(eng.value_load(flag[:], min_val=0, max_val=P) != P)


def sweep(nc, k, name, count, when=always, first=0):
    state, start = k["state"], k["start"]
    hist = k["xy"][:].rearrange("p t d -> p (t d)").rearrange("p (m c s) -> p m c s", m=DH, s=STEPS)
    drive = k["drive"][:].rearrange("p m (c s) -> p m c s", s=STEPS)
    gain = k["gain"][:].rearrange("p m (c s) -> p m c s", s=STEPS)
    at_step = lambda a, g, t: a[:, :, g * GL:(g + 1) * GL, bass.ds(t + first, 1)].rearrange("p m c o -> p m (c o)")
    S = STEPS - first
    with ExitStack() as ctx:
        sem = lambda n: ctx.enter_context(nc.semaphore(f"{name}_{n}"))
        sb = lambda n, shape, dt=F32: ctx.enter_context(nc.sbuf_tensor(f"{name}_{n}", shape, dt))
        ps = lambda n, shape, dt=F32: ctx.enter_context(nc.psum_tensor(f"{name}_{n}", shape, dt))
        kept = sb("kept", [P, 2, DH, GL])
        free = sb("free", [P, 2, DH, GL])
        bent = sb("bent", [P, 2, DH, GL])
        pred = ps("pred", [P, 2, 512])
        own = sem("own")
        state_ready = [sem(f"state_ready{g}") for g in range(2)]
        kept_ready = [sem(f"kept_ready{g}") for g in range(2)]
        free_ready = [sem(f"free_ready{g}") for g in range(2)]
        pred_ready = [sem(f"pred_ready{g}") for g in range(2)]
        stored = [sem(f"stored{g}") for g in range(2)]
        block = ctx.enter_context(nc.Block())
        TURN = 2

        @block.vector
        def _(vec):
            with when(vec), vec.Fori(0, count) as n:
                mine = Steps(own, n * (4 + TURN * S))
                for g in range(2):
                    for m in range(DH):
                        mine.add(nc.vector.tensor_copy(lanes_of(start, g)[:, m, :, 1:CHUNKS],
                                                       lanes_of(state, g)[:, m, :, 0:CHUNKS - 1]))
                mine.wait(vec)
                for g in range(2):
                    nc.vector.tensor_copy(state[:, g, :, :], start[:, g, :, :]).then_inc(state_ready[g], 1)
                with vec.Fori(0, S) as t:
                    turn = Steps(own, n * (4 + TURN * S) + 4 + t * TURN)
                    for g in range(2):
                        vec.wait_ge(pred_ready[g], n * S + t + 1)
                        turn.add(nc.vector.tensor_tensor(bent[:, g, :, :], pred[:, g, 0:DH * GL].rearrange("p (m c) -> p m c", m=DH),
                                                         at_step(gain, g, t), ALU.mult))
                        turn.wait(vec)
                        vec.wait_ge(free_ready[g], n * S + t + 1)
                        vec.wait_ge(stored[g], n * S + t + 1)
                        nc.vector.tensor_tensor(state[:, g, :, :], free[:, g, :, :], bent[:, g, :, :],
                                                ALU.subtract).then_inc(state_ready[g], 1)
                for g in range(2):
                    vec.wait_ge(state_ready[g], (n + 1) * (S + 1))
                    vec.wait_ge(stored[g], (n + 1) * S + 1)

        @block.tensor
        def _(pe):
            with when(pe), pe.Fori(0, count) as n:
                with pe.Fori(0, S) as t:
                    for g in range(2):
                        pe.wait_ge(state_ready[g], n * (S + 1) + t + 1)
                        for m in range(DH):
                            for q in range(DH):
                                ins = nc.tensor.matmul(pred[:, g, m * GL:(m + 1) * GL], k["wr"][:, q, m * P:(m + 1) * P],
                                                       state[:, g, q, :], start=(q == 0), stop=(q == DH - 1))
                        ins.then_inc(pred_ready[g], 1)

        @block.scalar
        def _(act):
            def keep_state(g):
                for m in range(DH):
                    nc.scalar.activation(kept[:, g, m, :], state[:, g, m, :], ACT.Copy,
                                         scale=k["keep"][:, m:m + 1]).then_inc(kept_ready[g], 1)

            for g in range(2):
                act.sem_inc(stored[g], 1)
            with when(act), act.Fori(0, count) as n:
                for g in range(2):
                    act.wait_ge(state_ready[g], n * (S + 1) + 1)
                    keep_state(g)
                with act.Fori(0, S) as t:
                    for g in range(2):
                        act.wait_ge(state_ready[g], n * (S + 1) + t + 2)
                        keep_state(g)
                        nc.scalar.copy(at_step(hist, g, t), state[:, g, :, :]).then_inc(stored[g], 1)

        @block.gpsimd
        def _(pool):
            with when(pool), pool.Fori(0, count) as n:
                with pool.Fori(0, S) as t:
                    for g in range(2):
                        for m in range(DH):
                            pool.wait_ge(kept_ready[g], (n * (S + 1) + t) * DH + m + 1)
                            ins = nc.gpsimd.tensor_tensor(free[:, g, m, :], kept[:, g, m, :], at_step(drive, g, t)[:, m, :], ALU.add)
                        ins.then_inc(free_ready[g], 1)


def prepare_sweeps(nc, k):
    with ExitStack() as ctx:
        wr_in = ctx.enter_context(nc.semaphore("wr_in"))
        block = ctx.enter_context(nc.Block())

        @block.sync
        def _(sp):
            sp.dma_start(k["wr"][:], k["in_wr"].rearrange("(k p) e -> p k e", p=P)).then_inc(wr_in, 16)
            sp.wait_ge(wr_in, 16)

        @block.vector
        def _(vec):
            nc.vector.memset(k["state"][:], 0.0)
            nc.vector.memset(k["start"][:], 0.0)
            nc.vector.memset(k["ones"][:], 1.0)


def look_at_defect(nc, k):
    with ExitStack() as ctx:
        sem = lambda n: ctx.enter_context(nc.semaphore(f"defect_{n}"))
        sb = lambda n, shape, dt=F32: ctx.enter_context(nc.sbuf_tensor(f"defect_{n}", shape, dt))
        size, gap, wide = sb("size", [P, 2, DH, GL]), sb("gap", [P, 2, DH, GL]), sb("wide", [P, 2, DH, GL])
        most, bound, close, all_close = sb("most", [P, DH]), sb("bound", [P, DH]), sb("close", [P, 2, DH, GL]), sb("all_close", [P, 1])
        total = ctx.enter_context(nc.psum_tensor("defect_total", [P, 1], F32))
        own, flags_ready, total_ready = sem("own"), sem("flags_ready"), sem("total_ready")
        block = ctx.enter_context(nc.Block())

        @block.vector
        def _(vec):
            mine = Steps(own)
            flat = lambda ap: ap[:].rearrange("p g m c -> p (g m c)")
            mine.add(nc.vector.scalar_tensor_tensor(out=flat(size), in0=flat(k["state"]), scalar=-1.0, in1=flat(k["state"]),
                                                    op0=ALU.mult, op1=ALU.max))
            mine.add(nc.vector.memset(gap[:], 0.0))
            mine.wait(vec)
            for g in range(2):
                for m in range(DH):
                    mine.add(nc.vector.tensor_tensor(lanes_of(gap, g)[:, m, :, 1:CHUNKS],
                                                     lanes_of(k["state"], g)[:, m, :, 0:CHUNKS - 1],
                                                     lanes_of(k["start"], g)[:, m, :, 1:CHUNKS], ALU.subtract))
            mine.add(nc.vector.tensor_reduce(most[:], size[:].rearrange("p g m c -> p m g c"), AX.XY, ALU.max))
            mine.wait(vec)
            mine.add(nc.vector.tensor_scalar(bound[:], most[:], TOLERANCE, None, ALU.mult))
            mine.add(nc.vector.scalar_tensor_tensor(out=flat(wide), in0=flat(gap), scalar=-1.0, in1=flat(gap),
                                                    op0=ALU.mult, op1=ALU.max))
            mine.wait(vec)
            for m in range(DH):
                mine.add(nc.vector.tensor_scalar(close[:, :, m, :], wide[:, :, m, :], bound[:, m:m + 1], None, ALU.is_le))
            mine.wait(vec)
            nc.vector.tensor_reduce(all_close[:], close[:], AX.XYZ, ALU.min).then_inc(flags_ready, 1)
            vec.wait_ge(total_ready, 1)
            nc.vector.tensor_copy(k["agree"][:], total[0:1, :])

        @block.tensor
        def _(pe):
            pe.wait_ge(flags_ready, 1)
            nc.tensor.matmul(total[:], k["ones"][:], all_close[:], start=True, stop=True).then_inc(total_ready, 1)


def project_states(nc, k):
    hist = k["xy"][:].rearrange("p t d -> p (t d)").rearrange("p (m t) -> p m t", m=DH)
    vec_in = k["vec"]
    SLOTS = 4
    with ExitStack() as ctx:
        sem = lambda n: ctx.enter_context(nc.semaphore(f"proj_{n}"))
        sb = lambda n, shape, dt=F32: ctx.enter_context(nc.sbuf_tensor(f"proj_{n}", shape, dt))
        ps = lambda n, shape, dt=F32: ctx.enter_context(nc.psum_tensor(f"proj_{n}", shape, dt))
        wo, bo = sb("wo", [P, DH, D]), sb("bo", [P, D])
        scaled, centred = sb("scaled", [P, DH, D]), sb("centred", [P, DH, D])
        shares = sb("shares", [P, P])
        shifts = sb("shifts", [P, DH, P])
        added = sb("added", [P, D])
        hs = sb("hs", [P, 2, DH, SPAN])
        x1 = sb("x1", [P, SLOTS, 4, D])
        sums, sums1 = sb("sums", [P, TILES, 6]), sb("sums1", [P, TILES, 6])
        s = {n: sb(f"st_{n}", [P, TILES]) for n in ("a", "b", "c", "d", "e", "mean", "var", "root", "rstd")}
        s1 = {n: sb(f"st1_{n}", [P, TILES]) for n in ("a", "b", "c", "d", "e", "var", "root")}
        s1["mean"], s1["rstd"] = k["mean1"], k["rstd1"]
        h_ps = ps("h_ps", [P, 2, 4, D])
        o_ps = ps("o_ps", [P, 2, 4, D])
        const_in, own, scaled_ready, sums_psum, added_ready = (
            sem(n) for n in ("const_in", "own", "scaled_ready", "sums_psum", "added_ready"))
        hs_ready, h_psum, h_taken, o_psum, x1_ready, xb_ready, var_ready, root_ready = (
            sem(n) for n in ("hs_ready", "h_psum", "h_taken", "o_psum", "x1_ready", "xb_ready", "var_ready", "root_ready"))
        x_in = [sem(f"x_in{u}") for u in range(SLOTS)]
        x1_out = [sem(f"x1_out{u}") for u in range(SLOTS)]
        block = ctx.enter_context(nc.Block())
        xv = k["in_x"].rearrange("(g j p) d -> p g j d", p=P, j=4)
        x1v = k["x1"].rearrange("(g j p) d -> p g j d", p=P, j=4)
        one = lambda v, g: v[:, bass.ds(g, 1), :, :].rearrange("p g j d -> p (g j) d")

        @block.sync
        def _(sp):
            sp.dma_start(wo[:], k["in_wo"].rearrange("(k p) e -> p k e", p=P)).then_inc(const_in, 16)
            sp.dma_start(bo[:], k["in_bo"]).then_inc(const_in, 16)
            for u in range(SLOTS):
                sp.dma_start(x1[:, u, :, :], xv[:, u, :, :]).then_inc(x_in[u], 16)
            with sp.Fori(0, SPANS // SLOTS - 1) as i:
                for u in range(SLOTS):
                    sp.wait_ge(x1_ready, i * SLOTS + u + 3)
                    sp.dma_start(one(x1v, i * SLOTS + u), x1[:, u, :, :]).then_inc(x1_out[u], 16)
                    if u:
                        sp.wait_ge(x1_out[u - 1], i * 16 + 16)
                        sp.dma_start(x1[:, u - 1, :, :], one(xv, i * SLOTS + SLOTS + u - 1)).then_inc(x_in[u - 1], 16)
                sp.wait_ge(x1_out[SLOTS - 1], i * 16 + 16)
                sp.dma_start(x1[:, SLOTS - 1, :, :], one(xv, i * SLOTS + 2 * SLOTS - 1)).then_inc(x_in[SLOTS - 1], 16)
            for u in range(SLOTS):
                sp.wait_ge(x1_ready, SPANS - SLOTS + u + 3)
                sp.dma_start(x1v[:, SPANS - SLOTS + u, :, :], x1[:, u, :, :]).then_inc(x1_out[u], 16)
            for u in range(SLOTS):
                sp.wait_ge(x1_out[u], 16 * SPANS // SLOTS)

        @block.gpsimd
        def _(pool):
            pool.wait_ge(added_ready, 1)
            with pool.Fori(0, SPANS // SLOTS) as i:
                for u in range(SLOTS):
                    pool.wait_ge(x_in[u], i * 16 + 16)
                    nc.gpsimd.tensor_tensor(x1[:, u, :, :], x1[:, u, :, :], added[:].unsqueeze(1).to_broadcast([P, 4, D]),
                                            ALU.add).then_inc(xb_ready, 1)

        @block.scalar
        def _(act):
            with act.Fori(0, SPANS // 2) as i:
                for u in range(2):
                    act.wait_ge(h_psum, i * 2 + u + 1)
                    nc.scalar.activation(hs[:, u, :, :], hist[:, :, bass.ds((i * 2 + u) * SPAN, SPAN)], ACT.Identity).then_inc(hs_ready, 1)
            act.wait_ge(h_psum, SPANS + 2)
            act.wait_ge(var_ready, 1)
            nc.scalar.activation(s["root"][:], s["var"][:], ACT.Sqrt).then_inc(root_ready, 1)
            with act.Fori(0, SPANS // 2) as i:
                for u in range(2):
                    act.wait_ge(o_psum, i * 2 + u + 1)
                    nc.scalar.activation(hs[:, u, :, :], hist[:, :, bass.ds((i * 2 + u) * SPAN, SPAN)], ACT.Identity).then_inc(hs_ready, 1)
            act.wait_ge(var_ready, 2)
            nc.scalar.activation(s1["root"][:], s1["var"][:], ACT.Sqrt).then_inc(root_ready, 1)

        @block.tensor
        def _(pe):
            pe.sem_inc(h_psum, 2)
            pe.sem_inc(o_psum, 2)
            with pe.Fori(0, SPANS // 2) as i:
                for u in range(2):
                    pe.wait_ge(hs_ready, i * 2 + u + 1)
                    pe.wait_ge(h_taken, i * 2 + u + 1)
                    for j in range(4):
                        for m in range(DH):
                            ins = nc.tensor.transpose(h_ps[:, u, j, m * P:(m + 1) * P], hs[:, u, m, j * P:(j + 1) * P], k["ident"][:])
                    ins.then_inc(h_psum, 1)
            pe.wait_ge(scaled_ready, 1)
            for q in range(DH):
                nc.tensor.matmul(o_ps[:, 0, 0, :], shares[:], scaled[:, q, :], start=(q == 0), stop=(q == DH - 1))
            for q in range(DH):
                ins = nc.tensor.matmul(o_ps[:, 1, 0, :], shifts[:, q, :], wo[:, q, :], start=(q == 0), stop=(q == DH - 1))
            ins.then_inc(sums_psum, 1)
            pe.wait_ge(added_ready, 1)
            with pe.Fori(0, SPANS // 2) as i:
                for u in range(2):
                    pe.wait_ge(hs_ready, i * 2 + u + SPANS + 1)
                    pe.wait_ge(x1_ready, i * 2 + u + 1)
                    for j in range(4):
                        for q in range(DH):
                            ins = nc.tensor.matmul(o_ps[:, u, j, :], hs[:, u, q, j * P:(j + 1) * P], centred[:, q, :],
                                                   start=(q == 0), stop=(q == DH - 1))
                    ins.then_inc(o_psum, 1)

        @block.vector
        def _(vec):
            vec.sem_inc(h_taken, 2)
            vec.sem_inc(x1_ready, 2)
            mine = Steps(own)
            mine.add(nc.vector.memset(shares[:], 1.0 / D))
            mine.wait(vec)
            vec.wait_ge(const_in, 32)
            for q in range(DH):
                nc.vector.tensor_scalar(scaled[:, q, :], wo[:, q, :], vec_in[:, V_LNW + q:V_LNW + q + 1], None, ALU.mult)
                ins = nc.vector.tensor_scalar(shifts[:, q, :], shares[:], vec_in[:, V_LNB + q:V_LNB + q + 1], float(D), ALU.mult, ALU.mult)
            ins.then_inc(scaled_ready, 1)
            with vec.Fori(0, SPANS // 2) as i:
                for u in range(2):
                    vec.wait_ge(h_psum, i * 2 + u + 3)
                    for j in range(4):
                        ins = nc.vector.bn_stats(sums[:, bass.ds((i * 2 + u) * 4 + j, 1), :].rearrange("p o c -> p (o c)"), h_ps[:, u, j, :])
                    ins.then_inc(h_taken, 1)
            vec.wait_ge(h_taken, SPANS + 2)
            statistics(nc, vec, mine, s, sums, lambda ins: ins.then_inc(var_ready, 1), TILES)
            vec.wait_ge(sums_psum, 1)
            for q in range(DH):
                nc.vector.tensor_tensor(centred[:, q, :], scaled[:, q, :], o_ps[:, 0, 0, :], ALU.subtract)
            nc.vector.tensor_tensor(added[:], o_ps[:, 1, 0, :], bo[:], ALU.add).then_inc(added_ready, 1)
            vec.wait_ge(root_ready, 1)
            inverse_root(nc, vec, mine, s, TILES)
            mine.wait(vec)
            before = mine.n
            with vec.Fori(0, SPANS // SLOTS) as i:
                for u in range(SLOTS):
                    g = i * SLOTS + u
                    turn = Steps(own, g * 4 + before)
                    vec.wait_ge(o_psum, g + 3)
                    vec.wait_ge(xb_ready, g + 1)
                    for j in range(4):
                        turn.add(nc.vector.scalar_tensor_tensor(out=x1[:, u, j, :], in0=o_ps[:, u % 2, j, :],
                                                                scalar=s["rstd"][:, bass.ds(g * 4 + j, 1)], in1=x1[:, u, j, :],
                                                                op0=ALU.mult, op1=ALU.add))
                    turn.wait(vec)
                    for j in range(4):
                        ins = nc.vector.bn_stats(sums1[:, bass.ds(g * 4 + j, 1), :].rearrange("p o c -> p (o c)"), x1[:, u, j, :])
                    ins.then_inc(x1_ready, 1)
            vec.wait_ge(x1_ready, SPANS + 2)
            mine = Steps(own, before + SPANS * 4)
            statistics(nc, vec, mine, s1, sums1, lambda ins: ins.then_inc(var_ready, 1), TILES)
            vec.wait_ge(root_ready, 2)
            inverse_root(nc, vec, mine, s1, TILES)


def run_block(nc, sems, build_block):
    with nc.Block() as block:
        build_block(block)
    for s in sems:
        nc.gpsimd.sem_clear(s)
    nc.all_engine_barrier()


SAFE = 160.0

Q_PARTS = (0, 0, 1, 0, 2, 1)
K_PARTS = (3, 4, 3, 5, 3, 4)
ROWS = 6 * 16
GH = 4


def load_stacks(nc, k, eng, s, m, arrived):
    for which, plan in (("qst", Q_PARTS), ("kst", K_PARTS)):
        for i, part in enumerate(plan):
            for h in range(GH):
                at = 64 * s + HD * h
                eng.dma_start(k[which][HD * i:HD * i + HD, s, h, :],
                              k["parts"][at:at + HD, part, bass.ds(m, 1), :].rearrange("p o t -> p (o t)")).then_inc(arrived, 16)
    return 2 * 6 * GH * 16


def shift_by_bound(nc, k, s, m):
    return nc.gpsimd.tensor_tensor(k["qst"][ROWS:ROWS + 3, s, :, :], k["kst"][ROWS:ROWS + 3, s, :, :],
                                   k["shift"][ROWS:ROWS + 3, bass.ds(m * 8 + s * GH, GH)].unsqueeze(2).to_broadcast([3, GH, L]),
                                   ALU.mult)


def project_queries_and_keys(nc, k, b):
    acc, parts, xnT, vec_in = k["acc"], k["parts"], k["xnT"], k["vec"]
    NT, G = L // P, L // SPAN
    with ExitStack() as ctx:
        names = []

        def sem(n):
            names.append(ctx.enter_context(nc.semaphore(f"qk_{n}")))
            return names[-1]

        sb = lambda n, shape, dt=F32: ctx.enter_context(nc.sbuf_tensor(f"qk_{n}", shape, dt))
        ps = lambda n, shape, dt=F32: ctx.enter_context(nc.psum_tensor(f"qk_{n}", shape, dt))
        wqk = sb("wqk", [P, DH, 2 * D])
        free = k["qst"][:].rearrange("p s h t -> p (s h t)").bitcast(F32).rearrange("p (n t) -> p n t", t=SPAN)
        whole = free[:, 0:4, :]
        size = free[:, 4:8, :]
        rest = free[:, 8:12, :]
        xn = free[:, 14:16, :].rearrange("p n (j d) -> p (n j) d", d=D)
        peaks = sb("peaks", [P, G, 4])
        wide, both, by_head = sb("wide", [P, 4]), sb("both", [P, DH]), sb("by_head", [P, HEADS])
        safe, all_safe = sb("safe", [P, HEADS]), sb("all_safe", [P, 1])
        xT_ps = ps("xT_ps", [P, 2, DH, SPAN])
        q_ps = ps("q_ps", [P, 4, SPAN])
        w_in, x_first, x_rest, own = sem("w_in"), sem("x_first"), sem("x_rest"), sem("own")
        xn_ready, xT_psum, low_ready, high_ready = sem("xn_ready"), sem("xT_psum"), sem("low_ready"), sem("high_ready")
        q_psum, whole_ready, size_ready, rest_ready, second_ready, third_ready = (
            sem(n) for n in ("q_psum", "whole_ready", "size_ready", "rest_ready", "second_ready", "third_ready"))
        peaks_ready = sem("peaks_ready")
        by_head_ready, bound_psum, safe_ready, safe_psum = (sem(n) for n in ("by_head_ready", "bound_psum", "safe_ready", "safe_psum"))

        def blocks(block):
            x1v = k["x1"].rearrange("(b j p) d -> p b j d", p=P, j=NT)

            @block.sync
            def _(sp):
                for arrived, lo, hi in ((x_first, 0, 4), (x_rest, 4, NT)):
                    sp.dma_start(acc[:, lo:hi, :], x1v[:, bass.ds(b, 1), lo:hi, :].rearrange("p b j d -> p (b j) d")).then_inc(arrived, 16)
                sp.dma_start(wqk[:], k["in_wqkv"].rearrange("(k p) e -> p k e", p=P)[:, :, 0:2 * D]).then_inc(w_in, 16)

            @block.scalar
            def _(act):
                def low_half(g):
                    act.wait_ge(xT_psum, g + 1)
                    nc.scalar.copy(xnT[:, 0, g * SPAN:(g + 1) * SPAN], xT_ps[:, g % 2, 0, :]).then_inc(low_ready, 1)

                low_half(0)
                for g in range(G):
                    at = slice(g * SPAN, (g + 1) * SPAN)
                    for o in range(4):
                        n = 4 * g + o
                        v = V_BQ + o if o < 2 else V_BK + o - 2
                        act.wait_ge(q_psum, n + 1)
                        if g:
                            act.wait_ge(rest_ready, n - 3)
                            act.wait_ge(peaks_ready, g)
                        nc.scalar.activation(whole[:, o, :], q_ps[:, o, :], ACT.Identity, bias=vec_in[:, v:v + 1])
                        nc.scalar.activation(parts[:, 3 * (o // 2), o % 2, at], q_ps[:, o, :],
                                             ACT.Identity, bias=vec_in[:, v:v + 1]).then_inc(whole_ready, 1)
                        nc.scalar.activation(size[:, o, :], q_ps[:, o, :], ACT.Abs, bias=vec_in[:, v:v + 1]).then_inc(size_ready, 1)
                        if o == 1 and g + 1 < G:
                            low_half(g + 1)

            @block.gpsimd
            def _(pool):
                for n in range(4 * G):
                    g, o = n // 4, n % 4
                    at, first = slice(g * SPAN, (g + 1) * SPAN), 3 * (o // 2)
                    pool.wait_ge(second_ready, n + 1)
                    nc.gpsimd.tensor_tensor(parts[:, first + 2, o % 2, at], rest[:, o, :],
                                            parts[:, first + 1, o % 2, at], ALU.subtract).then_inc(third_ready, 1)

            @block.tensor
            def _(pe):
                def turn(g):
                    pe.wait_ge(xn_ready, g + 1)
                    if g >= 2:
                        pe.wait_ge(low_ready, g - 1)
                        pe.wait_ge(high_ready, g - 1)
                    for m in range(DH):
                        for j in range(4):
                            ins = nc.tensor.transpose(xT_ps[:, g % 2, m, j * P:(j + 1) * P], xn[:, j, m * P:(m + 1) * P], k["ident"][:])
                    ins.then_inc(xT_psum, 1)

                turn(0)
                pe.wait_ge(w_in, 16)
                for g in range(G):
                    pe.wait_ge(low_ready, g + 1)
                    pe.wait_ge(high_ready, g + 1)
                    for o in range(4):
                        if o == 1 and g + 1 < G:
                            turn(g + 1)
                        if g:
                            pe.wait_ge(size_ready, 4 * g + o - 3)
                        for q in range(DH):
                            ins = nc.tensor.matmul(q_ps[:, o, :], wqk[:, q, o * P:(o + 1) * P], xnT[:, q, g * SPAN:(g + 1) * SPAN],
                                                   start=(q == 0), stop=(q == DH - 1))
                        ins.then_inc(q_psum, 1)
                pe.wait_ge(by_head_ready, 1)
                nc.tensor.matmul(q_ps[:, 0, 0:HEADS], k["all_ones"][:], by_head[:], start=True, stop=True).then_inc(bound_psum, 1)
                pe.wait_ge(safe_ready, 1)
                nc.tensor.matmul(q_ps[0:1, 1, 0:1], k["all_ones"][:, 0:1], all_safe[:], start=True, stop=True).then_inc(safe_psum, 1)

            @block.vector
            def _(vec):
                mine = Steps(own)

                def normalise(g):
                    if g:
                        vec.wait_ge(xT_psum, g)
                    for j in range(4):
                        t = b * NT + (g * 4 + j)
                        ins = nc.vector.tensor_scalar(xn[:, j, :], acc[:, g * 4 + j, :], k["mean1"][:, bass.ds(t, 1)],
                                                      k["rstd1"][:, bass.ds(t, 1)], ALU.subtract, ALU.mult)
                    ins.then_inc(xn_ready, 1)

                def high_half(g):
                    vec.wait_ge(xT_psum, g + 1)
                    nc.vector.tensor_copy(xnT[:, 1, g * SPAN:(g + 1) * SPAN], xT_ps[:, g % 2, 1, :]).then_inc(high_ready, 1)
                    if g + 1 < G:
                        normalise(g + 1)

                vec.wait_ge(x_first, 16)
                normalise(0)
                vec.wait_ge(x_rest, 16)
                high_half(0)
                for g in range(G):
                    at = slice(g * SPAN, (g + 1) * SPAN)
                    for o in range(4):
                        n, first = 4 * g + o, 3 * (o // 2)
                        vec.wait_ge(whole_ready, n + 1)
                        if g:
                            vec.wait_ge(third_ready, n - 3)
                        nc.vector.tensor_tensor(rest[:, o, :], whole[:, o, :], parts[:, first, o % 2, at],
                                                ALU.subtract).then_inc(rest_ready, 1)
                        vec.wait_ge(rest_ready, n + 1)
                        nc.vector.tensor_copy(parts[:, first + 1, o % 2, at], rest[:, o, :]).then_inc(second_ready, 1)
                        if o == 1 and g + 1 < G:
                            high_half(g + 1)
                    vec.wait_ge(size_ready, 4 * g + 4)
                    nc.vector.tensor_reduce(peaks[:, g, :], size, AX.X, ALU.max).then_inc(peaks_ready, 1)
                vec.wait_ge(peaks_ready, G)
                mine.add(nc.vector.tensor_reduce(wide[:], peaks[:].rearrange("p g o -> p o g"), AX.X, ALU.max))
                mine.wait(vec)
                mine.add(nc.vector.tensor_tensor(both[:], wide[:, 0:2], wide[:, 2:4], ALU.mult))
                mine.wait(vec)
                for m in range(DH):
                    ins = nc.vector.tensor_scalar(by_head[:, 8 * m:8 * m + 8], k["member"][:, 0:8], both[:, m:m + 1], None, ALU.mult)
                ins.then_inc(by_head_ready, 1)
                vec.wait_ge(bound_psum, 1)
                mine.add(nc.vector.tensor_scalar(k["shift"][:], q_ps[:, 0, 0:HEADS], k["member"][:, 8:9], None, ALU.mult))
                mine.add(nc.vector.tensor_scalar(safe[:], q_ps[:, 0, 0:HEADS], SAFE, None, ALU.is_le))
                mine.wait(vec)
                nc.vector.tensor_reduce(all_safe[:], safe[:], AX.X, ALU.min).then_inc(safe_ready, 1)
                vec.wait_ge(safe_psum, 1)
                nc.vector.tensor_copy(k["ranged"][:], q_ps[0:1, 1, 0:1])

        run_block(nc, names, blocks)


def route_and_project_values(nc, k):
    acc, values, xnT, share = k["acc"], k["values"], k["xnT"], k["share"]
    NT, G = L // P, L // SPAN
    with ExitStack() as ctx:
        names = []

        def sem(n):
            names.append(ctx.enter_context(nc.semaphore(f"v_{n}")))
            return names[-1]

        sb = lambda n, shape, dt=F32: ctx.enter_context(nc.sbuf_tensor(f"v_{n}", shape, dt))
        ps = lambda n, shape, dt=F32: ctx.enter_context(nc.psum_tensor(f"v_{n}", shape, dt))
        wv, bv, bexp = sb("wv", [P, DH, D]), sb("bv", [P, D]), sb("bexp", [P, D])
        top, tot, inv = sb("top", [P, NT]), sb("tot", [P, NT]), sb("inv", [P, NT])
        lg, ex, pr, rank = (sb(n, [P, NT, E]) for n in ("lg", "ex", "pr", "rank"))
        more, same = sb("more", [P, NT, E, E]), sb("same", [P, NT, E, E])
        shareT = sb("shareT", [P, NT, 32])
        l_ps, v_ps, b_ps = ps("l_ps", [P, NT, E]), ps("v_ps", [P, 2, 2, D]), ps("b_ps", [P, 2, 4, D])
        w_in, arrived, own = sem("w_in"), sem("arrived"), sem("own")
        l_psum, lg_ready, ex_ready, shareT_ready = sem("l_psum"), sem("lg_ready"), sem("ex_ready"), sem("shareT_ready")
        v_psum, v_taken, b_psum, b_taken = sem("v_psum"), sem("v_taken"), sem("b_psum"), sem("b_taken")

        def blocks(block):
            @block.sync
            def _(sp):
                sp.dma_start(wv[:], k["in_wqkv"].rearrange("(k p) e -> p k e", p=P)[:, :, 2 * D:3 * D]).then_inc(w_in, 16)
                sp.dma_start(bv[:], k["in_bv"]).then_inc(w_in, 16)
                sp.dma_start(bexp[:], k["in_bexp"]).then_inc(w_in, 16)
                sp.wait_ge(arrived, load_stacks(nc, k, sp, 0, 0, arrived))

            @block.gpsimd
            def _(pool):
                shift_by_bound(nc, k, 0, 0)

            @block.scalar
            def _(act):
                act.wait_ge(lg_ready, 1)
                nc.scalar.activation(ex[:], lg[:], ACT.Exp).then_inc(ex_ready, 1)

            @block.tensor
            def _(pe):
                for t in range(NT):
                    at = slice(t * P, (t + 1) * P)
                    for q in range(DH):
                        nc.tensor.matmul(l_ps[:, t, :], xnT[:, q, at], k["wgate"][:, q, :], start=(q == 0), stop=False)
                    ins = nc.tensor.matmul(l_ps[:, t, :], k["row"][0:1, 0:P], k["row"][0:1, P:P + E], start=False, stop=True)
                ins.then_inc(l_psum, 1)
                pe.wait_ge(w_in, 48)
                for n in range(NT // 2):
                    if n >= 2:
                        pe.wait_ge(v_taken, n - 1)
                    for j in range(2):
                        t = 2 * n + j
                        for q in range(DH):
                            ins = nc.tensor.matmul(v_ps[:, n % 2, j, :], xnT[:, q, t * P:(t + 1) * P], wv[:, q, :],
                                                   start=(q == 0), stop=(q == DH - 1))
                    ins.then_inc(v_psum, 1)
                pe.wait_ge(shareT_ready, 1)
                for g in range(G):
                    if g >= 2:
                        pe.wait_ge(b_taken, g - 1)
                    for j in range(4):
                        for r in range(4):
                            at = slice(32 * r, 32 * r + 32)
                            ins = nc.tensor.matmul(b_ps[at, g % 2, j, :], shareT[at, 4 * g + j, :], bexp[at, :], start=True, stop=True)
                    ins.then_inc(b_psum, 1)

            @block.vector
            def _(vec):
                mine = Steps(own)

                def take_values(n):
                    vec.wait_ge(v_psum, n + 1)
                    nc.vector.tensor_tensor(values[:, 2 * n:2 * n + 2, :, 0:HD],
                                            v_ps[:, n % 2, :, :].rearrange("p j (h d) -> p j h d", d=HD),
                                            bv[:].rearrange("p (h d) -> p h d", d=HD).unsqueeze(1).to_broadcast([P, 2, HEADS, HD]),
                                            ALU.add).then_inc(v_taken, 1)

                def then(ins):
                    mine.add(ins)
                    mine.wait(vec)

                spread = lambda a: a[:].unsqueeze(2).to_broadcast([P, NT, E])
                vec.wait_ge(l_psum, 1)
                then(nc.vector.tensor_reduce(top[:], l_ps[:], AX.X, ALU.max))
                nc.vector.tensor_tensor(lg[:], l_ps[:], spread(top), ALU.subtract).then_inc(lg_ready, 1)
                vec.wait_ge(w_in, 48)
                take_values(0)
                take_values(1)
                vec.wait_ge(ex_ready, 1)
                then(nc.vector.tensor_reduce(tot[:], ex[:], AX.X, ALU.add))
                then(nc.vector.reciprocal(inv[:], tot[:]))
                then(nc.vector.tensor_tensor(pr[:], ex[:], spread(inv), ALU.mult))
                take_values(2)
                take_values(3)
                full = [P, NT, E, E]
                each, other = pr[:].unsqueeze(3).to_broadcast(full), pr[:].unsqueeze(2).to_broadcast(full)
                mine.add(nc.vector.tensor_tensor(more[:], other, each, ALU.is_gt))
                then(nc.vector.tensor_tensor(same[:], other, each, ALU.is_equal))
                then(nc.vector.tensor_tensor(same[:], same[:], k["lower"][:].unsqueeze(1).to_broadcast(full), ALU.mult))
                take_values(4)
                take_values(5)
                then(nc.vector.tensor_tensor(more[:], more[:], same[:], ALU.add))
                then(nc.vector.tensor_reduce(rank[:], more[:], AX.X, ALU.add))
                then(nc.vector.scalar_tensor_tensor(out=share[:, :, 0:E], in0=rank[:], scalar=TOP_K - 0.5, in1=pr[:],
                                                    op0=ALU.is_lt, op1=ALU.mult))
                nc.vector.transpose(shareT[:].rearrange("p t c -> p (t c)"), share[:].rearrange("p t c -> p (t c)")).then_inc(shareT_ready, 1)
                take_values(6)
                take_values(7)
                for g in range(G):
                    vec.wait_ge(b_psum, g + 1)
                    nc.vector.tensor_tensor(acc[:, 4 * g:4 * g + 4, :], b_ps[:, g % 2, :, :], acc[:, 4 * g:4 * g + 4, :],
                                            ALU.add).then_inc(b_taken, 1)

        run_block(nc, names, blocks)


class Maxima:
    QT = L // P

    def __init__(self, nc, k, s, sem, s_ps, n_ps, room):
        self.nc, self.k, self.s, self.s_ps, self.n_ps = nc, k, s, s_ps, n_ps
        n = GH * self.QT
        self.big, self.neg = room[:, 0:n], room[:, n:2 * n]
        self.rows, self.left = room[0:n, SPAN:SPAN + P], room[0:n, SPAN + P:SPAN + 2 * P]
        self.three = room[0:n, 2 * SPAN:2 * SPAN + 3 * P // 2].bitcast(BF16).rearrange("n (i t) -> n i t", i=3)
        self.m_psum, self.m_taken, self.neg_ready, self.n_psum, self.m_own, self.three_ready, self.moved = (
            sem(x) for x in ("m_psum", "m_taken", "neg_ready", "n_psum", "m_own", "three_ready", "moved"))

    def tensor(self, pe):
        nc, k, s = self.nc, self.k, self.s
        flat = lambda a: a[0:ROWS, s, :, :].rearrange("r h t -> r (h t)")
        pe.sem_inc(self.m_taken, 1)
        with pe.Fori(0, GH * self.QT) as n:
            pe.wait_ge(self.m_taken, n + 1)
            for c in range(4):
                ins = nc.tensor.matmul(self.s_ps[:, c // 2, c % 2, :], flat(k["qst"])[:, bass.ds(n * P, P)],
                                       flat(k["kst"])[:, bass.ds((n // self.QT) * L + c * SPAN, SPAN)], start=True, stop=True)
            ins.then_inc(self.m_psum, 1)
        pe.wait_ge(self.neg_ready, 1)
        nc.tensor.transpose(self.n_ps, self.neg, k["ident"][:]).then_inc(self.n_psum, 1)
        pe.wait_ge(self.moved, 48)

    def vector(self, vec):
        nc = self.nc
        with vec.Fori(0, GH * self.QT) as n:
            vec.wait_ge(self.m_psum, n + 1)
            nc.vector.tensor_reduce(self.big[:, bass.ds(n, 1)], self.s_ps[:, 0:2, :, :], AX.XYZ, ALU.max).then_inc(self.m_taken, 1)
        vec.wait_ge(self.m_taken, GH * self.QT + 1)
        nc.vector.tensor_scalar(self.neg, self.big, -1.0, None, ALU.mult).then_inc(self.neg_ready, 1)
        mine = Steps(self.m_own)
        rows, left, three = self.rows, self.left, self.three
        vec.wait_ge(self.n_psum, 1)
        mine.add(nc.vector.tensor_copy(rows, self.n_ps))
        mine.wait(vec)
        mine.add(nc.vector.tensor_copy(three[:, 0, :], rows))
        mine.wait(vec)
        mine.add(nc.vector.tensor_tensor(left, rows, three[:, 0, :], ALU.subtract))
        mine.wait(vec)
        mine.add(nc.vector.tensor_copy(three[:, 1, :], left))
        mine.wait(vec)
        nc.vector.tensor_tensor(three[:, 2, :], left, three[:, 1, :], ALU.subtract).then_inc(self.three_ready, 1)

    def sync(self, sp):
        sp.wait_ge(self.three_ready, 1)
        for i in range(3):
            sp.dma_start(self.k["qst"][ROWS + i:ROWS + i + 1, self.s, :, :].rearrange("o h (t c) -> o (h t) c", c=P),
                         self.three[:, i, :]).then_inc(self.moved, 16)
        sp.wait_ge(self.moved, 48)


PIECES_AFTER = (0, 0, 1, 1, 1, 1, 1, 1, 2, 1, 1, 2, 1, 1, 0, 2)
TURN_AFTER = 1


def attend(nc, k, s, hp):
    qst, kst, acc, share = k["qst"], k["kst"], k["acc"], k["share"]
    KT, UNITS, QS = L // P, 2 * (L // P), L // SPAN
    VC = HD + 1
    when = unless(k["ranged"])
    with ExitStack() as ctx:
        names = []

        def sem(n):
            names.append(ctx.enter_context(nc.semaphore(f"att{s}_{n}")))
            return names[-1]

        sb = lambda n, shape, dt=F32: ctx.enter_context(nc.sbuf_tensor(f"att{s}_{n}", shape, dt))
        ps = lambda n, shape, dt=F32: ctx.enter_context(nc.psum_tensor(f"att{s}_{n}", shape, dt))
        probs = sb("probs", [P, 4, 2, SPAN])
        mixed = sb("mixed", [P, SPAN])
        vg = sb("vg", [P, KT, GH, VC])
        xt = sb("xt", [P, DH, P])
        inv, out = sb("inv", [P, 4 * GH]), sb("out", [P, 4 * GH, HD])
        s_ps = ps("s_ps", [P, 3, 2, SPAN])
        pv_ps, x_ps = ps("pv_ps", [P, SPAN]), ps("x_ps", [P, SPAN])
        s_psum, exp_done, pv_done, mixed_ready, turned, own, vg_ready, xt_ready, e_psum, x_taken, arrived, shifted = (
            sem(n) for n in ("s_psum", "exp_done", "pv_done", "mixed_ready", "turned", "own", "vg_ready", "xt_ready",
                             "e_psum", "x_taken", "arrived", "shifted"))
        maxima = Maxima(nc, k, s, sem, s_ps, x_ps[0:GH * (L // P), 0:P], probs[:].rearrange("p u h t -> p (u h t)"))
        NE = E // 2

        def query_spans(eng, body):
            body(0, True, False)
            with eng.Fori(1, QS - 1) as it:
                body(it, False, False)
            body(QS - 1, False, True)

        def blocks(block):
            @block.sync
            def _(sp):
                with when(sp):
                    maxima.sync(sp)
                sp.wait_ge(arrived, load_stacks(nc, k, sp, 1 - s, hp if s == 0 else 1 - hp, arrived))

            @block.gpsimd
            def _(pool):
                def tile(it):
                    return nc.gpsimd.tensor_copy(xt[:], k["xnT"][:, :, bass.ds((hp * 8 + s * 4 + it) * P, P)]).then_inc(xt_ready, 1)

                tile(0)
                pool.wait_ge(xt_ready, 1)
                shift_by_bound(nc, k, 1 - s, hp if s == 0 else 1 - hp).then_inc(shifted, 1)
                pool.wait_ge(shifted, 1)
                with pool.Fori(1, QS) as it:
                    pool.wait_ge(e_psum, it * NE)
                    tile(it)

            @block.tensor
            def _(pe):
                with when(pe):
                    maxima.tensor(pe)

                def scores(it, u, is_first=False):
                    if u >= 3:
                        pe.wait_ge(exp_done, it * UNITS + u - 2)
                    elif not is_first:
                        pe.wait_ge(exp_done, it * UNITS - UNITS + (31, 32, 30)[u])
                    kt, pair = u // 2, u % 2
                    for h in range(2):
                        ins = nc.tensor.matmul(s_ps[:, u % 3, h, :], kst[0:ROWS + 3, s, 2 * pair + h, kt * P:(kt + 1) * P],
                                               qst[0:ROWS + 3, s, 2 * pair + h, bass.ds(it * SPAN, SPAN)], start=True, stop=True)
                    ins.then_inc(s_psum, 1)

                def scores_ahead(it, u, is_last):
                    if u < UNITS:
                        scores(it, u)
                    elif not is_last:
                        scores(it + 1, u - UNITS)

                def turn_back(it):
                    pe.wait_ge(mixed_ready, it)
                    pe.wait_ge(x_taken, it * (NE + 1) - 1)
                    for c in range(4):
                        ins = nc.tensor.transpose(x_ps[:, c * P:(c + 1) * P], mixed[:, c * P:(c + 1) * P], k["ident"][:])
                    ins.then_inc(turned, 1)

                def experts(it, piece, is_first):
                    n, e, q = piece // 4, piece // 2 % 2, piece % 2
                    if piece == 0:
                        pe.wait_ge(xt_ready, it + 1)
                    if piece % 4 == 0 and (n or not is_first):
                        pe.wait_ge(x_taken, it * (NE + 1) + n)
                    ins = nc.tensor.matmul(x_ps[:, e * D:(e + 1) * D], xt[:, q, :],
                                           k["wexp"][:, q, (2 * n + e) * D:(2 * n + e + 1) * D], start=(q == 0), stop=(q == DH - 1))
                    if piece % 4 == 3:
                        ins.then_inc(e_psum, 1)

                def body(it, is_first, is_last):
                    if is_first:
                        for u in range(3):
                            scores(it, u, True)
                    for kt in range(KT):
                        scores_ahead(it, 2 * kt + 3, is_last)
                        pe.wait_ge(exp_done, it * UNITS + 2 * kt + 2)
                        if kt == 0:
                            if is_first:
                                pe.wait_ge(vg_ready, 1)
                            else:
                                pe.wait_ge(mixed_ready, it)
                        for h in range(GH):
                            ins = nc.tensor.matmul(pv_ps[32 * h:32 * h + VC, :], vg[:, kt, h, :],
                                                   probs[:, (2 * kt + h // 2) % 4, h % 2, :], start=(kt == 0), stop=(kt == KT - 1))
                        ins.then_inc(pv_done, 1)
                        if kt < KT - 1:
                            scores_ahead(it, 2 * kt + 4, is_last)
                        if kt == TURN_AFTER and not is_first:
                            turn_back(it)
                        for piece in range(sum(PIECES_AFTER[:kt]), sum(PIECES_AFTER[:kt + 1])):
                            experts(it, piece, is_first)
                    scores_ahead(it, 2 * KT + 2, is_last)

                nc.tensor.matmul(pv_ps[:], k["zero"][0:ROWS, :], kst[0:ROWS, s, 0, 0:SPAN], start=True, stop=True)
                query_spans(pe, body)
                turn_back(QS)

            @block.scalar
            def _(act):
                def body(it, is_first, is_last):
                    for u in range(UNITS):
                        act.wait_ge(s_psum, it * UNITS + u + 1)
                        if u >= 4 or not is_first:
                            act.wait_ge(pv_done, it * KT + u // 2 - 1)
                        nc.scalar.activation(probs[:, u % 4, :, :], s_ps[:, u % 3, :, :], ACT.Exp,
                                             scale=HD ** -0.5).then_inc(exp_done, 1)

                query_spans(act, body)

            @block.vector
            def _(vec):
                nc.vector.tensor_copy(vg[:], k["values"][:, :, bass.ds(hp * 8 + s * 4, 4), :]).then_inc(vg_ready, 1)
                with when(vec):
                    maxima.vector(vec)

                def take_turned(mine, it):
                    vec.wait_ge(turned, it)
                    heads = x_ps[:].rearrange("p (g e) -> p g e", e=32)
                    mine.add(nc.vector.reciprocal(inv[:], heads[:, :, HD]))
                    mine.wait(vec)
                    nc.vector.tensor_tensor(out[:], heads[:, :, 0:HD], inv[:].unsqueeze(2).to_broadcast([P, 4 * GH, HD]),
                                            ALU.mult).then_inc(x_taken, 1)
                    vec.wait_ge(x_taken, it * (NE + 1))
                    at = acc[:, bass.ds(it * 4 - 4, 4), bass.ds(hp * P + s * 64, GH * HD)]
                    mine.add(nc.vector.tensor_tensor(at, at, out[:].rearrange("p (c h) d -> p c (h d)", c=4), ALU.add))
                    mine.wait(vec)

                def body(it, is_first, is_last):
                    mine = Steps(own, 0 if is_first else it * (NE + 2) - 2)
                    if not is_first:
                        take_turned(mine, it)
                    t = hp * 8 + s * 4 + it
                    at = acc[:, bass.ds(t, 1), :].rearrange("p o d -> p (o d)")
                    for n in range(NE):
                        if n == NE - 1:
                            vec.wait_ge(pv_done, it * KT + KT)
                            nc.vector.tensor_copy(mixed[:], pv_ps[:]).then_inc(mixed_ready, 1)
                        vec.wait_ge(e_psum, it * NE + n + 1)
                        for e in range(2):
                            ins = nc.vector.scalar_tensor_tensor(
                                out=at, in0=x_ps[:, e * D:(e + 1) * D],
                                scalar=share[:, bass.ds(t, 1), 2 * n + e:2 * n + e + 1].rearrange("p o c -> p (o c)"),
                                in1=at, op0=ALU.mult, op1=ALU.add)
                            if e == 0:
                                mine.add(ins)
                                mine.wait(vec)
                        ins.then_inc(x_taken, 1)
                        vec.wait_ge(x_taken, it * (NE + 1) + n + 1)

                query_spans(vec, body)
                take_turned(Steps(own, QS * (NE + 2) - 2), QS)

        run_block(nc, names, blocks)


def store_batch(nc, k, b):
    with ExitStack() as ctx:
        stored = ctx.enter_context(nc.semaphore("batch_stored"))

        def blocks(block):
            @block.sync
            def _(sp):
                sp.dma_start(k["out"].rearrange("(b j p) d -> p b j d", p=P, j=L // P)[:, bass.ds(b, 1), :, :]
                             .rearrange("p b j d -> p (b j) d"), k["acc"][:]).then_inc(stored, 16)
                sp.wait_ge(stored, 16)

        run_block(nc, [stored], blocks)


def load_ffn_constants(nc, k):
    with ExitStack() as ctx:
        arrived = ctx.enter_context(nc.semaphore("ffn_arrived"))
        block = ctx.enter_context(nc.Block())

        @block.sync
        def _(sp):
            halves = lambda a: a.rearrange("(k p) e -> p k e", p=P)
            for dst, src in (("wexp", halves(k["in_wexp"])), ("wgate", halves(k["in_wgate"])),
                             ("row", k["in_row"]), ("lower", k["in_lower"]),
                             ("member", k["in_member"])):
                sp.dma_start(k[dst][:], src).then_inc(arrived, 16)
            sp.wait_ge(arrived, 5 * 16)

        @block.vector
        def _(vec):
            nc.vector.memset(k["zero"][:], 0.0)
            nc.vector.memset(k["all_ones"][:], 1.0)
            nc.vector.memset(k["share"][:], 0.0)
            nc.vector.memset(k["qst"][ROWS:ROWS + 3, :, :, :], 0.0)
            nc.vector.memset(k["values"][:], 1.0)
            nc.vector.memset(k["kst"][ROWS:ROWS + 3, :, :, :], 1.0)


def feed_forward(nc, k):
    with ExitStack() as ctx:
        sb = lambda n, shape, dt=F32: ctx.enter_context(nc.sbuf_tensor(n, shape, dt))
        k["acc"] = sb("acc", [P, L // P, D])
        k["parts"] = sb("parts", [P, 6, DH, L], BF16)
        k["values"] = sb("values", [P, L // P, HEADS, HD + 1])
        k["qst"] = sb("qst", [P, 2, GH, L], BF16)
        k["kst"] = sb("kst", [P, 2, GH, L], BF16)
        k["xnT"] = sb("xnT", [P, DH, L])
        k["share"] = sb("share", [P, L // P, 32])
        k["wexp"], k["wgate"] = sb("wexp", [P, DH, E * D]), sb("wgate", [P, DH, E])
        k["row"], k["lower"] = sb("row", [1, P + E]), sb("lower", [P, E, E])
        k["zero"] = sb("zero", [P, P], BF16)
        k["all_ones"], k["member"], k["shift"] = sb("all_ones", [P, P]), sb("member", [P, 9]), sb("shift", [P, HEADS])
        k["ranged"] = sb("ranged", [1, 1], I32)
        load_ffn_constants(nc, k)
        with nc.Fori(0, B) as b:
            project_queries_and_keys(nc, k, b)
            route_and_project_values(nc, k)
            with nc.Fori(0, 2) as hp:
                for s in range(2):
                    attend(nc, k, s, hp)
            store_batch(nc, k, b)


def build(nc, io):
    with ExitStack() as ctx:
        sb = lambda name, shape, dt=F32: ctx.enter_context(nc.sbuf_tensor(name, shape, dt))
        k = dict(io)
        k["vec"] = sb("vec", [P, NVEC])
        k["ident"] = sb("ident", [P, P])
        k["keep"] = sb("keep", [P, DH])
        k["away"] = sb("away", [P, DH])
        k["mean1"], k["rstd1"] = sb("mean1", [P, TILES]), sb("rstd1", [P, TILES])
        with ExitStack() as scan:
            sb2 = lambda name, shape, dt=F32: scan.enter_context(nc.sbuf_tensor(name, shape, dt))
            k["xy"] = sb2("xy", [P, TILES, D])
            inner = scan.enter_context(ExitStack())
            sb2 = lambda name, shape, dt=F32: inner.enter_context(nc.sbuf_tensor(name, shape, dt))
            k["gain"] = sb2("gain", [P, DH, T])
            k["drive"] = sb2("drive", [P, DH, T])
            normalise_and_gate(nc, k)
            k["state"] = sb2("state", [P, 2, DH, GL])
            k["start"] = sb2("start", [P, 2, DH, GL])
            k["ones"] = sb2("ones", [P, P])
            k["wr"] = sb2("wr", [P, DH, D])
            k["agree"] = sb2("agree", [1, 1], I32)
            prepare_sweeps(nc, k)
            sweep(nc, k, "sweep", SWEEPS)
            look_at_defect(nc, k)
            sweep(nc, k, "rest", CHUNKS, unless(k["agree"]))
            inner.close()
            project_states(nc, k)
        feed_forward(nc, k)


def kernel(L0_attn_x, L0_attn_decay, L0_attn_Wr, L0_attn_br, L0_attn_Wg, L0_attn_bg, L0_attn_Wo, L0_attn_bo,
           L0_attn_ln_w, L0_attn_ln_b, L0_ffn_W_qkv, L0_ffn_b_qkv, L0_ffn_W_gate, L0_ffn_b_gate,
           L0_ffn_W_experts, L0_ffn_b_experts):
    import numpy as np
    import concourse.bacc as bacc
    from concourse.bass_utils import run_bass_kernel_spmd

    lay = np.ascontiguousarray
    halves = lambda v: np.asarray(v).reshape(DH, P).T
    bqkv = np.asarray(L0_ffn_b_qkv)
    member = np.zeros((P, 9), np.float32)
    member[:, 0:8] = np.repeat(np.eye(8, dtype=np.float32), HD, axis=0)
    member[ROWS, 8] = -1.0
    spread = np.zeros((P, D), np.float32)
    for r in range(0, P, 32):
        spread[r:r + E] = np.asarray(L0_ffn_b_experts)
    arrays = {
        "in_x": lay(np.asarray(L0_attn_x).reshape(T, D)),
        "in_vec": lay(np.concatenate([halves(v) for v in (L0_attn_decay, L0_attn_br, L0_attn_bg, L0_attn_ln_w,
                                                          L0_attn_ln_b, bqkv[0:D], bqkv[D:2 * D])], axis=1)),
        "in_ident": np.eye(P, dtype=np.float32),
        "in_wg": lay(np.asarray(L0_attn_Wg).T),
        "in_wr": lay(np.asarray(L0_attn_Wr).T),
        "in_wo": lay(np.asarray(L0_attn_Wo).T),
        "in_wqkv": lay(np.asarray(L0_ffn_W_qkv)),
        "in_wexp": lay(np.asarray(L0_ffn_W_experts).transpose(1, 0, 2).reshape(D, E * D)),
        "in_wgate": lay(np.asarray(L0_ffn_W_gate)),
        "in_bv": lay(np.broadcast_to(bqkv[2 * D:], (P, D))),
        "in_bexp": spread,
        "in_row": lay(np.concatenate([np.ones(P, np.float32), np.asarray(L0_ffn_b_gate)])[None]),
        "in_member": member,
        "in_lower": lay(np.broadcast_to(np.tri(E, k=-1, dtype=np.float32), (P, E, E))),
        "in_bo": lay(np.broadcast_to(np.asarray(L0_attn_bo), (P, D))),
    }
    nc = bacc.Bacc("TRN2", target_bir_lowering=False, num_devices=1)
    io = {n: nc.dram_tensor(n, a.shape, mybir.dt.from_np(a.dtype), kind="ExternalInput").ap() for n, a in arrays.items()}
    io["out"] = nc.dram_tensor("out", (T, D), F32, kind="ExternalOutput").ap()
    io["x1"] = nc.dram_tensor("x1", (T, D), F32).ap()
    build(nc, io)
    r = run_bass_kernel_spmd(nc, [arrays], core_ids=[0])
    return r.results[0]["out"].reshape(B, L, D)
```

```python
from contextlib import ExitStack, nullcontext

import concourse.bass as bass
from concourse import mybir

F32 = mybir.dt.float32
F32R = mybir.dt.float32r
BF16 = mybir.dt.bfloat16
I32 = mybir.dt.int32
ALU = mybir.AluOpType
ACT = mybir.ActivationFunctionType
AX = mybir.AxisListType

P = 128
B, L, D = 4, 2048, 256
DH = D // P
T = B * L
TILES = T // P
EPS = 1e-5

SPAN = 512
SPANS = T // SPAN

STEPS = 32
CHUNKS = L // STEPS
LANES = B * CHUNKS
GL = LANES // 2
SWEEPS = 4
TOLERANCE = 2.0 ** -21

HEADS, HD = 16, 16
E, TOP_K = 8, 2

V_DECAY, V_BR, V_BG, V_LNW, V_LNB, V_BQ, V_BK = range(0, 14, 2)
NVEC = 14


class Steps:

    def __init__(self, sem, start=0):
        self.sem, self.start, self.n = sem, start, 0

    def add(self, ins):
        ins.then_inc(self.sem, 1)
        self.n += 1
        return self.start + self.n

    def wait(self, eng):
        eng.wait_ge(self.sem, self.start + self.n)


def statistics(nc, vec, own, s, sums, spread, n):
    me, mo = sums[:, 0:n, 1], sums[:, 0:n, 4]
    qe, qo = sums[:, 0:n, 2], sums[:, 0:n, 5]
    own.wait(vec)
    own.add(nc.vector.tensor_tensor(s["a"][:, 0:n], me, mo, ALU.add))
    own.add(nc.vector.tensor_tensor(s["b"][:, 0:n], me, mo, ALU.subtract))
    own.add(nc.vector.tensor_tensor(s["c"][:, 0:n], qe, qo, ALU.add))
    own.wait(vec)
    own.add(nc.vector.tensor_scalar(s["mean"][:, 0:n], s["a"][:, 0:n], 0.5, None, ALU.mult))
    own.add(nc.vector.tensor_tensor(s["d"][:, 0:n], s["b"][:, 0:n], s["b"][:, 0:n], ALU.mult))
    own.wait(vec)
    own.add(nc.vector.tensor_scalar(s["e"][:, 0:n], s["d"][:, 0:n], 0.25, EPS, ALU.mult, ALU.add))
    own.wait(vec)
    spread(nc.vector.scalar_tensor_tensor(out=s["var"][:, 0:n], in0=s["c"][:, 0:n], scalar=1.0 / D,
                                          in1=s["e"][:, 0:n], op0=ALU.mult, op1=ALU.add))


def inverse_root(nc, vec, own, s, n):
    own.add(nc.vector.reciprocal(s["a"][:, 0:n], s["root"][:, 0:n]))
    own.wait(vec)
    own.add(nc.vector.tensor_tensor(s["b"][:, 0:n], s["a"][:, 0:n], s["a"][:, 0:n], ALU.mult))
    own.wait(vec)
    own.add(nc.vector.tensor_tensor(s["c"][:, 0:n], s["b"][:, 0:n], s["var"][:, 0:n], ALU.mult))
    own.wait(vec)
    own.add(nc.vector.tensor_scalar(s["d"][:, 0:n], s["c"][:, 0:n], -0.5, 1.5, ALU.mult, ALU.add))
    own.wait(vec)
    own.add(nc.vector.tensor_tensor(s["rstd"][:, 0:n], s["a"][:, 0:n], s["d"][:, 0:n], ALU.mult))


def over_spans(eng, body):
    for u in range(2):
        body(u, u, u == 0, False, False)
    with eng.Fori(1, SPANS // 2 - 1) as i:
        for u in range(2):
            body(i * 2 + u, u, False, False, False)
    for u in range(2):
        body(SPANS - 2 + u, u, False, u == 1, True)


def normalise_and_gate(nc, k):
    X, gain, drive, vec_in = k["xy"], k["gain"], k["drive"], k["vec"]
    with ExitStack() as ctx:
        sem = lambda name: ctx.enter_context(nc.semaphore(name))
        sb = lambda name, shape, dt=F32: ctx.enter_context(nc.sbuf_tensor(name, shape, dt))
        ps = lambda name, shape, dt=F32: ctx.enter_context(nc.psum_tensor(name, shape, dt))
        PARTS = 8
        PT = TILES // PARTS
        x_in = [sem(f"x_in{c}") for c in range(PARTS)]
        const_in, stats_own, var_ready, root_ready = sem("const_in"), sem("stats_own"), sem("var_ready"), sem("root_ready")
        decay_ready = sem("decay_ready")
        xn_ready, xnT_psum, xnT_ready, z_psum, z_ready, drive_own, xnT_act = (
            sem("xn_ready"), sem("xnT_psum"), sem("xnT_ready"), sem("z_psum"), sem("z_ready"), sem("drive_own"), sem("xnT_act"))
        sums = sb("sums", [P, TILES, 6])
        s = {n: sb(f"st_{n}", [P, TILES]) for n in ("a", "b", "c", "d", "e", "mean", "var", "root", "rstd")}
        xn = sb("xn", [P, 2, 4, D])
        wg = sb("wg", [P, DH, D])
        xnT_ps = ps("xnT_ps", [P, 2, DH, SPAN])
        z_ps = ps("z_ps", [P, 2, DH, SPAN])
        block = ctx.enter_context(nc.Block())

        @block.sync
        def _(sp):
            xv = k["in_x"].rearrange("(t p) d -> p t d", p=P)
            for c in range(PARTS):
                sp.dma_start(X[:, c * PT:(c + 1) * PT, :], xv[:, c * PT:(c + 1) * PT, :]).then_inc(x_in[c], 16)
                if c == 0:
                    sp.dma_start(vec_in[:], k["in_vec"]).then_inc(const_in, 16)
                    sp.dma_start(k["ident"][:], k["in_ident"]).then_inc(const_in, 16)
                    sp.dma_start(wg[:], k["in_wg"].rearrange("(k p) e -> p k e", p=P)).then_inc(const_in, 16)

        @block.vector
        def _(vec):
            own = Steps(stats_own)
            for c in range(PARTS):
                vec.wait_ge(x_in[c], 16)
                for t in range(c * PT, (c + 1) * PT):
                    own.add(nc.vector.bn_stats(sums[:, t, :], X[:, t, :]))
            statistics(nc, vec, own, s, sums, lambda ins: ins.then_inc(var_ready, 1), TILES)
            vec.wait_ge(decay_ready, 1)
            own.add(nc.vector.tensor_scalar(k["away"][:], k["keep"][:], -1.0, 1.0, ALU.mult, ALU.add))
            vec.wait_ge(root_ready, 1)
            inverse_root(nc, vec, own, s, TILES)
            own.wait(vec)

            def normalised(g, u):
                for j in range(4):
                    ins = nc.vector.tensor_scalar(xn[:, u, j, :], X[:, bass.ds(g * 4 + j, 1), :].rearrange("p o d -> p (o d)"),
                                                  s["mean"][:, bass.ds(g * 4 + j, 1)],
                                                  s["rstd"][:, bass.ds(g * 4 + j, 1)], ALU.subtract, ALU.mult)
                ins.then_inc(xn_ready, 1)

            def second_half(g, u):
                vec.wait_ge(xnT_psum, g + 1)
                nc.vector.tensor_copy(drive[:, 1, bass.ds(g * SPAN, SPAN)], xnT_ps[:, u, 1, :]).then_inc(xnT_ready, 1)

            def gain_and_drive(mine, g):
                vec.wait_ge(z_ready, 2 * g + 6)
                for m in range(DH):
                    mine.add(nc.vector.tensor_scalar(gain[:, m, bass.ds(g * SPAN, SPAN)], gain[:, m, bass.ds(g * SPAN, SPAN)],
                                                     k["away"][:, m:m + 1], None, ALU.mult))
                mine.wait(vec)
                for m in range(DH):
                    mine.add(nc.vector.scalar_tensor_tensor(
                        out=drive[:, m, bass.ds(g * SPAN, SPAN)], in0=drive[:, m, bass.ds(g * SPAN, SPAN)],
                        scalar=vec_in[:, V_BR + m:V_BR + m + 1], in1=gain[:, m, bass.ds(g * SPAN, SPAN)],
                        op0=ALU.subtract, op1=ALU.mult))

            def body(g, u, is_first, is_last, ends):
                if not is_last:
                    second_half(g + 1, 1 - u)
                if not ends:
                    normalised(g + 2, u)
                if not is_first:
                    gain_and_drive(Steps(drive_own, g * 4 - 4), g - 1)

            for u in range(2):
                normalised(u, u)
            second_half(0, 0)
            over_spans(vec, body)
            gain_and_drive(Steps(drive_own, SPANS * 4 - 4), SPANS - 1)

        @block.scalar
        def _(act):
            act.sem_inc(z_ready, 4)
            act.wait_ge(var_ready, 1)
            nc.scalar.activation(s["root"][:], s["var"][:], ACT.Sqrt).then_inc(root_ready, 1)
            act.wait_ge(const_in, 48)
            nc.scalar.activation(k["keep"][:], vec_in[:, V_DECAY:V_DECAY + DH], ACT.Sigmoid).then_inc(decay_ready, 1)

            def first_half(g, u):
                act.wait_ge(xnT_psum, g + 1)
                nc.scalar.activation(drive[:, 0, bass.ds(g * SPAN, SPAN)], xnT_ps[:, u, 0, :], ACT.Identity).then_inc(xnT_act, 1)

            def body(g, u, is_first, is_last, ends):
                if not is_last:
                    first_half(g + 1, 1 - u)
                for m in range(DH):
                    act.wait_ge(z_psum, 2 * g + m + 1)
                    nc.scalar.activation(gain[:, m, bass.ds(g * SPAN, SPAN)], z_ps[:, u, m, :], ACT.Sigmoid,
                                         bias=vec_in[:, V_BG + m:V_BG + m + 1]).then_inc(z_ready, 1)

            first_half(0, 0)
            over_spans(act, body)

        @block.tensor
        def _(pe):
            def turn(g, u):
                pe.wait_ge(xn_ready, g + 1)
                for m in range(DH):
                    for j in range(4):
                        ins = nc.tensor.transpose(xnT_ps[:, u, m, j * P:(j + 1) * P],
                                                  xn[:, u, j, m * P:(m + 1) * P], k["ident"][:])
                ins.then_inc(xnT_psum, 1)

            def body(g, u, is_first, is_last, ends):
                if not is_last:
                    turn(g + 1, 1 - u)
                pe.wait_ge(xnT_ready, g + 1)
                pe.wait_ge(xnT_act, g + 1)
                pe.wait_ge(z_ready, 2 * g + 2)
                for m in range(DH):
                    for q in range(DH):
                        ins = nc.tensor.matmul(z_ps[:, u, m, :], wg[:, q, m * P:(m + 1) * P],
                                               drive[:, q, bass.ds(g * SPAN, SPAN)], start=(q == 0), stop=(q == DH - 1))
                    ins.then_inc(z_psum, 1)

            pe.wait_ge(const_in, 48)
            turn(0, 0)
            over_spans(pe, body)


def lanes_of(ap, g):
    return ap[:, g, :, :].rearrange("p m (b c) -> p m b c", c=CHUNKS)


def always(eng):
    return nullcontext()


def unless(flag):
    return lambda eng: eng.If(eng.value_load(flag[:], min_val=0, max_val=P) != P)


def sweep(nc, k, name, count, when=always, first=0):
    state, start = k["state"], k["start"]
    hist = k["xy"][:].rearrange("p t d -> p (t d)").rearrange("p (m c s) -> p m c s", m=DH, s=STEPS)
    drive = k["drive"][:].rearrange("p m (c s) -> p m c s", s=STEPS)
    gain = k["gain"][:].rearrange("p m (c s) -> p m c s", s=STEPS)
    at_step = lambda a, g, t: a[:, :, g * GL:(g + 1) * GL, bass.ds(t + first, 1)].rearrange("p m c o -> p m (c o)")
    S = STEPS - first
    with ExitStack() as ctx:
        sem = lambda n: ctx.enter_context(nc.semaphore(f"{name}_{n}"))
        sb = lambda n, shape, dt=F32: ctx.enter_context(nc.sbuf_tensor(f"{name}_{n}", shape, dt))
        ps = lambda n, shape, dt=F32: ctx.enter_context(nc.psum_tensor(f"{name}_{n}", shape, dt))
        kept = sb("kept", [P, 2, DH, GL])
        free = sb("free", [P, 2, DH, GL])
        bent = sb("bent", [P, 2, DH, GL])
        pred = ps("pred", [P, 2, 512])
        own = sem("own")
        state_ready = [sem(f"state_ready{g}") for g in range(2)]
        kept_ready = [sem(f"kept_ready{g}") for g in range(2)]
        free_ready = [sem(f"free_ready{g}") for g in range(2)]
        pred_ready = [sem(f"pred_ready{g}") for g in range(2)]
        stored = [sem(f"stored{g}") for g in range(2)]
        block = ctx.enter_context(nc.Block())
        TURN = 2

        @block.vector
        def _(vec):
            with when(vec), vec.Fori(0, count) as n:
                mine = Steps(own, n * (4 + TURN * S))
                for g in range(2):
                    for m in range(DH):
                        mine.add(nc.vector.tensor_copy(lanes_of(start, g)[:, m, :, 1:CHUNKS],
                                                       lanes_of(state, g)[:, m, :, 0:CHUNKS - 1]))
                mine.wait(vec)
                for g in range(2):
                    nc.vector.tensor_copy(state[:, g, :, :], start[:, g, :, :]).then_inc(state_ready[g], 1)
                with vec.Fori(0, S) as t:
                    turn = Steps(own, n * (4 + TURN * S) + 4 + t * TURN)
                    for g in range(2):
                        vec.wait_ge(pred_ready[g], n * S + t + 1)
                        turn.add(nc.vector.tensor_tensor(bent[:, g, :, :], pred[:, g, 0:DH * GL].rearrange("p (m c) -> p m c", m=DH),
                                                         at_step(gain, g, t), ALU.mult))
                        turn.wait(vec)
                        vec.wait_ge(free_ready[g], n * S + t + 1)
                        vec.wait_ge(stored[g], n * S + t + 1)
                        nc.vector.tensor_tensor(state[:, g, :, :], free[:, g, :, :], bent[:, g, :, :],
                                                ALU.subtract).then_inc(state_ready[g], 1)
                for g in range(2):
                    vec.wait_ge(state_ready[g], (n + 1) * (S + 1))
                    vec.wait_ge(stored[g], (n + 1) * S + 1)

        @block.tensor
        def _(pe):
            with when(pe), pe.Fori(0, count) as n:
                with pe.Fori(0, S) as t:
                    for g in range(2):
                        pe.wait_ge(state_ready[g], n * (S + 1) + t + 1)
                        for m in range(DH):
                            for q in range(DH):
                                ins = nc.tensor.matmul(pred[:, g, m * GL:(m + 1) * GL], k["wr"][:, q, m * P:(m + 1) * P],
                                                       state[:, g, q, :], start=(q == 0), stop=(q == DH - 1))
                        ins.then_inc(pred_ready[g], 1)

        @block.scalar
        def _(act):
            def keep_state(g):
                for m in range(DH):
                    nc.scalar.activation(kept[:, g, m, :], state[:, g, m, :], ACT.Copy,
                                         scale=k["keep"][:, m:m + 1]).then_inc(kept_ready[g], 1)

            for g in range(2):
                act.sem_inc(stored[g], 1)
            with when(act), act.Fori(0, count) as n:
                for g in range(2):
                    act.wait_ge(state_ready[g], n * (S + 1) + 1)
                    keep_state(g)
                with act.Fori(0, S) as t:
                    for g in range(2):
                        act.wait_ge(state_ready[g], n * (S + 1) + t + 2)
                        keep_state(g)
                        nc.scalar.copy(at_step(hist, g, t), state[:, g, :, :]).then_inc(stored[g], 1)

        @block.gpsimd
        def _(pool):
            with when(pool), pool.Fori(0, count) as n:
                with pool.Fori(0, S) as t:
                    for g in range(2):
                        for m in range(DH):
                            pool.wait_ge(kept_ready[g], (n * (S + 1) + t) * DH + m + 1)
                            ins = nc.gpsimd.tensor_tensor(free[:, g, m, :], kept[:, g, m, :], at_step(drive, g, t)[:, m, :], ALU.add)
                        ins.then_inc(free_ready[g], 1)


def prepare_sweeps(nc, k):
    with ExitStack() as ctx:
        wr_in = ctx.enter_context(nc.semaphore("wr_in"))
        block = ctx.enter_context(nc.Block())

        @block.sync
        def _(sp):
            sp.dma_start(k["wr"][:], k["in_wr"].rearrange("(k p) e -> p k e", p=P)).then_inc(wr_in, 16)
            sp.wait_ge(wr_in, 16)

        @block.vector
        def _(vec):
            nc.vector.memset(k["state"][:], 0.0)
            nc.vector.memset(k["start"][:], 0.0)
            nc.vector.memset(k["ones"][:], 1.0)


def look_at_defect(nc, k):
    with ExitStack() as ctx:
        sem = lambda n: ctx.enter_context(nc.semaphore(f"defect_{n}"))
        sb = lambda n, shape, dt=F32: ctx.enter_context(nc.sbuf_tensor(f"defect_{n}", shape, dt))
        size, gap, wide = sb("size", [P, 2, DH, GL]), sb("gap", [P, 2, DH, GL]), sb("wide", [P, 2, DH, GL])
        most, bound, close, all_close = sb("most", [P, DH]), sb("bound", [P, DH]), sb("close", [P, 2, DH, GL]), sb("all_close", [P, 1])
        total = ctx.enter_context(nc.psum_tensor("defect_total", [P, 1], F32))
        own, flags_ready, total_ready = sem("own"), sem("flags_ready"), sem("total_ready")
        block = ctx.enter_context(nc.Block())

        @block.vector
        def _(vec):
            mine = Steps(own)
            flat = lambda ap: ap[:].rearrange("p g m c -> p (g m c)")
            mine.add(nc.vector.scalar_tensor_tensor(out=flat(size), in0=flat(k["state"]), scalar=-1.0, in1=flat(k["state"]),
                                                    op0=ALU.mult, op1=ALU.max))
            mine.add(nc.vector.memset(gap[:], 0.0))
            mine.wait(vec)
            for g in range(2):
                for m in range(DH):
                    mine.add(nc.vector.tensor_tensor(lanes_of(gap, g)[:, m, :, 1:CHUNKS],
                                                     lanes_of(k["state"], g)[:, m, :, 0:CHUNKS - 1],
                                                     lanes_of(k["start"], g)[:, m, :, 1:CHUNKS], ALU.subtract))
            mine.add(nc.vector.tensor_reduce(most[:], size[:].rearrange("p g m c -> p m g c"), AX.XY, ALU.max))
            mine.wait(vec)
            mine.add(nc.vector.tensor_scalar(bound[:], most[:], TOLERANCE, None, ALU.mult))
            mine.add(nc.vector.scalar_tensor_tensor(out=flat(wide), in0=flat(gap), scalar=-1.0, in1=flat(gap),
                                                    op0=ALU.mult, op1=ALU.max))
            mine.wait(vec)
            for m in range(DH):
                mine.add(nc.vector.tensor_scalar(close[:, :, m, :], wide[:, :, m, :], bound[:, m:m + 1], None, ALU.is_le))
            mine.wait(vec)
            nc.vector.tensor_reduce(all_close[:], close[:], AX.XYZ, ALU.min).then_inc(flags_ready, 1)
            vec.wait_ge(total_ready, 1)
            nc.vector.tensor_copy(k["agree"][:], total[0:1, :])

        @block.tensor
        def _(pe):
            pe.wait_ge(flags_ready, 1)
            nc.tensor.matmul(total[:], k["ones"][:], all_close[:], start=True, stop=True).then_inc(total_ready, 1)


def project_states(nc, k):
    hist = k["xy"][:].rearrange("p t d -> p (t d)").rearrange("p (m t) -> p m t", m=DH)
    vec_in = k["vec"]
    SLOTS = 4
    with ExitStack() as ctx:
        sem = lambda n: ctx.enter_context(nc.semaphore(f"proj_{n}"))
        sb = lambda n, shape, dt=F32: ctx.enter_context(nc.sbuf_tensor(f"proj_{n}", shape, dt))
        ps = lambda n, shape, dt=F32: ctx.enter_context(nc.psum_tensor(f"proj_{n}", shape, dt))
        wo, bo = sb("wo", [P, DH, D]), sb("bo", [P, D])
        scaled, centred = sb("scaled", [P, DH, D]), sb("centred", [P, DH, D])
        shares = sb("shares", [P, P])
        shifts = sb("shifts", [P, DH, P])
        added = sb("added", [P, D])
        hs = sb("hs", [P, 2, DH, SPAN])
        x1 = sb("x1", [P, SLOTS, 4, D])
        sums, sums1 = sb("sums", [P, TILES, 6]), sb("sums1", [P, TILES, 6])
        s = {n: sb(f"st_{n}", [P, TILES]) for n in ("a", "b", "c", "d", "e", "mean", "var", "root", "rstd")}
        s1 = {n: sb(f"st1_{n}", [P, TILES]) for n in ("a", "b", "c", "d", "e", "var", "root")}
        s1["mean"], s1["rstd"] = k["mean1"], k["rstd1"]
        h_ps = ps("h_ps", [P, 2, 4, D])
        o_ps = ps("o_ps", [P, 2, 4, D])
        const_in, own, scaled_ready, sums_psum, added_ready = (
            sem(n) for n in ("const_in", "own", "scaled_ready", "sums_psum", "added_ready"))
        hs_ready, h_psum, h_taken, o_psum, x1_ready, xb_ready, var_ready, root_ready = (
            sem(n) for n in ("hs_ready", "h_psum", "h_taken", "o_psum", "x1_ready", "xb_ready", "var_ready", "root_ready"))
        x_in = [sem(f"x_in{u}") for u in range(SLOTS)]
        x1_out = [sem(f"x1_out{u}") for u in range(SLOTS)]
        block = ctx.enter_context(nc.Block())
        xv = k["in_x"].rearrange("(g j p) d -> p g j d", p=P, j=4)
        x1v = k["x1"].rearrange("(g j p) d -> p g j d", p=P, j=4)
        one = lambda v, g: v[:, bass.ds(g, 1), :, :].rearrange("p g j d -> p (g j) d")

        @block.sync
        def _(sp):
            sp.dma_start(wo[:], k["in_wo"].rearrange("(k p) e -> p k e", p=P)).then_inc(const_in, 16)
            sp.dma_start(bo[:], k["in_bo"]).then_inc(const_in, 16)
            for u in range(SLOTS):
                sp.dma_start(x1[:, u, :, :], xv[:, u, :, :]).then_inc(x_in[u], 16)
            with sp.Fori(0, SPANS // SLOTS - 1) as i:
                for u in range(SLOTS):
                    sp.wait_ge(x1_ready, i * SLOTS + u + 3)
                    sp.dma_start(one(x1v, i * SLOTS + u), x1[:, u, :, :]).then_inc(x1_out[u], 16)
                    if u:
                        sp.wait_ge(x1_out[u - 1], i * 16 + 16)
                        sp.dma_start(x1[:, u - 1, :, :], one(xv, i * SLOTS + SLOTS + u - 1)).then_inc(x_in[u - 1], 16)
                sp.wait_ge(x1_out[SLOTS - 1], i * 16 + 16)
                sp.dma_start(x1[:, SLOTS - 1, :, :], one(xv, i * SLOTS + 2 * SLOTS - 1)).then_inc(x_in[SLOTS - 1], 16)
            for u in range(SLOTS):
                sp.wait_ge(x1_ready, SPANS - SLOTS + u + 3)
                sp.dma_start(x1v[:, SPANS - SLOTS + u, :, :], x1[:, u, :, :]).then_inc(x1_out[u], 16)
            for u in range(SLOTS):
                sp.wait_ge(x1_out[u], 16 * SPANS // SLOTS)

        @block.gpsimd
        def _(pool):
            pool.wait_ge(added_ready, 1)
            with pool.Fori(0, SPANS // SLOTS) as i:
                for u in range(SLOTS):
                    pool.wait_ge(x_in[u], i * 16 + 16)
                    nc.gpsimd.tensor_tensor(x1[:, u, :, :], x1[:, u, :, :], added[:].unsqueeze(1).to_broadcast([P, 4, D]),
                                            ALU.add).then_inc(xb_ready, 1)

        @block.scalar
        def _(act):
            with act.Fori(0, SPANS // 2) as i:
                for u in range(2):
                    act.wait_ge(h_psum, i * 2 + u + 1)
                    nc.scalar.activation(hs[:, u, :, :], hist[:, :, bass.ds((i * 2 + u) * SPAN, SPAN)], ACT.Identity).then_inc(hs_ready, 1)
            act.wait_ge(h_psum, SPANS + 2)
            act.wait_ge(var_ready, 1)
            nc.scalar.activation(s["root"][:], s["var"][:], ACT.Sqrt).then_inc(root_ready, 1)
            with act.Fori(0, SPANS // 2) as i:
                for u in range(2):
                    act.wait_ge(o_psum, i * 2 + u + 1)
                    nc.scalar.activation(hs[:, u, :, :], hist[:, :, bass.ds((i * 2 + u) * SPAN, SPAN)], ACT.Identity).then_inc(hs_ready, 1)
            act.wait_ge(var_ready, 2)
            nc.scalar.activation(s1["root"][:], s1["var"][:], ACT.Sqrt).then_inc(root_ready, 1)

        @block.tensor
        def _(pe):
            pe.sem_inc(h_psum, 2)
            pe.sem_inc(o_psum, 2)
            with pe.Fori(0, SPANS // 2) as i:
                for u in range(2):
                    pe.wait_ge(hs_ready, i * 2 + u + 1)
                    pe.wait_ge(h_taken, i * 2 + u + 1)
                    for j in range(4):
                        for m in range(DH):
                            ins = nc.tensor.transpose(h_ps[:, u, j, m * P:(m + 1) * P], hs[:, u, m, j * P:(j + 1) * P], k["ident"][:])
                    ins.then_inc(h_psum, 1)
            pe.wait_ge(scaled_ready, 1)
            for q in range(DH):
                nc.tensor.matmul(o_ps[:, 0, 0, :], shares[:], scaled[:, q, :], start=(q == 0), stop=(q == DH - 1))
            for q in range(DH):
                ins = nc.tensor.matmul(o_ps[:, 1, 0, :], shifts[:, q, :], wo[:, q, :], start=(q == 0), stop=(q == DH - 1))
            ins.then_inc(sums_psum, 1)
            pe.wait_ge(added_ready, 1)
            with pe.Fori(0, SPANS // 2) as i:
                for u in range(2):
                    pe.wait_ge(hs_ready, i * 2 + u + SPANS + 1)
                    pe.wait_ge(x1_ready, i * 2 + u + 1)
                    for j in range(4):
                        for q in range(DH):
                            ins = nc.tensor.matmul(o_ps[:, u, j, :], hs[:, u, q, j * P:(j + 1) * P], centred[:, q, :],
                                                   start=(q == 0), stop=(q == DH - 1))
                    ins.then_inc(o_psum, 1)

        @block.vector
        def _(vec):
            vec.sem_inc(h_taken, 2)
            vec.sem_inc(x1_ready, 2)
            mine = Steps(own)
            mine.add(nc.vector.memset(shares[:], 1.0 / D))
            mine.wait(vec)
            vec.wait_ge(const_in, 32)
            for q in range(DH):
                nc.vector.tensor_scalar(scaled[:, q, :], wo[:, q, :], vec_in[:, V_LNW + q:V_LNW + q + 1], None, ALU.mult)
                ins = nc.vector.tensor_scalar(shifts[:, q, :], shares[:], vec_in[:, V_LNB + q:V_LNB + q + 1], float(D), ALU.mult, ALU.mult)
            ins.then_inc(scaled_ready, 1)
            with vec.Fori(0, SPANS // 2) as i:
                for u in range(2):
                    vec.wait_ge(h_psum, i * 2 + u + 3)
                    for j in range(4):
                        ins = nc.vector.bn_stats(sums[:, bass.ds((i * 2 + u) * 4 + j, 1), :].rearrange("p o c -> p (o c)"), h_ps[:, u, j, :])
                    ins.then_inc(h_taken, 1)
            vec.wait_ge(h_taken, SPANS + 2)
            statistics(nc, vec, mine, s, sums, lambda ins: ins.then_inc(var_ready, 1), TILES)
            vec.wait_ge(sums_psum, 1)
            for q in range(DH):
                nc.vector.tensor_tensor(centred[:, q, :], scaled[:, q, :], o_ps[:, 0, 0, :], ALU.subtract)
            nc.vector.tensor_tensor(added[:], o_ps[:, 1, 0, :], bo[:], ALU.add).then_inc(added_ready, 1)
            vec.wait_ge(root_ready, 1)
            inverse_root(nc, vec, mine, s, TILES)
            mine.wait(vec)
            before = mine.n
            with vec.Fori(0, SPANS // SLOTS) as i:
                for u in range(SLOTS):
                    g = i * SLOTS + u
                    turn = Steps(own, g * 4 + before)
                    vec.wait_ge(o_psum, g + 3)
                    vec.wait_ge(xb_ready, g + 1)
                    for j in range(4):
                        turn.add(nc.vector.scalar_tensor_tensor(out=x1[:, u, j, :], in0=o_ps[:, u % 2, j, :],
                                                                scalar=s["rstd"][:, bass.ds(g * 4 + j, 1)], in1=x1[:, u, j, :],
                                                                op0=ALU.mult, op1=ALU.add))
                    turn.wait(vec)
                    for j in range(4):
                        ins = nc.vector.bn_stats(sums1[:, bass.ds(g * 4 + j, 1), :].rearrange("p o c -> p (o c)"), x1[:, u, j, :])
                    ins.then_inc(x1_ready, 1)
            vec.wait_ge(x1_ready, SPANS + 2)
            mine = Steps(own, before + SPANS * 4)
            statistics(nc, vec, mine, s1, sums1, lambda ins: ins.then_inc(var_ready, 1), TILES)
            vec.wait_ge(root_ready, 2)
            inverse_root(nc, vec, mine, s1, TILES)


def run_block(nc, sems, build_block):
    with nc.Block() as block:
        build_block(block)
    for s in sems:
        nc.gpsimd.sem_clear(s)
    nc.all_engine_barrier()


SAFE = 160.0

Q_PARTS = (0, 0, 1, 0, 2, 1)
K_PARTS = (3, 4, 3, 5, 3, 4)
ROWS = 6 * 16
GH = 4


def load_stacks(nc, k, eng, s, m, arrived):
    for which, plan in (("qst", Q_PARTS), ("kst", K_PARTS)):
        for i, part in enumerate(plan):
            for h in range(GH):
                at = 64 * s + HD * h
                eng.dma_start(k[which][HD * i:HD * i + HD, s, h, :],
                              k["parts"][at:at + HD, part, bass.ds(m, 1), :].rearrange("p o t -> p (o t)")).then_inc(arrived, 16)
    return 2 * 6 * GH * 16


def shift_by_bound(nc, k, s, m):
    return nc.gpsimd.tensor_tensor(k["qst"][ROWS:ROWS + 3, s, :, :], k["kst"][ROWS:ROWS + 3, s, :, :],
                                   k["shift"][ROWS:ROWS + 3, bass.ds(m * 8 + s * GH, GH)].unsqueeze(2).to_broadcast([3, GH, L]),
                                   ALU.mult)


def project_queries_and_keys(nc, k, b):
    acc, parts, xnT, vec_in = k["acc"], k["parts"], k["xnT"], k["vec"]
    NT, G = L // P, L // SPAN
    with ExitStack() as ctx:
        names = []

        def sem(n):
            names.append(ctx.enter_context(nc.semaphore(f"qk_{n}")))
            return names[-1]

        sb = lambda n, shape, dt=F32: ctx.enter_context(nc.sbuf_tensor(f"qk_{n}", shape, dt))
        ps = lambda n, shape, dt=F32: ctx.enter_context(nc.psum_tensor(f"qk_{n}", shape, dt))
        wqk = sb("wqk", [P, DH, 2 * D])
        free = k["qst"][:].rearrange("p s h t -> p (s h t)").bitcast(F32).rearrange("p (n t) -> p n t", t=SPAN)
        whole = free[:, 0:4, :]
        size = free[:, 4:8, :]
        rest = free[:, 8:12, :]
        xn = free[:, 14:16, :].rearrange("p n (j d) -> p (n j) d", d=D)
        peaks = sb("peaks", [P, G, 4])
        wide, both, by_head = sb("wide", [P, 4]), sb("both", [P, DH]), sb("by_head", [P, HEADS])
        safe, all_safe = sb("safe", [P, HEADS]), sb("all_safe", [P, 1])
        xT_ps = ps("xT_ps", [P, 2, DH, SPAN])
        q_ps = ps("q_ps", [P, 4, SPAN])
        w_in, x_first, x_rest, own = sem("w_in"), sem("x_first"), sem("x_rest"), sem("own")
        xn_ready, xT_psum, low_ready, high_ready = sem("xn_ready"), sem("xT_psum"), sem("low_ready"), sem("high_ready")
        q_psum, whole_ready, size_ready, rest_ready, second_ready, third_ready = (
            sem(n) for n in ("q_psum", "whole_ready", "size_ready", "rest_ready", "second_ready", "third_ready"))
        peaks_ready = sem("peaks_ready")
        by_head_ready, bound_psum, safe_ready, safe_psum = (sem(n) for n in ("by_head_ready", "bound_psum", "safe_ready", "safe_psum"))

        def blocks(block):
            x1v = k["x1"].rearrange("(b j p) d -> p b j d", p=P, j=NT)

            @block.sync
            def _(sp):
                for arrived, lo, hi in ((x_first, 0, 4), (x_rest, 4, NT)):
                    sp.dma_start(acc[:, lo:hi, :], x1v[:, bass.ds(b, 1), lo:hi, :].rearrange("p b j d -> p (b j) d")).then_inc(arrived, 16)
                sp.dma_start(wqk[:], k["in_wqkv"].rearrange("(k p) e -> p k e", p=P)[:, :, 0:2 * D]).then_inc(w_in, 16)

            @block.scalar
            def _(act):
                def low_half(g):
                    act.wait_ge(xT_psum, g + 1)
                    nc.scalar.copy(xnT[:, 0, g * SPAN:(g + 1) * SPAN], xT_ps[:, g % 2, 0, :]).then_inc(low_ready, 1)

                low_half(0)
                for g in range(G):
                    at = slice(g * SPAN, (g + 1) * SPAN)
                    for o in range(4):
                        n = 4 * g + o
                        v = V_BQ + o if o < 2 else V_BK + o - 2
                        act.wait_ge(q_psum, n + 1)
                        if g:
                            act.wait_ge(rest_ready, n - 3)
                            act.wait_ge(peaks_ready, n - 3)
                        nc.scalar.activation(whole[:, o, :], q_ps[:, o, :], ACT.Identity, bias=vec_in[:, v:v + 1])
                        nc.scalar.activation(parts[:, 3 * (o // 2), o % 2, at], q_ps[:, o, :],
                                             ACT.Identity, bias=vec_in[:, v:v + 1]).then_inc(whole_ready, 1)
                        nc.scalar.activation(size[:, o, :], q_ps[:, o, :], ACT.Abs, bias=vec_in[:, v:v + 1]).then_inc(size_ready, 1)
                        if o == 1 and g + 1 < G:
                            low_half(g + 1)

            @block.gpsimd
            def _(pool):
                for n in range(4 * G):
                    g, o = n // 4, n % 4
                    at, first = slice(g * SPAN, (g + 1) * SPAN), 3 * (o // 2)
                    pool.wait_ge(second_ready, n + 1)
                    nc.gpsimd.tensor_tensor(parts[:, first + 2, o % 2, at], rest[:, o, :],
                                            parts[:, first + 1, o % 2, at], ALU.subtract).then_inc(third_ready, 1)

            @block.tensor
            def _(pe):
                def turn(g):
                    pe.wait_ge(xn_ready, g + 1)
                    if g >= 2:
                        pe.wait_ge(low_ready, g - 1)
                        pe.wait_ge(high_ready, g - 1)
                    for m in range(DH):
                        for j in range(4):
                            ins = nc.tensor.transpose(xT_ps[:, g % 2, m, j * P:(j + 1) * P], xn[:, j, m * P:(m + 1) * P], k["ident"][:])
                    ins.then_inc(xT_psum, 1)

                turn(0)
                pe.wait_ge(w_in, 16)
                for g in range(G):
                    pe.wait_ge(low_ready, g + 1)
                    pe.wait_ge(high_ready, g + 1)
                    for o in range(4):
                        if o == 1 and g + 1 < G:
                            turn(g + 1)
                        if g:
                            pe.wait_ge(size_ready, 4 * g + o - 3)
                        for q in range(DH):
                            ins = nc.tensor.matmul(q_ps[:, o, :], wqk[:, q, o * P:(o + 1) * P], xnT[:, q, g * SPAN:(g + 1) * SPAN],
                                                   start=(q == 0), stop=(q == DH - 1))
                        ins.then_inc(q_psum, 1)
                pe.wait_ge(by_head_ready, 1)
                nc.tensor.matmul(q_ps[:, 0, 0:HEADS], k["all_ones"][:], by_head[:], start=True, stop=True).then_inc(bound_psum, 1)
                pe.wait_ge(safe_ready, 1)
                nc.tensor.matmul(q_ps[0:1, 1, 0:1], k["all_ones"][:, 0:1], all_safe[:], start=True, stop=True).then_inc(safe_psum, 1)

            @block.vector
            def _(vec):
                mine = Steps(own)

                def normalise(g):
                    if g:
                        vec.wait_ge(xT_psum, g)
                    for j in range(4):
                        t = b * NT + (g * 4 + j)
                        ins = nc.vector.tensor_scalar(xn[:, j, :], acc[:, g * 4 + j, :], k["mean1"][:, bass.ds(t, 1)],
                                                      k["rstd1"][:, bass.ds(t, 1)], ALU.subtract, ALU.mult)
                    ins.then_inc(xn_ready, 1)

                def high_half(g):
                    vec.wait_ge(xT_psum, g + 1)
                    nc.vector.tensor_copy(xnT[:, 1, g * SPAN:(g + 1) * SPAN], xT_ps[:, g % 2, 1, :]).then_inc(high_ready, 1)
                    if g + 1 < G:
                        normalise(g + 1)

                vec.wait_ge(x_first, 16)
                normalise(0)
                vec.wait_ge(x_rest, 16)
                high_half(0)
                for g in range(G):
                    at = slice(g * SPAN, (g + 1) * SPAN)
                    for o in range(4):
                        n, first = 4 * g + o, 3 * (o // 2)
                        vec.wait_ge(whole_ready, n + 1)
                        if g:
                            vec.wait_ge(third_ready, n - 3)
                        nc.vector.tensor_tensor(rest[:, o, :], whole[:, o, :], parts[:, first, o % 2, at],
                                                ALU.subtract).then_inc(rest_ready, 1)
                        vec.wait_ge(rest_ready, n + 1)
                        nc.vector.tensor_copy(parts[:, first + 1, o % 2, at], rest[:, o, :]).then_inc(second_ready, 1)
                        vec.wait_ge(size_ready, n + 1)
                        nc.vector.tensor_reduce(peaks[:, g, o:o + 1], size[:, o, :], AX.X, ALU.max).then_inc(peaks_ready, 1)
                        if o == 1 and g + 1 < G:
                            high_half(g + 1)
                vec.wait_ge(peaks_ready, 4 * G)
                mine.add(nc.vector.tensor_reduce(wide[:], peaks[:].rearrange("p g o -> p o g"), AX.X, ALU.max))
                mine.wait(vec)
                mine.add(nc.vector.tensor_tensor(both[:], wide[:, 0:2], wide[:, 2:4], ALU.mult))
                mine.wait(vec)
                for m in range(DH):
                    ins = nc.vector.tensor_scalar(by_head[:, 8 * m:8 * m + 8], k["member"][:, 0:8], both[:, m:m + 1], None, ALU.mult)
                ins.then_inc(by_head_ready, 1)
                vec.wait_ge(bound_psum, 1)
                mine.add(nc.vector.tensor_scalar(k["shift"][:], q_ps[:, 0, 0:HEADS], k["member"][:, 8:9], None, ALU.mult))
                mine.add(nc.vector.tensor_scalar(safe[:], q_ps[:, 0, 0:HEADS], SAFE, None, ALU.is_le))
                mine.wait(vec)
                nc.vector.tensor_reduce(all_safe[:], safe[:], AX.X, ALU.min).then_inc(safe_ready, 1)
                vec.wait_ge(safe_psum, 1)
                nc.vector.tensor_copy(k["ranged"][:], q_ps[0:1, 1, 0:1])

        run_block(nc, names, blocks)


def route_and_project_values(nc, k):
    values, xnT, share = k["values"], k["xnT"], k["share"]
    NT = L // P
    with ExitStack() as ctx:
        names = []

        def sem(n):
            names.append(ctx.enter_context(nc.semaphore(f"v_{n}")))
            return names[-1]

        sb = lambda n, shape, dt=F32: ctx.enter_context(nc.sbuf_tensor(f"v_{n}", shape, dt))
        ps = lambda n, shape, dt=F32: ctx.enter_context(nc.psum_tensor(f"v_{n}", shape, dt))
        wv, bv = sb("wv", [P, DH, D]), sb("bv", [P, D])
        top, tot, inv = sb("top", [P, NT]), sb("tot", [P, NT]), sb("inv", [P, NT])
        lg, ex, pr, rank = (sb(n, [P, NT, E]) for n in ("lg", "ex", "pr", "rank"))
        more, same = sb("more", [P, NT, E, E]), sb("same", [P, NT, E, E])
        l_ps, v_ps = ps("l_ps", [P, NT, E]), ps("v_ps", [P, 2, 2, D])
        w_in, arrived, own = sem("w_in"), sem("arrived"), sem("own")
        l_psum, lg_ready, ex_ready = sem("l_psum"), sem("lg_ready"), sem("ex_ready")
        v_psum, v_taken = sem("v_psum"), sem("v_taken")

        def note_range(eng):
            k["ranged_of"][eng.engine] = eng.value_load(k["ranged"][:], min_val=0, max_val=P)

        def blocks(block):
            @block.sync
            def _(sp):
                note_range(sp)
                sp.dma_start(wv[:], k["in_wqkv"].rearrange("(k p) e -> p k e", p=P)[:, :, 2 * D:3 * D]).then_inc(w_in, 16)
                sp.dma_start(bv[:], k["in_bv"]).then_inc(w_in, 16)
                sp.wait_ge(arrived, load_stacks(nc, k, sp, 0, 0, arrived))

            @block.gpsimd
            def _(pool):
                shift_by_bound(nc, k, 0, 0)

            @block.scalar
            def _(act):
                note_range(act)
                act.wait_ge(lg_ready, 1)
                nc.scalar.activation(ex[:], lg[:], ACT.Exp).then_inc(ex_ready, 1)

            @block.tensor
            def _(pe):
                note_range(pe)
                for t in range(NT):
                    at = slice(t * P, (t + 1) * P)
                    for q in range(DH):
                        ins = nc.tensor.matmul(l_ps[:, t, :], xnT[:, q, at], k["wgate"][:, q, :], start=(q == 0), stop=(q == DH - 1))
                ins.then_inc(l_psum, 1)
                pe.wait_ge(w_in, 32)
                for n in range(NT // 2):
                    if n >= 2:
                        pe.wait_ge(v_taken, n - 1)
                    for j in range(2):
                        t = 2 * n + j
                        for q in range(DH):
                            ins = nc.tensor.matmul(v_ps[:, n % 2, j, :], xnT[:, q, t * P:(t + 1) * P], wv[:, q, :],
                                                   start=(q == 0), stop=(q == DH - 1))
                    ins.then_inc(v_psum, 1)

            @block.vector
            def _(vec):
                note_range(vec)
                mine = Steps(own)

                def take_values(n):
                    vec.wait_ge(v_psum, n + 1)
                    nc.vector.tensor_tensor(values[:, 2 * n:2 * n + 2, :, 0:HD],
                                            v_ps[:, n % 2, :, :].rearrange("p j (h d) -> p j h d", d=HD),
                                            bv[:].rearrange("p (h d) -> p h d", d=HD).unsqueeze(1).to_broadcast([P, 2, HEADS, HD]),
                                            ALU.add).then_inc(v_taken, 1)

                def then(ins):
                    mine.add(ins)
                    mine.wait(vec)

                spread = lambda a: a[:].unsqueeze(2).to_broadcast([P, NT, E])
                vec.wait_ge(l_psum, 1)
                then(nc.vector.tensor_tensor(pr[:], l_ps[:], k["bgate"][:].unsqueeze(1).to_broadcast([P, NT, E]), ALU.add))
                then(nc.vector.tensor_reduce(top[:], pr[:], AX.X, ALU.max))
                nc.vector.tensor_tensor(lg[:], pr[:], spread(top), ALU.subtract).then_inc(lg_ready, 1)
                vec.wait_ge(w_in, 32)
                take_values(0)
                take_values(1)
                vec.wait_ge(ex_ready, 1)
                then(nc.vector.tensor_reduce(tot[:], ex[:], AX.X, ALU.add))
                then(nc.vector.reciprocal(inv[:], tot[:]))
                then(nc.vector.tensor_tensor(pr[:], ex[:], spread(inv), ALU.mult))
                take_values(2)
                take_values(3)
                full = [P, NT, E, E]
                each, other = pr[:].unsqueeze(3).to_broadcast(full), pr[:].unsqueeze(2).to_broadcast(full)
                mine.add(nc.vector.tensor_tensor(more[:], other, each, ALU.is_gt))
                then(nc.vector.tensor_tensor(same[:], other, each, ALU.is_equal))
                then(nc.vector.tensor_tensor(same[:], same[:], k["lower"][:].unsqueeze(1).to_broadcast(full), ALU.mult))
                take_values(4)
                take_values(5)
                then(nc.vector.tensor_tensor(more[:], more[:], same[:], ALU.add))
                then(nc.vector.tensor_reduce(rank[:], more[:], AX.X, ALU.add))
                nc.vector.scalar_tensor_tensor(out=share[:], in0=rank[:], scalar=TOP_K - 0.5, in1=pr[:],
                                               op0=ALU.is_lt, op1=ALU.mult)
                take_values(6)
                take_values(7)

        run_block(nc, names, blocks)


class Maxima:
    QT = L // P

    def __init__(self, nc, k, s, sem, s_ps, n_ps, room):
        self.nc, self.k, self.s, self.s_ps, self.n_ps = nc, k, s, s_ps, n_ps
        n = GH * self.QT
        self.big, self.neg = room[:, 0:n], room[:, n:2 * n]
        self.rows, self.left = room[0:n, SPAN:SPAN + P], room[0:n, SPAN + P:SPAN + 2 * P]
        self.three = room[0:n, 2 * SPAN:2 * SPAN + 3 * P // 2].bitcast(BF16).rearrange("n (i t) -> n i t", i=3)
        self.m_psum, self.m_taken, self.neg_ready, self.n_psum, self.m_own, self.three_ready, self.moved = (
            sem(x) for x in ("m_psum", "m_taken", "neg_ready", "n_psum", "m_own", "three_ready", "moved"))

    def tensor(self, pe):
        nc, k, s = self.nc, self.k, self.s
        flat = lambda a: a[0:ROWS, s, :, :].rearrange("r h t -> r (h t)")
        pe.sem_inc(self.m_taken, 1)
        with pe.Fori(0, GH * self.QT) as n:
            pe.wait_ge(self.m_taken, n + 1)
            for c in range(4):
                ins = nc.tensor.matmul(self.s_ps[:, c // 2, c % 2, :], flat(k["qst"])[:, bass.ds(n * P, P)],
                                       flat(k["kst"])[:, bass.ds((n // self.QT) * L + c * SPAN, SPAN)], start=True, stop=True)
            ins.then_inc(self.m_psum, 1)
        pe.wait_ge(self.neg_ready, 1)
        nc.tensor.transpose(self.n_ps, self.neg, k["ident"][:]).then_inc(self.n_psum, 1)
        pe.wait_ge(self.moved, 48)

    def vector(self, vec):
        nc = self.nc
        with vec.Fori(0, GH * self.QT) as n:
            vec.wait_ge(self.m_psum, n + 1)
            nc.vector.tensor_reduce(self.big[:, bass.ds(n, 1)], self.s_ps[:, 0:2, :, :], AX.XYZ, ALU.max).then_inc(self.m_taken, 1)
        vec.wait_ge(self.m_taken, GH * self.QT + 1)
        nc.vector.tensor_scalar(self.neg, self.big, -1.0, None, ALU.mult).then_inc(self.neg_ready, 1)
        mine = Steps(self.m_own)
        rows, left, three = self.rows, self.left, self.three
        vec.wait_ge(self.n_psum, 1)
        mine.add(nc.vector.tensor_copy(rows, self.n_ps))
        mine.wait(vec)
        mine.add(nc.vector.tensor_copy(three[:, 0, :], rows))
        mine.wait(vec)
        mine.add(nc.vector.tensor_tensor(left, rows, three[:, 0, :], ALU.subtract))
        mine.wait(vec)
        mine.add(nc.vector.tensor_copy(three[:, 1, :], left))
        mine.wait(vec)
        nc.vector.tensor_tensor(three[:, 2, :], left, three[:, 1, :], ALU.subtract).then_inc(self.three_ready, 1)

    def sync(self, sp):
        sp.wait_ge(self.three_ready, 1)
        for i in range(3):
            sp.dma_start(self.k["qst"][ROWS + i:ROWS + i + 1, self.s, :, :].rearrange("o h (t c) -> o (h t) c", c=P),
                         self.three[:, i, :]).then_inc(self.moved, 16)
        sp.wait_ge(self.moved, 48)


PIECES = tuple((x_part, w_part, q) for x_part, w_part in ((0, 0), (0, 1), (1, 0)) for q in range(DH))
PIECES_AFTER = (0, 0, 2, 2, 2, 2, 2, 2, 2, 2, 2, 1, 1, 1, 1, 2)
PIECES_AFTER_IN_LAST = (0, 0, 2, 2, 2, 2, 2, 2, 2, 2, 2, 2, 2, 2, 0, 0)
TURN_AFTER = 1


ATTEND_SEMS = ("s_psum", "exp_done", "pv_done", "mixed_ready", "turned", "own", "vg_ready", "xt_ready", "e_psum", "x_taken",
               "arrived", "shifted", "w_in", "b_in", "w_ready", "copied", "stored",
               "m_psum", "m_taken", "neg_ready", "n_psum", "m_own", "three_ready", "moved")


def attend(nc, k, b, s, hp):
    qst, kst, acc, share = k["qst"], k["kst"], k["acc"], k["share"]
    KT, UNITS, QS = L // P, 2 * (L // P), L // SPAN
    VC = HD + 1
    when = lambda eng: eng.If(k["ranged_of"][eng.engine] != P)
    with ExitStack() as ctx:
        sem = lambda n: k["attend_sems"][s][n]
        sb = lambda n, shape, dt=F32: ctx.enter_context(nc.sbuf_tensor(f"att{s}_{n}", shape, dt))
        ps = lambda n, shape, dt=F32: ctx.enter_context(nc.psum_tensor(f"att{s}_{n}", shape, dt))
        probs = sb("probs", [P, 4, 2, SPAN])
        wpair = sb("wpair", [P, DH, 2 * D])
        mixed = wpair[:, 0, :]
        biased = wpair[:, 1, :]
        bpair = sb("bpair", [P, 2 * D])
        vg = sb("vg", [P, KT, GH, VC])
        xt = sb("xt", [P, 2, 2, DH, P], F32R)
        whole = sb("whole", [P, DH, P])
        wp = sb("wp", [P, 2, DH, 2 * D], F32R)
        inv, out = sb("inv", [P, 4 * GH]), sb("out", [P, 4 * GH, HD])
        s_ps = ps("s_ps", [P, 3, 2, SPAN])
        pv_ps, x_ps = ps("pv_ps", [P, SPAN]), ps("x_ps", [P, SPAN])
        s_psum, exp_done, pv_done, mixed_ready, turned, own, vg_ready, xt_ready, e_psum, x_taken, arrived, shifted = (
            sem(n) for n in ("s_psum", "exp_done", "pv_done", "mixed_ready", "turned", "own", "vg_ready", "xt_ready",
                             "e_psum", "x_taken", "arrived", "shifted"))
        maxima = Maxima(nc, k, s, sem, s_ps, x_ps[0:GH * (L // P), 0:P], probs[:].rearrange("p u h t -> p (u h t)"))
        NT = SPAN // P
        TAKEN = NT + 1
        pair = hp * 2 + s
        w_in, b_in, stored = sem("w_in"), sem("b_in"), sem("stored")
        w_ready, copied = sem("w_ready"), sem("copied")

        def query_spans(eng, body):
            body(0, True, False)
            with eng.Fori(1, QS - 1) as it:
                body(it, False, False)
            body(QS - 1, False, True)

        def blocks(block):
            @block.sync
            def _(sp):
                columns = bass.ds(pair * 2 * D, 2 * D)
                sp.dma_start(wpair[:], k["in_wexp"].rearrange("(k p) e -> p k e", p=P)[:, :, columns]).then_inc(w_in, 16)
                sp.dma_start(bpair[:], k["in_bexp"][:, columns]).then_inc(b_in, 16)
                with when(sp):
                    maxima.sync(sp)
                stacks = load_stacks(nc, k, sp, 1 - s, hp if s == 0 else 1 - hp, arrived)
                sp.wait_ge(arrived, stacks)
                if s == 1:
                    with sp.If(hp == 1):
                        rows = k["out"].rearrange("(b j p) d -> p b j d", p=P, j=L // P)
                        for it in range(QS):
                            sp.wait_ge(own, (it + 1) * (2 * NT + 2))
                            sp.dma_start(rows[:, bass.ds(b, 1), it * NT:(it + 1) * NT, :].rearrange("p b j d -> p (b j) d"),
                                         acc[:, it * NT:(it + 1) * NT, :]).then_inc(stored, 16)
                        sp.wait_ge(stored, 16 * QS)

            @block.gpsimd
            def _(pool):
                def tiles(it, is_first):
                    for n in range(NT):
                        t = it * NT + n
                        if n >= 2 or not is_first:
                            pool.wait_ge(e_psum, t - 1)
                        if n or not is_first:
                            pool.wait_ge(xt_ready, t)
                        first, second = xt[:, n % 2, 0, :, :], xt[:, n % 2, 1, :, :]
                        tokens = k["xnT"][:, :, bass.ds(t * P, P)]
                        nc.gpsimd.tensor_copy(whole[:], tokens).then_inc(copied, 1)
                        nc.gpsimd.tensor_copy(first, tokens).then_inc(copied, 1)
                        pool.wait_ge(copied, 2 * t + 2)
                        nc.gpsimd.tensor_tensor(second, whole[:], first.bitcast(F32), ALU.subtract).then_inc(xt_ready, 1)

                for other in k["attend_sems"][1 - s].values():
                    nc.gpsimd.sem_clear(other)
                tiles(0, True)
                pool.wait_ge(xt_ready, NT)
                shift_by_bound(nc, k, 1 - s, hp if s == 0 else 1 - hp).then_inc(shifted, 1)
                pool.wait_ge(shifted, 1)
                with pool.Fori(1, QS) as it:
                    tiles(it, False)

            @block.tensor
            def _(pe):
                with when(pe):
                    maxima.tensor(pe)

                def scores(it, u, is_first=False):
                    if u >= 3:
                        pe.wait_ge(exp_done, it * UNITS + u - 2)
                    elif not is_first:
                        pe.wait_ge(exp_done, it * UNITS - UNITS + (31, 32, 30)[u])
                    kt, pair = u // 2, u % 2
                    for h in range(2):
                        ins = nc.tensor.matmul(s_ps[:, u % 3, h, :], kst[0:ROWS + 3, s, 2 * pair + h, kt * P:(kt + 1) * P],
                                               qst[0:ROWS + 3, s, 2 * pair + h, bass.ds(it * SPAN, SPAN)], start=True, stop=True)
                    ins.then_inc(s_psum, 1)

                def scores_ahead(it, u, is_last):
                    if u < UNITS:
                        scores(it, u)
                    elif not is_last:
                        scores(it + 1, u - UNITS)

                def turn_back(it):
                    pe.wait_ge(mixed_ready, it)
                    pe.wait_ge(x_taken, it * TAKEN - 1)
                    for c in range(4):
                        ins = nc.tensor.transpose(x_ps[:, c * P:(c + 1) * P], mixed[:, c * P:(c + 1) * P], k["ident"][:])
                    ins.then_inc(turned, 1)

                def experts(it, piece, is_first):
                    n, i = piece // len(PIECES), piece % len(PIECES)
                    if i == 0:
                        pe.wait_ge(xt_ready, it * NT + n + 1)
                        if n == 0 and is_first:
                            pe.wait_ge(w_ready, 2)
                        if n or not is_first:
                            pe.wait_ge(x_taken, it * TAKEN + n)
                    x_part, w_part, q = PIECES[i]
                    ins = nc.tensor.matmul(x_ps[:], xt[:, n % 2, x_part, q, :], wp[:, w_part, q, :],
                                           start=(i == 0), stop=(i == len(PIECES) - 1))
                    if i == len(PIECES) - 1:
                        ins.then_inc(e_psum, 1)

                def body(it, is_first, is_last):
                    if is_first:
                        for u in range(3):
                            scores(it, u, True)
                    for kt in range(KT):
                        scores_ahead(it, 2 * kt + 3, is_last)
                        pe.wait_ge(exp_done, it * UNITS + 2 * kt + 2)
                        if kt == 0:
                            if is_first:
                                pe.wait_ge(vg_ready, 1)
                            else:
                                pe.wait_ge(mixed_ready, it)
                        for h in range(GH):
                            ins = nc.tensor.matmul(pv_ps[32 * h:32 * h + VC, :], vg[:, kt, h, :],
                                                   probs[:, (2 * kt + h // 2) % 4, h % 2, :], start=(kt == 0), stop=(kt == KT - 1))
                        ins.then_inc(pv_done, 1)
                        if kt < KT - 1:
                            scores_ahead(it, 2 * kt + 4, is_last)
                        if kt == TURN_AFTER and not is_first:
                            turn_back(it)
                        pieces = PIECES_AFTER_IN_LAST if is_last else PIECES_AFTER
                        for piece in range(sum(pieces[:kt]), sum(pieces[:kt + 1])):
                            experts(it, piece, is_first)
                    scores_ahead(it, 2 * KT + 2, is_last)

                nc.tensor.matmul(pv_ps[:], k["zero"][0:ROWS, :], kst[0:ROWS, s, 0, 0:SPAN], start=True, stop=True)
                query_spans(pe, body)
                turn_back(QS)

            @block.scalar
            def _(act):
                def body(it, is_first, is_last):
                    for u in range(UNITS):
                        act.wait_ge(s_psum, it * UNITS + u + 1)
                        if u >= 4 or not is_first:
                            act.wait_ge(pv_done, it * KT + u // 2 - 1)
                        nc.scalar.activation(probs[:, u % 4, :, :], s_ps[:, u % 3, :, :], ACT.Exp,
                                             scale=HD ** -0.5).then_inc(exp_done, 1)

                query_spans(act, body)

            @block.vector
            def _(vec):
                nc.vector.tensor_copy(vg[:], k["values"][:, :, bass.ds(hp * 8 + s * 4, 4), :]).then_inc(vg_ready, 1)
                vec.wait_ge(w_in, 16)
                nc.vector.tensor_copy(wp[:, 0, :, :], wpair[:]).then_inc(w_ready, 1)
                vec.wait_ge(w_ready, 1)
                nc.vector.tensor_tensor(wp[:, 1, :, :], wpair[:], wp[:, 0, :, :].bitcast(F32), ALU.subtract).then_inc(w_ready, 1)
                with when(vec):
                    maxima.vector(vec)

                def empty_products(it):
                    vec.wait_ge(pv_done, it * KT + KT)
                    nc.vector.tensor_copy(mixed, pv_ps[:]).then_inc(mixed_ready, 1)

                def take_turned(mine, it):
                    vec.wait_ge(turned, it)
                    heads = x_ps[:].rearrange("p (g e) -> p g e", e=32)
                    mine.add(nc.vector.reciprocal(inv[:], heads[:, :, HD]))
                    mine.wait(vec)
                    nc.vector.tensor_tensor(out[:], heads[:, :, 0:HD], inv[:].unsqueeze(2).to_broadcast([P, 4 * GH, HD]),
                                            ALU.mult).then_inc(x_taken, 1)
                    vec.wait_ge(x_taken, it * TAKEN)
                    at = acc[:, bass.ds(it * 4 - 4, 4), bass.ds(hp * P + s * 64, GH * HD)]
                    mine.add(nc.vector.tensor_tensor(at, at, out[:].rearrange("p (c h) d -> p c (h d)", c=4), ALU.add))
                    mine.wait(vec)

                def body(it, is_first, is_last):
                    mine = Steps(own, 0 if is_first else it * (2 * NT + 2) - 2)
                    if not is_first:
                        take_turned(mine, it)
                    for n in range(NT):
                        t = it * NT + n
                        at = acc[:, bass.ds(t, 1), :].rearrange("p o d -> p (o d)")
                        if n == 0 and is_first:
                            vec.wait_ge(b_in, 16)
                        if n == NT - 1 and not is_last:
                            empty_products(it)
                        vec.wait_ge(e_psum, t + 1)
                        nc.vector.tensor_tensor(biased, x_ps[:], bpair[:], ALU.add).then_inc(x_taken, 1)
                        vec.wait_ge(x_taken, it * TAKEN + n + 1)
                        for e in range(2):
                            mine.add(nc.vector.scalar_tensor_tensor(
                                out=at, in0=biased[:, e * D:(e + 1) * D],
                                scalar=share[:, bass.ds(t, 1), bass.ds(pair * 2 + e, 1)].rearrange("p o c -> p (o c)"),
                                in1=at, op0=ALU.mult, op1=ALU.add))
                            mine.wait(vec)
                    if is_last:
                        empty_products(it)

                query_spans(vec, body)
                take_turned(Steps(own, QS * (2 * NT + 2) - 2), QS)

        with nc.Block() as block:
            blocks(block)


def load_ffn_constants(nc, k):
    with ExitStack() as ctx:
        arrived, ones_set = ctx.enter_context(nc.semaphore("ffn_arrived")), ctx.enter_context(nc.semaphore("ones_set"))
        block = ctx.enter_context(nc.Block())

        @block.sync
        def _(sp):
            halves = lambda a: a.rearrange("(k p) e -> p k e", p=P)
            for dst, src in (("wgate", halves(k["in_wgate"])),
                             ("bgate", k["in_bgate"]), ("lower", k["in_lower"]),
                             ("member", k["in_member"])):
                sp.dma_start(k[dst][:], src).then_inc(arrived, 16)
            sp.wait_ge(arrived, 4 * 16)

        @block.vector
        def _(vec):
            nc.vector.memset(k["zero"][:], 0.0)
            nc.vector.memset(k["all_ones"][:], 1.0)
            nc.vector.memset(k["kst"][ROWS:ROWS + 3, 0, :, :], 1.0)

        @block.gpsimd
        def _(pool):
            nc.gpsimd.memset(k["kst"][ROWS:ROWS + 3, 1, :, :], 1.0).then_inc(ones_set, 1)
            pool.wait_ge(ones_set, 1)
            nc.gpsimd.memset(k["values"][:], 1.0)


def feed_forward(nc, k):
    with ExitStack() as ctx:
        sb = lambda n, shape, dt=F32: ctx.enter_context(nc.sbuf_tensor(n, shape, dt))
        k["acc"] = sb("acc", [P, L // P, D])
        k["parts"] = sb("parts", [P, 6, DH, L], BF16)
        k["values"] = sb("values", [P, L // P, HEADS, HD + 1])
        k["qst"] = sb("qst", [P, 2, GH, L], BF16)
        k["kst"] = sb("kst", [P, 2, GH, L], BF16)
        k["xnT"] = sb("xnT", [P, DH, L])
        k["share"] = sb("share", [P, L // P, E])
        k["wgate"] = sb("wgate", [P, DH, E])
        k["bgate"], k["lower"] = sb("bgate", [P, E]), sb("lower", [P, E, E])
        k["zero"] = sb("zero", [P, P], BF16)
        k["all_ones"], k["member"], k["shift"] = sb("all_ones", [P, P]), sb("member", [P, 9]), sb("shift", [P, HEADS])
        k["ranged"] = sb("ranged", [1, 1], I32)
        k["ranged_of"] = {}
        k["attend_sems"] = [{n: ctx.enter_context(nc.semaphore(f"att{s}_{n}")) for n in ATTEND_SEMS} for s in range(2)]
        load_ffn_constants(nc, k)
        with nc.Fori(0, B) as b:
            project_queries_and_keys(nc, k, b)
            route_and_project_values(nc, k)
            with nc.Fori(0, 2) as hp:
                for s in range(2):
                    attend(nc, k, b, s, hp)


def build(nc, io):
    with ExitStack() as ctx:
        sb = lambda name, shape, dt=F32: ctx.enter_context(nc.sbuf_tensor(name, shape, dt))
        k = dict(io)
        k["vec"] = sb("vec", [P, NVEC])
        k["ident"] = sb("ident", [P, P])
        k["keep"] = sb("keep", [P, DH])
        k["away"] = sb("away", [P, DH])
        k["mean1"], k["rstd1"] = sb("mean1", [P, TILES]), sb("rstd1", [P, TILES])
        with ExitStack() as scan:
            sb2 = lambda name, shape, dt=F32: scan.enter_context(nc.sbuf_tensor(name, shape, dt))
            k["xy"] = sb2("xy", [P, TILES, D])
            inner = scan.enter_context(ExitStack())
            sb2 = lambda name, shape, dt=F32: inner.enter_context(nc.sbuf_tensor(name, shape, dt))
            k["gain"] = sb2("gain", [P, DH, T])
            k["drive"] = sb2("drive", [P, DH, T])
            normalise_and_gate(nc, k)
            k["state"] = sb2("state", [P, 2, DH, GL])
            k["start"] = sb2("start", [P, 2, DH, GL])
            k["ones"] = sb2("ones", [P, P])
            k["wr"] = sb2("wr", [P, DH, D])
            k["agree"] = sb2("agree", [1, 1], I32)
            prepare_sweeps(nc, k)
            sweep(nc, k, "sweep", SWEEPS)
            look_at_defect(nc, k)
            sweep(nc, k, "rest", CHUNKS, unless(k["agree"]))
            inner.close()
            project_states(nc, k)
        feed_forward(nc, k)


def kernel(L0_attn_x, L0_attn_decay, L0_attn_Wr, L0_attn_br, L0_attn_Wg, L0_attn_bg, L0_attn_Wo, L0_attn_bo,
           L0_attn_ln_w, L0_attn_ln_b, L0_ffn_W_qkv, L0_ffn_b_qkv, L0_ffn_W_gate, L0_ffn_b_gate,
           L0_ffn_W_experts, L0_ffn_b_experts):
    import numpy as np
    import concourse.bacc as bacc
    from concourse.bass_utils import run_bass_kernel_spmd

    lay = np.ascontiguousarray
    halves = lambda v: np.asarray(v).reshape(DH, P).T
    bqkv = np.asarray(L0_ffn_b_qkv)
    member = np.zeros((P, 9), np.float32)
    member[:, 0:8] = np.repeat(np.eye(8, dtype=np.float32), HD, axis=0)
    member[ROWS, 8] = -1.0
    arrays = {
        "in_x": lay(np.asarray(L0_attn_x).reshape(T, D)),
        "in_vec": lay(np.concatenate([halves(v) for v in (L0_attn_decay, L0_attn_br, L0_attn_bg, L0_attn_ln_w,
                                                          L0_attn_ln_b, bqkv[0:D], bqkv[D:2 * D])], axis=1)),
        "in_ident": np.eye(P, dtype=np.float32),
        "in_wg": lay(np.asarray(L0_attn_Wg).T),
        "in_wr": lay(np.asarray(L0_attn_Wr).T),
        "in_wo": lay(np.asarray(L0_attn_Wo).T),
        "in_wqkv": lay(np.asarray(L0_ffn_W_qkv)),
        "in_wexp": lay(np.asarray(L0_ffn_W_experts).transpose(1, 0, 2).reshape(D, E * D)),
        "in_wgate": lay(np.asarray(L0_ffn_W_gate)),
        "in_bv": lay(np.broadcast_to(bqkv[2 * D:], (P, D))),
        "in_bexp": lay(np.broadcast_to(np.asarray(L0_ffn_b_experts).reshape(-1), (P, E * D))),
        "in_bgate": lay(np.broadcast_to(np.asarray(L0_ffn_b_gate), (P, E))),
        "in_member": member,
        "in_lower": lay(np.broadcast_to(np.tri(E, k=-1, dtype=np.float32), (P, E, E))),
        "in_bo": lay(np.broadcast_to(np.asarray(L0_attn_bo), (P, D))),
    }
    nc = bacc.Bacc("TRN2", target_bir_lowering=False, num_devices=1)
    io = {n: nc.dram_tensor(n, a.shape, mybir.dt.from_np(a.dtype), kind="ExternalInput").ap() for n, a in arrays.items()}
    io["out"] = nc.dram_tensor("out", (T, D), F32, kind="ExternalOutput").ap()
    io["x1"] = nc.dram_tensor("x1", (T, D), F32).ap()
    build(nc, io)
    r = run_bass_kernel_spmd(nc, [arrays], core_ids=[0])
    return r.results[0]["out"].reshape(B, L, D)
```
